# Optimizing a Trainium2 kernel written in Bass

```python
import numpy as np
import jax
import jax.numpy as jnp

def _softmax(x, axis=-1):
    return jax.nn.softmax(x, axis=axis)

def _gelu(x):
    return jax.nn.gelu(x, approximate=True)

def _silu(x):
    return jax.nn.silu(x)

def _sigmoid(x):
    return jax.nn.sigmoid(x)

def _layernorm(x, axis=-1, eps=1e-05):
    m = jnp.mean(x, axis=axis, keepdims=True)
    v = jnp.var(x, axis=axis, keepdims=True)
    return (x - m) / jnp.sqrt(v + eps)

def _scatter_add(tgt, idx, src, axis=0):
    return tgt.at[idx].add(src)

def _segment_sum(src, seg, n):
    return jax.ops.segment_sum(src, seg, n)
kernel_name = 'mk_flamingo_gated_d2_seqx_r8_6d2371'

def setup_inputs(seed: int=0):
    np.random.seed(seed)
    _w = jnp.asarray

    def _rec_inputs():
        import jax
        import jax.numpy as jnp
        _rk = jax.random.key(seed)
        x = -0.0005146 + 1 * jax.random.normal(jax.random.fold_in(_rk, 1), (128, 64, 128), jnp.float32)
        _lenS = 64 - jax.random.randint(jax.random.fold_in(_rk, 7), (128,), 0, max(1, 64 // 4) + 1, jnp.int32)
        _lenS2 = 64 - jax.random.randint(jax.random.fold_in(_rk, 8), (128,), 0, max(1, 64 // 4) + 1, jnp.int32)
        _ctx_1024P = jax.random.normal(jax.random.fold_in(_rk, 11), (128, 16, 128), jnp.float32)
        _ctx_1024c = jax.random.dirichlet(jax.random.fold_in(_rk, 511), 0.3 * jnp.ones((16,), jnp.float32), (128, 64))
        _ctx_1024t = jnp.einsum('bsk,bkd->bsd', _ctx_1024c, _ctx_1024P)
        _ctx_1024t = _ctx_1024t * jax.lax.rsqrt(jnp.mean(jnp.square(_ctx_1024t)) + 1e-12) * 0.953939
        ctx_1024 = -0.000392918 + 0.999932 * (_ctx_1024t + 0.3 * jax.random.normal(jax.random.fold_in(_rk, 611), (128, 64, 128), jnp.float32))
        _g = jax.random.normal(jax.random.fold_in(_rk, 9001), (2, 2), jnp.float32)
        _g = jnp.sign(_g) * jnp.maximum(jnp.abs(_g), 1.0) + (_g == 0) * 1.0
        g_xattn = _g[0]
        g_ffn = _g[1]
        return (x, ctx_1024, g_xattn, g_ffn)
    x, ctx_1024, g_xattn, g_ffn = _rec_inputs()

    def _L0_xattn_setup():
        import jax, jax.numpy as jnp
        import numpy as np
        DIM = 128
        DIM_HEAD = 64
        HEADS = 16
        INNER = DIM_HEAD * HEADS
        EPS = 1e-05

        def layer_norm(x, g, b):
            m = jnp.mean(x, axis=-1, keepdims=True)
            v = jnp.mean(jnp.square(x - m), axis=-1, keepdims=True)
            return (x - m) * jax.lax.rsqrt(v + EPS) * g + b
        key = jax.random.key(seed)
        ks = jax.random.split(key, 8)
        B, N_IMG, N_LAT = (4, 512, 64)
        std = 1.0 / np.sqrt(DIM)
        return {'image_embeds': jax.random.normal(ks[0], (B, N_IMG, DIM), dtype=jnp.float32), 'latents': jax.random.normal(ks[1], (B, N_LAT, DIM), dtype=jnp.float32), 'ln1_g': jnp.ones((DIM,), jnp.float32), 'ln1_b': jnp.zeros((DIM,), jnp.float32), 'ln2_g': jnp.ones((DIM,), jnp.float32), 'ln2_b': jnp.zeros((DIM,), jnp.float32), 'Wq': jax.random.normal(ks[2], (DIM, INNER), dtype=jnp.float32) * std, 'Wkv': jax.random.normal(ks[3], (DIM, 2 * INNER), dtype=jnp.float32) * std, 'Wo': jax.random.normal(ks[4], (INNER, DIM), dtype=jnp.float32) * std}
    _L0_xattn_all = _L0_xattn_setup()
    _L0_xattn_in = {k: v for k, v in _L0_xattn_all.items() if k in ('ln1_g', 'ln1_b', 'ln2_g', 'ln2_b', 'Wq', 'Wkv', 'Wo')}
    del _L0_xattn_all

    def _L0_ffn_setup():
        import jax, jax.numpy as jnp
        import numpy as np
        B, S, F, E, K = (4, 128, 128, 8, 2)
        H = 4 * F
        key = jax.random.key(seed)
        ks = jax.random.split(key, 7)

        def xavier(k, shape):
            fan_in, fan_out = (shape[-2], shape[-1])
            scale = jnp.sqrt(6.0 / (fan_in + fan_out))
            return jax.random.uniform(k, shape, jnp.float32, -scale, scale)
        return {'x': jax.random.normal(ks[0], (B, S, F), jnp.float32), 'Wg': xavier(ks[1], (F, E)), 'bg': jnp.zeros((E,), jnp.float32), 'W1': xavier(ks[2], (E, F, H)), 'b1': jnp.zeros((E, H), jnp.float32), 'W2': xavier(ks[3], (E, H, F)), 'b2': jnp.zeros((E, F), jnp.float32)}
    _L0_ffn_all = _L0_ffn_setup()
    _L0_ffn_in = {k: v for k, v in _L0_ffn_all.items() if k in ('Wg', 'bg', 'W1', 'b1', 'W2', 'b2')}
    del _L0_ffn_all

    def _L1_xattn_setup():
        import jax, jax.numpy as jnp
        import numpy as np
        B, S, DIM, H = (2, 256, 128, 16)
        HD = DIM // H
        key = jax.random.key(seed)
        ks = jax.random.split(key, 11)
        s = 0.02
        return {'q': jax.random.normal(ks[0], (B, S, DIM), jnp.float32), 'k': jax.random.normal(ks[1], (B, S, DIM), jnp.float32), 'v': jax.random.normal(ks[2], (B, S, DIM), jnp.float32), 'wq': jax.random.normal(ks[3], (DIM, DIM), jnp.float32) * s, 'bq': jax.random.normal(ks[4], (DIM,), jnp.float32) * s, 'wk': jax.random.normal(ks[5], (DIM, DIM), jnp.float32) * s, 'bk': jax.random.normal(ks[6], (DIM,), jnp.float32) * s, 'wv': jax.random.normal(ks[7], (DIM, DIM), jnp.float32) * s, 'bv': jax.random.normal(ks[8], (DIM,), jnp.float32) * s, 'wo': jax.random.normal(ks[9], (DIM, DIM), jnp.float32) * s, 'bo': jax.random.normal(ks[10], (DIM,), jnp.float32) * s}
    _L1_xattn_all = _L1_xattn_setup()
    _L1_xattn_in = {k: v for k, v in _L1_xattn_all.items() if k in ('wq', 'bq', 'wk', 'bk', 'wv', 'bv', 'wo', 'bo')}
    del _L1_xattn_all

    def _L1_ffn_setup():
        import jax, jax.numpy as jnp
        import numpy as np
        TOP_K = 2
        key = jax.random.key(seed)
        k0, k1, k2, k3, k4 = jax.random.split(key, 5)
        B, S, H, I, E = (1, 512, 128, 256, 8)
        hidden_states = jax.random.normal(k0, (B, S, H), dtype=jnp.float32)
        wg = jax.random.normal(k1, (E, H), dtype=jnp.float32) * 0.02
        w1 = jax.random.normal(k2, (E, I, H), dtype=jnp.float32) * 0.02
        w3 = jax.random.normal(k3, (E, I, H), dtype=jnp.float32) * 0.02
        w2 = jax.random.normal(k4, (E, H, I), dtype=jnp.float32) * 0.02
        return {'hidden_states': hidden_states, 'wg': wg, 'w1': w1, 'w3': w3, 'w2': w2}
    _L1_ffn_all = _L1_ffn_setup()
    _L1_ffn_in = {k: v for k, v in _L1_ffn_all.items() if k in ('wg', 'w1', 'w3', 'w2')}
    del _L1_ffn_all
    return {'x': x, 'ctx_1024': ctx_1024, 'g_xattn': g_xattn, 'g_ffn': g_ffn, 'L0_xattn_ln1_g': _L0_xattn_in['ln1_g'], 'L0_xattn_ln1_b': _L0_xattn_in['ln1_b'], 'L0_xattn_ln2_g': _L0_xattn_in['ln2_g'], 'L0_xattn_ln2_b': _L0_xattn_in['ln2_b'], 'L0_xattn_Wq': _L0_xattn_in['Wq'], 'L0_xattn_Wkv': _L0_xattn_in['Wkv'], 'L0_xattn_Wo': _L0_xattn_in['Wo'], 'L0_ffn_Wg': _L0_ffn_in['Wg'], 'L0_ffn_bg': _L0_ffn_in['bg'], 'L0_ffn_W1': _L0_ffn_in['W1'], 'L0_ffn_b1': _L0_ffn_in['b1'], 'L0_ffn_W2': _L0_ffn_in['W2'], 'L0_ffn_b2': _L0_ffn_in['b2'], 'L1_xattn_wq': _L1_xattn_in['wq'], 'L1_xattn_bq': _L1_xattn_in['bq'], 'L1_xattn_wk': _L1_xattn_in['wk'], 'L1_xattn_bk': _L1_xattn_in['bk'], 'L1_xattn_wv': _L1_xattn_in['wv'], 'L1_xattn_bv': _L1_xattn_in['bv'], 'L1_xattn_wo': _L1_xattn_in['wo'], 'L1_xattn_bo': _L1_xattn_in['bo'], 'L1_ffn_wg': _L1_ffn_in['wg'], 'L1_ffn_w1': _L1_ffn_in['w1'], 'L1_ffn_w3': _L1_ffn_in['w3'], 'L1_ffn_w2': _L1_ffn_in['w2']}

def reference(x, ctx_1024, g_xattn, g_ffn, L0_xattn_ln1_g, L0_xattn_ln1_b, L0_xattn_ln2_g, L0_xattn_ln2_b, L0_xattn_Wq, L0_xattn_Wkv, L0_xattn_Wo, L0_ffn_Wg, L0_ffn_bg, L0_ffn_W1, L0_ffn_b1, L0_ffn_W2, L0_ffn_b2, L1_xattn_wq, L1_xattn_bq, L1_xattn_wk, L1_xattn_bk, L1_xattn_wv, L1_xattn_bv, L1_xattn_wo, L1_xattn_bo, L1_ffn_wg, L1_ffn_w1, L1_ffn_w3, L1_ffn_w2):
    import jax
    import jax.numpy as jnp

    def _L0_xattn_ref(image_embeds, latents, ln1_g, ln1_b, ln2_g, ln2_b, Wq, Wkv, Wo):
        import jax, jax.numpy as jnp
        import numpy as np
        DIM = 128
        DIM_HEAD = 64
        HEADS = 16
        INNER = DIM_HEAD * HEADS
        EPS = 1e-05

        def layer_norm(x, g, b):
            m = jnp.mean(x, axis=-1, keepdims=True)
            v = jnp.mean(jnp.square(x - m), axis=-1, keepdims=True)
            return (x - m) * jax.lax.rsqrt(v + EPS) * g + b
        B, S_lat, _ = latents.shape
        x = layer_norm(image_embeds, ln1_g, ln1_b)
        l = layer_norm(latents, ln2_g, ln2_b)
        q = l @ Wq
        kv_in = jnp.concatenate([x, l], axis=1)
        kv = kv_in @ Wkv
        k, v = jnp.split(kv, 2, axis=-1)

        def to_heads(t):
            return t.reshape(t.shape[0], t.shape[1], HEADS, DIM_HEAD).transpose(0, 2, 1, 3)
        q, k, v = (to_heads(q), to_heads(k), to_heads(v))
        scale = 1.0 / np.sqrt(np.sqrt(DIM_HEAD))
        w = jnp.einsum('bhqd,bhkd->bhqk', q * scale, k * scale)
        w = jax.nn.softmax(w.astype(jnp.float32), axis=-1).astype(q.dtype)
        out = jnp.einsum('bhqk,bhkd->bhqd', w, v)
        out = out.transpose(0, 2, 1, 3).reshape(B, S_lat, INNER)
        return out @ Wo

    def _L0_ffn_ref(x, Wg, bg, W1, b1, W2, b2):
        import jax, jax.numpy as jnp
        import numpy as np
        B, S, F, E, K = (4, 128, 128, 8, 2)
        H = 4 * F
        gate_probs = jax.nn.softmax(x @ Wg + bg, axis=-1)
        k = K
        _, top_idx = jax.lax.top_k(gate_probs, k)
        expert_mask = jax.nn.one_hot(top_idx, gate_probs.shape[-1], dtype=gate_probs.dtype).sum(-2)
        selected = gate_probs * expert_mask
        selected = selected / (selected.sum(-1, keepdims=True) + 1e-08)
        h = jax.nn.gelu(jnp.einsum('bsf,efh->bseh', x, W1) + b1)
        expert_out = jnp.einsum('bseh,ehf->bsef', h, W2) + b2[None, None]
        return jnp.einsum('bsef,bse->bsf', expert_out, selected)

    def _L1_xattn_ref(q, k, v, wq, bq, wk, bk, wv, bv, wo, bo):
        import jax, jax.numpy as jnp
        import numpy as np
        B, S, DIM, H = (2, 256, 128, 16)
        HD = DIM // H
        b, s, _ = k.shape
        qh = (q @ wq + bq).reshape(b, -1, H, HD).transpose(0, 2, 1, 3)
        kh = (k @ wk + bk).reshape(b, -1, H, HD).transpose(0, 2, 1, 3)
        vh = (v @ wv + bv).reshape(b, -1, H, HD).transpose(0, 2, 1, 3)
        scores = jax.nn.softmax(jnp.einsum('bhqd,bhkd->bhqk', qh, kh), axis=-1)
        attn = jnp.einsum('bhqk,bhkd->bhqd', scores, vh)
        concat = attn.transpose(0, 2, 1, 3).reshape(b, -1, H * HD)
        return concat @ wo + bo

    def _L1_ffn_ref(hidden_states, wg, w1, w3, w2):
        import jax, jax.numpy as jnp
        import numpy as np
        TOP_K = 2
        orig_shape = hidden_states.shape
        H = orig_shape[-1]
        E = wg.shape[0]
        x = hidden_states.reshape(-1, H)
        router_logits = x @ wg.T
        probs = jax.nn.softmax(router_logits, axis=-1)
        topk_w, topk_idx = jax.lax.top_k(probs, TOP_K)
        topk_w = topk_w / jnp.sum(topk_w, axis=-1, keepdims=True)
        expert_w = jnp.sum(jax.nn.one_hot(topk_idx, E, dtype=x.dtype) * topk_w[..., None], axis=1)
        h1 = jnp.einsum('th,eih->tei', x, w1)
        h3 = jnp.einsum('th,eih->tei', x, w3)
        y = jnp.einsum('tei,ehi->teh', jax.nn.silu(h1) * h3, w2)
        out = jnp.einsum('te,teh->th', expert_w, y)
        return out.reshape(orig_shape)
    x = x + jnp.tanh(g_xattn[0]) * _L0_xattn_ref(ctx_1024, _layernorm(x, axis=-1), L0_xattn_ln1_g, L0_xattn_ln1_b, L0_xattn_ln2_g, L0_xattn_ln2_b, L0_xattn_Wq, L0_xattn_Wkv, L0_xattn_Wo)
    x = x + jnp.tanh(g_ffn[0]) * _L0_ffn_ref(_layernorm(x, axis=-1), L0_ffn_Wg, L0_ffn_bg, L0_ffn_W1, L0_ffn_b1, L0_ffn_W2, L0_ffn_b2)
    x = x + jnp.tanh(g_xattn[1]) * _L1_xattn_ref(_layernorm(x, axis=-1), ctx_1024, ctx_1024, L1_xattn_wq, L1_xattn_bq, L1_xattn_wk, L1_xattn_bk, L1_xattn_wv, L1_xattn_bv, L1_xattn_wo, L1_xattn_bo)
    x = x + jnp.tanh(g_ffn[1]) * _L1_ffn_ref(_layernorm(x, axis=-1), L1_ffn_wg, L1_ffn_w1, L1_ffn_w3, L1_ffn_w2)
    return x

_drawn_inputs = setup_inputs


def setup_inputs(seed=0):
    import zlib

    import numpy as np

    out = dict(_drawn_inputs(seed))
    spreads = {'g_ffn': (-1.0, 0.6),
     'L0_xattn_ln1_g': (1.0, 0.2),
     'L0_xattn_ln1_b': (0.0, 0.1),
     'L0_xattn_ln2_g': (1.0, 0.2),
     'L0_xattn_ln2_b': (0.0, 0.1),
     'L0_ffn_bg': (0.0, 0.1),
     'L0_ffn_b1': (0.0, 0.1),
     'L0_ffn_b2': (0.0, 0.1)}
    factors = {'L1_xattn_wq': 8.0,
     'L1_xattn_bq': 8.0,
     'L1_xattn_wk': 8.0,
     'L1_xattn_bk': 8.0,
     'L1_xattn_wv': 2.784,
     'L1_xattn_bv': 8.0,
     'L1_xattn_wo': 2.839,
     'L1_xattn_bo': 3.316,
     'L1_ffn_wg': 8.0,
     'L1_ffn_w1': 8.0,
     'L1_ffn_w3': 8.0,
     'L1_ffn_w2': 8.0}
    for name, (base, spread) in spreads.items():
        noise = np.random.default_rng([zlib.crc32(name.encode()), seed]).standard_normal(out[name].shape)
        drawn = base * np.exp(spread * noise) if base else spread * noise
        out[name] = jnp.asarray(drawn.astype(out[name].dtype))
    for name, factor in factors.items():
        out[name] = (out[name] * factor).astype(out[name].dtype)
    return out
```

```python
from contextlib import ExitStack

import concourse.bass as bass
from concourse import mybir
from concourse.alu_op_type import AluOpType as ALU

F32 = mybir.dt.float32
F32R = mybir.dt.float32r
ACT = mybir.ActivationFunctionType
AX = mybir.AxisListType

P = 128
B, S, D = 128, 64, 128
TOK = B * S
NT = TOK // P
EPS = 1e-5
H0, DH0 = 16, 64
INNER = H0 * DH0
SCALE0 = 1.0 / 8.0
GB = 4
GT = GB * S
NG = B // GB
UN = 2 * GB
E0, F0 = 8, 512
H1, DH1 = 16, 8
E1, I1 = 8, 256
MT = 512
NM = TOK // MT


def exists(g, n):
    return (0 <= g < n) if isinstance(g, int) else True


ROOT_AT = 8
ROOTS_AT = (8, 12)
LN_STEPS = 9


def layer_norm_factors(nc, vec, stats, mean, rstd, tmp, step_done, sqrt_ready, steps, roots, twice):
    m_even, v_even, m_odd, v_odd = stats[:, :, 1], stats[:, :, 2], stats[:, :, 4], stats[:, :, 5]
    arg, var, root = tmp[:, 0, :], tmp[:, 1, :], tmp[:, 2, :]

    def step(instruction):
        nonlocal steps
        steps += 1
        instruction.then_inc(step_done, 1)
        vec.wait_ge(step_done, steps)

    def rsqrt(to):
        nonlocal roots
        roots += 1
        vec.wait_ge(sqrt_ready, roots)
        step(nc.vector.reciprocal(to, root))

    step(nc.vector.tensor_tensor(mean[:], m_even, m_odd, ALU.add))
    step(nc.vector.tensor_scalar(mean[:], mean[:], 0.5, None, ALU.mult))
    step(nc.vector.tensor_tensor(arg, m_even, m_odd, ALU.subtract))
    step(nc.vector.tensor_tensor(arg, arg, arg, ALU.mult))
    step(nc.vector.tensor_tensor(var, v_even, v_odd, ALU.add))
    step(nc.vector.tensor_scalar(var, var, 1.0 / P, None, ALU.mult))
    step(nc.vector.scalar_tensor_tensor(var, arg, 0.25, var, ALU.mult, ALU.add))
    step(nc.vector.tensor_scalar(arg, var, EPS, None, ALU.add))
    rsqrt(rstd[:])
    if twice:
        step(nc.vector.tensor_tensor(arg, rstd[:], rstd[:], ALU.mult))
        step(nc.vector.tensor_tensor(arg, arg, var, ALU.mult))
        step(nc.vector.tensor_scalar(arg, arg, EPS, None, ALU.add))
        rsqrt(var)
        step(nc.vector.tensor_tensor(rstd[:], rstd[:], var, ALU.mult))
    return steps


def build(nc, x, ctx_in, g_xattn, g_ffn, ln1_g, ln1_b, ln2_g, ln2_b, wq0, wkv0, wo0,
          gate0, gate0_b, w1_0, b1_0, w2_0, b2_0, wq1, bq1, wk1, bk1, wv1, bv1, wo1, bo1,
          gate1, w1_1, w3_1, w2_1, out):
    with ExitStack() as stack:
        def sem(name):
            return stack.enter_context(nc.semaphore(name))

        def sb(name, shape, dt=F32):
            return stack.enter_context(nc.sbuf_tensor(name, shape, dt))

        x_sb = sb("x_sb", [P, NT, D])
        ctx_sb = sb("ctx_sb", [P, NT, D])
        ident = sb("ident", [P, P])
        gates = sb("gates", [P, 4])
        stats = sb("stats", [P, NT, 6])
        mean = sb("mean", [P, NT])
        rstd = sb("rstd", [P, NT])
        cmean = sb("cmean", [P, NT])
        crstd = sb("crstd", [P, NT])
        tmp = sb("ln_tmp", [P, 3, NT])
        cols = sb("cols", [P, 4])

        with ExitStack() as inner:
            attention_0(nc, inner, sem, x, ctx_in, g_xattn, g_ffn, ln1_g, ln1_b, ln2_g, ln2_b, wq0, wkv0, wo0,
                        x_sb, ctx_sb, ident, gates, stats, mean, rstd, cmean, crstd, tmp, cols)
        with ExitStack() as inner:
            experts_0(nc, inner, sem, gate0, gate0_b, w1_0, b1_0, w2_0, b2_0,
                      x_sb, ident, gates, stats, mean, rstd, tmp)
        with ExitStack() as inner:
            attention_1(nc, inner, sem, wq1, bq1, wk1, bk1, wv1, bv1, wo1, bo1,
                        x_sb, ctx_sb, ident, gates, stats, mean, rstd, tmp)
        with ExitStack() as inner:
            experts_1(nc, inner, sem, gate1, w1_1, w3_1, w2_1,
                      x_sb, ident, gates, stats, mean, rstd, tmp, out)


def attention_0(nc, stack, new_sem, x, ctx_in, g_xattn, g_ffn, ln1_g, ln1_b, ln2_g, ln2_b, wq0, wkv0, wo0,
                x_sb, ctx_sb, ident, gates, stats, mean, rstd, cmean, crstd, tmp, cols):
    def sb(name, shape, dt=F32):
        return stack.enter_context(nc.sbuf_tensor(name, shape, dt))

    def sem(name):
        return new_sem("a0_" + name)

    score_hi = sb("score_hi", [P, H0, P], F32R)
    score_lo = sb("score_lo", [P, H0, P], F32R)
    value_w = sb("value_w", [P, H0, P])

    with ExitStack() as setup:
        def ssb(name, shape, dt=F32):
            return setup.enter_context(nc.sbuf_tensor(name, shape, dt))

        def ssem(name):
            return new_sem("s_" + name)

        wq_sb = ssb("wq_sb", [P, INNER])
        wkv_sb = ssb("wkv_sb", [P, 2 * INNER])
        wo_sb = ssb("wo_sb", [DH0, H0, P])
        wT = ssb("wT", [DH0, 3, 4, P])
        scaled = ssb("scaled", [P, 4, P])
        cstats = ssb("cstats", [P, NT, 6])
        g_row = ssb("g_row", [P, 4])
        pT = [setup.enter_context(nc.psum_tensor(f"s_pT{i}", [DH0, 4, P], F32)) for i in range(3)]
        pA = setup.enter_context(nc.psum_tensor("s_pA", [P, 4, P], F32))
        pB = setup.enter_context(nc.psum_tensor("s_pB", [P, 4, P], F32))
        NL = 8
        LT = NT // NL
        rows_in = [ssem(f"rows_in{i}") for i in range(NL)]
        weights_in, small_in = ssem("weights_in"), ssem("small_in")
        ident_zero, ident_ready = ssem("ident_zero"), ssem("ident_ready")
        gates_ready = ssem("gates_ready")
        stats_done, ln_step, sqrt_ready = ssem("stats_done"), ssem("ln_step"), ssem("sqrt_ready")
        wT_filled, wT_taken = ssem("wT_filled"), ssem("wT_taken")
        ab_filled, score_hi_ready, scaled_ready, ab_taken = ssem("ab_filled"), ssem("score_hi_ready"), ssem("scaled_ready"), ssem("ab_taken")
        block = setup.enter_context(nc.Block())
        xv = x.rearrange("(t two) s d -> (two s) t d", two=2)
        cv = ctx_in.rearrange("(t two) s d -> (two s) t d", two=2)

        @block.sync
        def _(sp):
            sp.dma_start(wq_sb[:], wq0).then_inc(weights_in, 16)
            sp.dma_start(wkv_sb[:], wkv0).then_inc(weights_in, 16)
            sp.dma_start(wo_sb[:], wo0.rearrange("(h e) f -> e h f", h=H0)).then_inc(weights_in, 16)
            for i in range(NL):
                sp.dma_start(x_sb[:, i * LT:(i + 1) * LT, :], xv[:, i * LT:(i + 1) * LT, :]).then_inc(rows_in[i], 16)

        @block.gpsimd
        def _(pool):
            for i, v in enumerate((ln1_g, ln1_b, ln2_g, ln2_b)):
                pool.dma_start(cols[:, i:i + 1], v.rearrange("(p a) -> p a", a=1)).then_inc(small_in, 16)
            for i, v in enumerate((g_xattn, g_ffn)):
                pool.dma_start(g_row[:, 2 * i:2 * i + 2],
                               v.rearrange("(a n) -> a n", a=1).broadcast_to([P, 2])).then_inc(small_in, 16)
            nc.gpsimd.memset(ident[:], 0.0).then_inc(ident_zero, 1)
            pool.wait_ge(ident_zero, 1)
            nc.gpsimd.affine_select(out=ident[:], in_=ident[:], compare_op=ALU.not_equal, fill=1.0, base=0,
                                    pattern=[[-1, P]], channel_multiplier=1).then_inc(ident_ready, 1)

        @block.scalar
        def _(act):
            for i in range(NL):
                act.dma_start(ctx_sb[:, i * LT:(i + 1) * LT, :], cv[:, i * LT:(i + 1) * LT, :]).then_inc(rows_in[i], 16)
            act.wait_ge(small_in, 16 * 6)
            nc.scalar.activation(gates[:], g_row[:], ACT.Tanh).then_inc(gates_ready, 1)
            for c in range(4):
                for i in range(3):
                    act.wait_ge(wT_filled, 3 * c + i + 1)
                    if c:
                        act.wait_ge(ab_filled, c)
                    nc.scalar.copy(wT[:, i, :, :], pT[i][:]).then_inc(wT_taken, 1)
                act.wait_ge(ab_filled, c + 1)
                if c == 0:
                    act.wait_ge(gates_ready, 1)
                nc.scalar.activation(value_w[:, 4 * c:4 * c + 4, :], pB[:], ACT.Copy,
                                     scale=gates[:, 0:1]).then_inc(ab_taken, 1)
            for n in (ROOT_AT, LN_STEPS + ROOTS_AT[0], LN_STEPS + ROOTS_AT[1]):
                act.wait_ge(ln_step, n)
                nc.scalar.activation(tmp[:, 2, :], tmp[:, 0, :], ACT.Sqrt).then_inc(sqrt_ready, 1)

        @block.tensor
        def _(pe):
            pe.wait_ge(ident_ready, 1)
            pe.wait_ge(weights_in, 48)
            for c in range(4):
                for i in range(3):
                    if c:
                        pe.wait_ge(wT_taken, 3 * (c - 1) + i + 1)
                    for h in range(4):
                        col = (4 * c + h) * DH0
                        src = (wq_sb, wkv_sb, wkv_sb)[i][:, (0, 0, INNER)[i] + col:(0, 0, INNER)[i] + col + DH0]
                        last = nc.tensor.transpose(pT[i][:, h, :], src, ident[:])
                    last.then_inc(wT_filled, 1)
                pe.wait_ge(wT_taken, 3 * c + 3)
                if c:
                    pe.wait_ge(ab_taken, 2 * c)
                for h in range(4):
                    nc.tensor.matmul(pA[:, h, :], wT[:, 0, h, :], wT[:, 1, h, :], start=True, stop=True)
                    last = nc.tensor.matmul(pB[:, h, :], wT[:, 2, h, :], wo_sb[:, 4 * c + h, :], start=True, stop=True)
                last.then_inc(ab_filled, 1)

        @block.vector
        def _(vec):
            for c in range(4):
                hs = slice(4 * c, 4 * c + 4)
                vec.wait_ge(ab_filled, c + 1)
                nc.vector.tensor_scalar(scaled[:], pA[:], SCALE0, None, ALU.mult).then_inc(scaled_ready, 1)
                vec.wait_ge(scaled_ready, c + 1)
                nc.vector.tensor_copy(score_hi[:, hs, :], scaled[:]).then_inc(score_hi_ready, 1)
                vec.wait_ge(score_hi_ready, c + 1)
                nc.vector.tensor_tensor(score_lo[:, hs, :], scaled[:], score_hi[:, hs, :].bitcast(F32),
                                        ALU.subtract).then_inc(ab_taken, 1)
            for i in range(NL):
                vec.wait_ge(rows_in[i], 32)
                for t in range(i * LT, (i + 1) * LT):
                    nc.vector.bn_stats(stats[:, t, :], x_sb[:, t, :])
                    last = nc.vector.bn_stats(cstats[:, t, :], ctx_sb[:, t, :])
            last.then_inc(stats_done, 1)
            vec.wait_ge(stats_done, 1)
            steps = layer_norm_factors(nc, vec, cstats, cmean, crstd, tmp, ln_step, sqrt_ready, 0, 0, False)
            layer_norm_factors(nc, vec, stats, mean, rstd, tmp, ln_step, sqrt_ready, steps, 1, True)

    normed = sb("a0_normed", [P, 4, D])
    kvT = [sb(f"a0_kvT{j}", [P, GB, 2, S]) for j in range(2)]
    latT_hi, latT_lo = sb("a0_latT_hi", [P, GB, S], F32R), sb("a0_latT_lo", [P, GB, S], F32R)
    kv_rows = [sb(f"a0_kv_rows{j}", [P, GB, D]) for j in range(2)]
    queries = [sb(f"a0_queries{j}", [P, H0 // 2, GB, 2, S]) for j in range(2)]
    attended = [sb(f"a0_attended{j}", [P, H0, GB, S]) for j in range(2)]
    shifted = [sb(f"a0_shifted{i}", [P, 4, P]) for i in range(2)]
    exps = [sb(f"a0_exps{i}", [P, 4, P]) for i in range(2)]
    probs = [sb(f"a0_probs{i}", [P, 4, P]) for i in range(2)]
    probsT = [sb(f"a0_probsT{i}", [P, 4 * P]) for i in range(2)]
    negmax = [sb(f"a0_negmax{i}", [P, 4]) for i in range(2)]
    sums = [sb(f"a0_sums{i}", [P, 4]) for i in range(2)]
    rsums = [sb(f"a0_rsums{i}", [P, 4]) for i in range(2)]
    projT = sb("a0_projT", [P, GT])

    def ps(name, shape):
        return stack.enter_context(nc.psum_tensor("a0_" + name, shape, F32))

    p_scores = [ps(f"p_scores{i}", [P, 4, P]) for i in range(2)]
    p_probsT = [ps(f"p_probsT{i}", [P, 4 * P]) for i in range(2)]
    p_attended = ps("p_attended", [P, UN, S])
    p_queries = ps("p_queries", [P, 2, GB, S])
    p_turn = ps("p_turn", [P, 4, P])
    p_proj = ps("p_proj", [P, GT])

    normed_ready = sem("normed_ready")
    rows_turned = sem("rows_turned")
    kvT_ready = sem("kvT_ready")
    lat_hi_ready, lat_ready = sem("lat_hi_ready"), sem("lat_ready")
    keys_turned = sem("keys_turned")
    kv_rows_ready = sem("kv_rows_ready")
    queries_made, queries_ready = sem("queries_made"), sem("queries_ready")
    scores_made = sem("scores_made")
    max_ready, shifted_ready, exps_ready = sem("max_ready"), sem("shifted_ready"), sem("exps_ready")
    sums_ready, rsums_ready, probs_ready = sem("sums_ready"), sem("rsums_ready"), sem("probs_ready")
    probs_turned, probsT_ready = sem("probs_turned"), sem("probsT_ready")
    attended_made, attended_ready = sem("attended_made"), sem("attended_ready")
    proj_made, proj_ready = sem("proj_made"), sem("proj_ready")
    proj_turned, stream_ready = sem("proj_turned"), sem("stream_ready")
    stats_written = sem("stats_written")
    block = stack.enter_context(nc.Block())

    QUERY_CHUNKS = {2: [0], 3: [1], 4: [2], 5: [3, 4], 6: [5, 6], 7: [7]}

    def unit_before(g, u, lag):
        return (g, u - lag) if u >= lag else (g - 1, u - lag + UN)

    def over_groups(engine, steps):
        for g in range(-2, 2):
            steps(g, g % 2)
        with engine.Fori(1, NG // 2 - 1) as it:
            for j in range(2):
                steps(2 * it + j, j)
        for g in range(NG - 2, NG + 2):
            steps(g, g % 2)

    @block.tensor
    def _(pe):
        def query_chunk(g, j, c):
            pe.wait_ge(lat_ready, g + 1)
            if exists(g - 1, NG) or c:
                pe.wait_ge(queries_ready, 8 * g + c)
            for h in range(2):
                o = p_queries[:, h, :, :]
                w_hi, w_lo = score_hi[:, 2 * c + h, :], score_lo[:, 2 * c + h, :]
                nc.tensor.matmul(o, w_hi, latT_hi[:], start=True, stop=False)
                nc.tensor.matmul(o, w_hi, latT_lo[:], start=False, stop=False)
                last = nc.tensor.matmul(o, w_lo, latT_hi[:], start=False, stop=True)
            last.then_inc(queries_made, 1)

        def project(g, j, quarter):
            if quarter == 0:
                pe.wait_ge(attended_ready, UN * (g + 1))
                if exists(g - 1, NG):
                    pe.wait_ge(proj_ready, g)
            for h in range(4 * quarter, 4 * quarter + 4):
                last = nc.tensor.matmul(p_proj[:], value_w[:, h, :], attended[j][:, h, :, :],
                                        start=h == 0, stop=h == H0 - 1)
            if quarter == 3:
                last.then_inc(proj_made, 1)

        def steps(g, j):
            for u in range(UN):
                if exists(g, NG):
                    b, half = u // 2, u % 2
                    if u < 2:
                        pe.wait_ge(queries_ready, 8 * g + 4 * half + 4)
                    if exists(g - 1, NG) or u >= 2:
                        pe.wait_ge(shifted_ready, UN * g + u - 1)
                    for i in range(4):
                        last = nc.tensor.matmul(p_scores[u % 2][:, i, :], queries[j][:, 4 * half + i, b, :, :],
                                                kvT[j][:, b, :, :], start=True, stop=True)
                    last.then_inc(scores_made, 1)
                gt, ut = unit_before(g, u, 2)
                if exists(gt, NG):
                    pe.wait_ge(probs_ready, UN * gt + ut + 1)
                    if exists(gt - 1, NG) or ut >= 2:
                        pe.wait_ge(probsT_ready, UN * gt + ut - 1)
                    for i in range(4):
                        last = nc.tensor.transpose(p_probsT[u % 2][:, i * P:(i + 1) * P], probs[u % 2][:, i, :], ident[:])
                    last.then_inc(probs_turned, 1)
                ga, ua = unit_before(g, u, 3)
                ja = j if u >= 3 else 1 - j
                if exists(ga, NG):
                    pe.wait_ge(probsT_ready, UN * ga + ua + 1)
                    if ua == 0:
                        pe.wait_ge(kv_rows_ready, ga + 1)
                    if exists(ga - 1, NG) or ua >= 1:
                        pe.wait_ge(attended_ready, UN * ga + ua)
                    nc.tensor.matmul(p_attended[:], kv_rows[ja][:, ua // 2, :], probsT[ua % 2][:],
                                     start=True, stop=True).then_inc(attended_made, 1)
                if u == 0 and exists(g + 1, NG):
                    pe.wait_ge(normed_ready, g + 2)
                    if exists(g - 3, NG):
                        pe.wait_ge(stream_ready, g - 2)
                    for i in range(4):
                        last = nc.tensor.transpose(p_turn[:, i, :], normed[:, i, :], ident[:])
                    last.then_inc(rows_turned, 1)
                if u == 1 and exists(g + 1, NG):
                    pe.wait_ge(kvT_ready, 2 * (g + 2))
                    for b in range(GB):
                        last = nc.tensor.transpose(p_turn[:, b, :], kvT[1 - j][:, b, :, :], ident[:])
                    last.then_inc(keys_turned, 1)
                if u == 2 and exists(g - 2, NG):
                    if exists(g + 1, NG):
                        pe.wait_ge(kv_rows_ready, g + 2)
                    elif exists(g - 3, NG):
                        pe.wait_ge(stream_ready, g - 2)
                    pe.wait_ge(proj_ready, g - 1)
                    for t in range(2):
                        last = nc.tensor.transpose(p_turn[:, t, :], projT[:, t * P:(t + 1) * P], ident[:])
                    last.then_inc(proj_turned, 1)
                chunks = QUERY_CHUNKS.get(u, []) if exists(g + 1, NG) else []
                if chunks:
                    query_chunk(g + 1, 1 - j, chunks[0])
                if 3 <= u < 7 and exists(g - 1, NG):
                    project(g - 1, 1 - j, u - 3)
                if len(chunks) > 1:
                    query_chunk(g + 1, 1 - j, chunks[1])

        over_groups(pe, steps)

    @block.scalar
    def _(act):
        def take_queries(g, j, c):
            act.wait_ge(queries_made, 8 * g + c + 1)
            if c == 0 and exists(g - 2, NG):
                act.wait_ge(scores_made, UN * (g - 1))
            nc.scalar.copy(queries[j][:, c, :, :, :].rearrange("p b h s -> p h b s"), p_queries[:]).then_inc(queries_ready, 1)

        def steps(g, j):
            for u in range(UN):
                if exists(g, NG):
                    act.wait_ge(shifted_ready, UN * g + u + 1)
                    if exists(g - 1, NG) or u >= 2:
                        act.wait_ge(probs_ready, UN * g + u - 1)
                    nc.scalar.activation(exps[u % 2][:], shifted[u % 2][:], ACT.Exp).then_inc(exps_ready, 1)
                gt, ut = unit_before(g, u, 2)
                if exists(gt, NG):
                    act.wait_ge(probs_turned, UN * gt + ut + 1)
                    if exists(gt - 1, NG) or ut >= 2:
                        act.wait_ge(attended_made, UN * gt + ut - 1)
                    nc.scalar.copy(probsT[u % 2][:], p_probsT[u % 2][:]).then_inc(probsT_ready, 1)
                ga, ua = unit_before(g, u, 3)
                ja = j if u >= 3 else 1 - j
                if exists(ga, NG):
                    act.wait_ge(attended_made, UN * ga + ua + 1)
                    if ua == 0 and exists(ga - 2, NG):
                        act.wait_ge(proj_made, ga - 1)
                    nc.scalar.copy(attended[ja][:, UN * (ua % 2):UN * (ua % 2) + UN, ua // 2, :],
                                   p_attended[:]).then_inc(attended_ready, 1)
                if u == 0 and exists(g + 1, NG):
                    act.wait_ge(rows_turned, g + 2)
                    if exists(g - 1, NG):
                        act.wait_ge(scores_made, UN * g)
                    for kind in range(2):
                        src = p_turn[:, 2 * kind:2 * kind + 2, :].rearrange("p t (two s) -> p (t two) s", two=2)
                        nc.scalar.activation(kvT[1 - j][:, :, kind, :], src, ACT.Identity,
                                             scale=cols[:, 2 * kind:2 * kind + 1],
                                             bias=cols[:, 2 * kind + 1:2 * kind + 2]).then_inc(kvT_ready, 1)
                if exists(g + 1, NG):
                    for c in QUERY_CHUNKS.get(u, []):
                        take_queries(g + 1, 1 - j, c)
                if u == 7 and exists(g - 1, NG):
                    act.wait_ge(proj_made, g)
                    if exists(g - 2, NG):
                        act.wait_ge(proj_turned, g - 1)
                    nc.scalar.copy(projT[:], p_proj[:]).then_inc(proj_ready, 1)

        over_groups(act, steps)

    @block.vector
    def _(vec):
        def steps(g, j):
            for u in range(UN):
                if u == 1 and exists(g + 1, NG):
                    vec.wait_ge(kvT_ready, 2 * (g + 2))
                    if exists(g, NG):
                        vec.wait_ge(queries_made, 8 * (g + 1))
                    nc.vector.tensor_copy(latT_hi[:], kvT[1 - j][:, :, 1, :]).then_inc(lat_hi_ready, 1)
                    vec.wait_ge(lat_hi_ready, g + 2)
                    nc.vector.tensor_tensor(latT_lo[:], kvT[1 - j][:, :, 1, :], latT_hi[:].bitcast(F32),
                                            ALU.subtract).then_inc(lat_ready, 1)
                if exists(g, NG):
                    k = UN * g + u
                    vec.wait_ge(scores_made, k + 1)
                    if exists(g - 1, NG) or u >= 2:
                        vec.wait_ge(shifted_ready, k - 1)
                    nc.vector.tensor_reduce(negmax[u % 2][:], p_scores[u % 2][:], AX.X, ALU.max,
                                            negate=True).then_inc(max_ready, 1)
                    vec.wait_ge(max_ready, k + 1)
                    if exists(g - 1, NG) or u >= 2:
                        vec.wait_ge(exps_ready, k - 1)
                    nc.vector.tensor_tensor(shifted[u % 2][:], p_scores[u % 2][:],
                                            negmax[u % 2][:].unsqueeze(2).broadcast_to([P, 4, P]),
                                            ALU.add).then_inc(shifted_ready, 1)
                gs, us = unit_before(g, u, 1)
                if exists(gs, NG):
                    k = UN * gs + us
                    vec.wait_ge(exps_ready, k + 1)
                    if exists(gs - 1, NG) or us >= 2:
                        vec.wait_ge(probs_ready, k - 1)
                    nc.vector.tensor_reduce(sums[us % 2][:], exps[us % 2][:], AX.X, ALU.add).then_inc(sums_ready, 1)
                    vec.wait_ge(sums_ready, k + 1)
                    nc.vector.reciprocal(rsums[us % 2][:], sums[us % 2][:]).then_inc(rsums_ready, 1)
                if u == 1 and exists(g + 1, NG):
                    vec.wait_ge(keys_turned, g + 2)
                    if exists(g - 1, NG):
                        vec.wait_ge(attended_made, UN * g)
                    nc.vector.tensor_copy(kv_rows[1 - j][:], p_turn[:]).then_inc(kv_rows_ready, 1)
                if u == 3 and exists(g - 2, NG):
                    vec.wait_ge(proj_turned, g - 1)
                    tiles = x_sb[:, bass.ds(2 * (g - 2), 2), :]
                    nc.vector.tensor_tensor(tiles, p_turn[:, 0:2, :], tiles, ALU.add).then_inc(stream_ready, 1)
                if u == 4 and exists(g + 2, NG):
                    if exists(g + 1, NG):
                        vec.wait_ge(rows_turned, g + 2)
                    for kind, (rows, m, r) in enumerate(((ctx_sb, cmean, crstd), (x_sb, mean, rstd))):
                        for t in range(2):
                            tile = 2 * (g + 2) + t
                            last = nc.vector.tensor_scalar(normed[:, 2 * kind + t, :], rows[:, bass.ds(tile, 1), :],
                                                           m[:, bass.ds(tile, 1)], r[:, bass.ds(tile, 1)],
                                                           ALU.subtract, ALU.mult)
                    last.then_inc(normed_ready, 1)
                if u == 5 and exists(g - 2, NG):
                    vec.wait_ge(stream_ready, g - 1)
                    for t in range(2):
                        tile = 2 * (g - 2) + t
                        last = nc.vector.bn_stats(stats[:, bass.ds(tile, 1), :], x_sb[:, bass.ds(tile, 1), :])
                    last.then_inc(stats_written, 1)

        over_groups(vec, steps)
        vec.wait_ge(stats_written, NG)

    @block.gpsimd
    def _(pool):
        def steps(g, j):
            for u in range(UN):
                gs, us = unit_before(g, u, 1)
                if exists(gs, NG):
                    k = UN * gs + us
                    pool.wait_ge(rsums_ready, k + 1)
                    if exists(gs - 1, NG) or us >= 2:
                        pool.wait_ge(probs_turned, k - 1)
                    nc.gpsimd.tensor_tensor(probs[us % 2][:], exps[us % 2][:],
                                            rsums[us % 2][:].unsqueeze(2).broadcast_to([P, 4, P]),
                                            ALU.mult).then_inc(probs_ready, 1)

        over_groups(pool, steps)


def new_factors(nc, new_sem, tag, stats, mean, rstd, tmp):
    step_done = new_sem(tag + "_ln_step")
    sqrt_ready = new_sem(tag + "_sqrt_ready")

    def on_vector(vec):
        layer_norm_factors(nc, vec, stats, mean, rstd, tmp, step_done, sqrt_ready, 0, 0, False)

    def on_scalar(act):
        act.wait_ge(step_done, ROOT_AT)
        nc.scalar.activation(tmp[:, 2, :], tmp[:, 0, :], ACT.Sqrt).then_inc(sqrt_ready, 1)

    return on_vector, on_scalar


def expert_weights_0(nc, stack, new_sem, gate0, gate0_b, w1_0, b1_0, w2_0, b2_0, stats, mean, rstd, tmp):
    def sb(name, shape, dt=F32):
        return stack.enter_context(nc.sbuf_tensor("m0_" + name, shape, dt))

    n_chunks = F0 // P
    up = [(sb("up_hi", [P, E0 * n_chunks, P], F32R), sb("up_lo", [P, E0 * n_chunks, P], F32R))]
    down = (sb("down_hi", [P, E0 * n_chunks, P], F32R), sb("down_lo", [P, E0 * n_chunks, P], F32R))
    router, router_b = sb("router", [P, E0]), sb("router_b", [P, E0])
    up_b, down_b = sb("up_b", [P, E0, n_chunks]), sb("down_b", [P, E0])
    with ExitStack() as setup:
        raw = [setup.enter_context(nc.sbuf_tensor(f"m0_raw{i}", [P, E0 * n_chunks, P], F32)) for i in range(2)]
        weights_in = [new_sem(f"m0_in{i}") for i in range(4)]
        small_in = new_sem("m0_small_in")
        hi_ready = new_sem("m0_weights_hi")
        factors_vector, factors_scalar = new_factors(nc, new_sem, "m0", stats, mean, rstd, tmp)
        block = setup.enter_context(nc.Block())
        half = E0 // 2
        views = [(raw[0], w1_0.rearrange("e d (c m) -> d e c m", m=P)), (raw[1], w2_0.rearrange("e (c p) f -> p e c f", p=P))]
        parts = [(i, s) for s in range(2) for i in range(2)]

        @block.sync
        def _(sp):
            for n, (i, s) in enumerate(parts):
                dst = views[i][0][:].rearrange("p (e c) m -> p e c m", e=E0)
                for e in range(s * half, (s + 1) * half):
                    sp.dma_start(dst[:, e, :, :], views[i][1][:, e, :, :]).then_inc(weights_in[n], 16)

        @block.gpsimd
        def _(pool):
            pool.dma_start(router[:], gate0).then_inc(small_in, 16)
            pool.dma_start(router_b[:], gate0_b.rearrange("(a n) -> a n", a=1).broadcast_to([P, E0])).then_inc(small_in, 16)
            for e in range(E0):
                pool.dma_start(up_b[:, e, :], b1_0[e, :].rearrange("(c p) -> p c", p=P),
                               allow_slow_non_contiguous=True).then_inc(small_in, 16)
            pool.dma_start(down_b[:], b2_0.rearrange("e f -> f e"), allow_slow_non_contiguous=True).then_inc(small_in, 16)
            pool.wait_ge(small_in, 16 * (E0 + 3))

        @block.scalar
        def _(act):
            factors_scalar(act)
            for n, (i, s) in enumerate(parts):
                rows = slice(s * half * n_chunks, (s + 1) * half * n_chunks)
                act.wait_ge(weights_in[n], 16 * half)
                nc.scalar.copy((up[0], down)[i][0][:, rows, :], raw[i][:, rows, :]).then_inc(hi_ready, 1)

        @block.vector
        def _(vec):
            factors_vector(vec)
            for n, (i, s) in enumerate(parts):
                rows = slice(s * half * n_chunks, (s + 1) * half * n_chunks)
                hi, lo = (up[0], down)[i]
                vec.wait_ge(hi_ready, n + 1)
                nc.vector.tensor_tensor(lo[:, rows, :], raw[i][:, rows, :], hi[:, rows, :].bitcast(F32), ALU.subtract)

    return up, down, router, router_b, up_b, down_b


def expert_weights_1(nc, stack, new_sem, gate1, w1_1, w3_1, w2_1, ident, stats, mean, rstd, tmp):
    def sb(name, shape, dt=F32):
        return stack.enter_context(nc.sbuf_tensor("m1_" + name, shape, dt))

    n_chunks = I1 // P
    up = [(sb(f"up_hi{i}", [P, E1 * n_chunks, P], F32R), sb(f"up_lo{i}", [P, E1 * n_chunks, P], F32R)) for i in range(2)]
    down = (sb("down_hi", [P, E1 * n_chunks, P], F32R), sb("down_lo", [P, E1 * n_chunks, P], F32R))
    router = sb("router", [P, E1])
    with ExitStack() as setup:
        raw = [setup.enter_context(nc.sbuf_tensor(f"m1_raw{i}", [P, E1 * n_chunks, P], F32)) for i in range(3)]
        raw_router = setup.enter_context(nc.sbuf_tensor("m1_raw_router", [E1, P], F32))
        banks = [setup.enter_context(nc.psum_tensor(f"m1_bank{i}", [P, 4, P], F32)) for i in range(4)]
        weights_in = [new_sem(f"m1_in{i}") for i in range(4)]
        turned = new_sem("m1_turned")
        hi_ready = new_sem("m1_weights_hi")
        lo_ready = new_sem("m1_weights_lo")
        router_turned = new_sem("m1_router_turned")
        factors_vector, factors_scalar = new_factors(nc, new_sem, "m1", stats, mean, rstd, tmp)
        block = setup.enter_context(nc.Block())
        quads = E1 * n_chunks // 4
        hi_lo = [up[0], up[1], down]

        @block.sync
        def _(sp):
            sp.dma_start(raw_router[:], gate1).then_inc(weights_in[3], 16)
            for i, w in enumerate((w1_1, w3_1)):
                sp.dma_start(raw[i][:].rearrange("p (e c) h -> p e c h", e=E1),
                             w.rearrange("e (c p) h -> p e c h", p=P)).then_inc(weights_in[i], 16)
            sp.dma_start(raw[2][:].rearrange("p (e c) i -> p e (c i)", e=E1),
                         w2_1.rearrange("e h i -> h e i")).then_inc(weights_in[2], 16)

        @block.tensor
        def _(pe):
            for i in range(3):
                pe.wait_ge(weights_in[i], 16)
                for q in range(quads):
                    n = quads * i + q
                    if n >= 4:
                        pe.wait_ge(lo_ready, n - 3)
                    for b in range(4):
                        last = nc.tensor.transpose(banks[n % 4][:, b, :], raw[i][:, 4 * q + b, :], ident[:])
                    last.then_inc(turned, 1)
            pe.wait_ge(weights_in[3], 16)
            pe.wait_ge(lo_ready, 3 * quads - 3)
            nc.tensor.transpose(banks[0][:, 0, 0:E1], raw_router[:], ident[0:E1, 0:E1]).then_inc(router_turned, 1)

        @block.scalar
        def _(act):
            factors_scalar(act)
            for n in range(3 * quads):
                i, q = divmod(n, quads)
                act.wait_ge(turned, n + 1)
                nc.scalar.copy(hi_lo[i][0][:, 4 * q:4 * q + 4, :], banks[n % 4][:]).then_inc(hi_ready, 1)

        @block.vector
        def _(vec):
            factors_vector(vec)
            for n in range(3 * quads):
                i, q = divmod(n, quads)
                hi, lo = hi_lo[i]
                vec.wait_ge(hi_ready, n + 1)
                nc.vector.tensor_tensor(lo[:, 4 * q:4 * q + 4, :], banks[n % 4][:], hi[:, 4 * q:4 * q + 4, :].bitcast(F32),
                                        ALU.subtract).then_inc(lo_ready, 1)
            vec.wait_ge(router_turned, 1)
            nc.vector.tensor_copy(router[:], banks[0][:, 0, 0:E1])

    return up, down, router


def experts(nc, stack, new_sem, tag, up, down, router, router_b, up_b, down_b, sum_eps, gate_col,
            x_sb, ident, gates, stats, mean, rstd, out):
    n_exp = 8
    n_chunks = down[0].shape[1] // n_exp
    gated = up_b is None
    N = n_exp * n_chunks
    LAG = 2 if gated else 3
    OUT_TURN, ROWS_TURN, LOGITS = (4, 5, 7) if gated else (7, 9, 12)
    BROADCAST = 1 if gated else 2
    GATE_A, GATE_B, GATE_C = (8, 10, 12) if gated else (14, 18, 22)
    TT = MT // P

    def sb(name, shape, dt=F32):
        return stack.enter_context(nc.sbuf_tensor(f"{tag}_{name}", shape, dt))

    def sem(name):
        return new_sem(f"{tag}_{name}")

    def ps(name, shape):
        return stack.enter_context(nc.psum_tensor(f"{tag}_{name}", shape, F32))

    normed = sb("normed", [P, TT, D])
    xT = sb("xT", [P, MT])
    xT_hi, xT_lo = sb("xT_hi", [P, MT], F32R), sb("xT_lo", [P, MT], F32R)
    silu = [sb(f"silu{i}", [P, MT]) for i in range(2)] if gated else None
    hidden = [sb(f"hidden{i}", [P, MT]) for i in range(4)]
    hidden_hi = [sb(f"hidden_hi{i}", [P, MT], F32R) for i in range(4)]
    hidden_lo = [sb(f"hidden_lo{i}", [P, MT], F32R) for i in range(4)]
    gate_rows = [sb(f"gate_rows{i}", [P, MT]) for i in range(2)]
    terms = [sb(f"terms{i}", [P, MT]) for i in range(2)]
    acc = sb("acc", [P, MT])
    small = {name: sb(name, [P, TT, n_exp]) for name in ("logits", "shifted", "exps", "soft", "rank", "mask", "weights")}
    per_row = {name: sb(name, [P, TT]) for name in ("negmax", "sums", "rsums", "chosen", "rchosen")}
    above, equal = sb("above", [P, TT, n_exp, n_exp]), sb("equal", [P, TT, n_exp, n_exp])
    earlier = sb("earlier", [P, n_exp, n_exp])
    ones = sb("ones", [P, 1])
    picks = sb("picks", [64, n_exp, P])
    picks_r = sb("picks_r", [64, n_exp, P], F32R)
    gatesT = sb("gatesT", [64, MT], F32R)

    p_hidden = [ps(f"p_hidden{i}", [P, MT]) for i in range(4)]
    p_out = [ps(f"p_out{i}", [P, MT]) for i in range(2)]
    p_turn = ps("p_turn", [P, MT])
    p_gate = ps("p_gate", [P, MT])

    const_step, const_ready = sem("const_step"), sem("const_ready")
    normed_ready, rows_turned, xT_ready = sem("normed_ready"), sem("rows_turned"), sem("xT_ready")
    xT_hi_ready, split_ready = sem("xT_hi_ready"), sem("split_ready")
    logits_made, gate_step, exps_ready = sem("logits_made"), sem("gate_step"), sem("exps_ready")
    weights_turned, gatesT_hi_ready, gatesT_ready = sem("weights_turned"), sem("gatesT_hi_ready"), sem("gatesT_ready")
    gate_spread, gate_rows_ready = sem("gate_spread"), sem("gate_rows_ready")
    up_made, silu_ready, hidden_ready = sem("up_made"), sem("silu_ready"), sem("hidden_ready")
    own_hi_ready = sem("own_hi_ready")
    hi_ready, lo_ready, down_made = sem("hi_ready"), sem("lo_ready"), sem("down_made")
    term_ready, added = sem("term_ready"), sem("added")
    acc_turned, stream_ready, stats_written = sem("acc_turned"), sem("stream_ready"), sem("stats_written")
    stored = sem("stored") if out is not None else None
    block = stack.enter_context(nc.Block())
    STEPS_A, STEPS_B, STEPS_C = 3, 5, 8
    STEPS = STEPS_A + STEPS_B + STEPS_C

    SHARE = 1 if gated else 2
    POOL_CHUNKS = N // SHARE

    def on_pool(n):
        return n % SHARE == 0

    def chunk_before(g, n, lag):
        return (g, n - lag) if n >= lag else (g - 1, n - lag + N)

    def over_groups(engine, steps):
        for g in (-1, 0):
            steps(g)
        with engine.Fori(1, NM - 1) as g:
            steps(g)
        for g in (NM - 1, NM):
            steps(g)

    @block.sync
    def _(sp):
        if out is not None:
            view = out.rearrange("(t two) s d -> (two s) t d", two=2)
            with sp.Fori(0, NM) as g:
                sp.wait_ge(stream_ready, g + 1)
                sp.dma_start(view[:, bass.ds(TT * g, TT), :], x_sb[:, bass.ds(TT * g, TT), :]).then_inc(stored, 16)
            sp.wait_ge(stored, 16 * NM)

    @block.tensor
    def _(pe):
        pe.wait_ge(const_ready, 3)

        def split_product(o, w, row, hi, lo, first, last_one):
            nc.tensor.matmul(o, w[0][:, row, :], hi, start=first, stop=False)
            nc.tensor.matmul(o, w[0][:, row, :], lo, start=False, stop=False)
            return nc.tensor.matmul(o, w[1][:, row, :], hi, start=False, stop=last_one)

        def steps(g):
            for n in range(N):
                e, c = divmod(n, n_chunks)
                if exists(g, NM):
                    if n == 0:
                        pe.wait_ge(split_ready, g + 1)
                    if gated:
                        if exists(g - 1, NM) or n >= 2:
                            pe.wait_ge(hidden_ready, N * g + n - 1)
                        split_product(p_hidden[n % 2][:], up[0], n, xT_hi[:], xT_lo[:], True, True)
                        split_product(p_hidden[2 + n % 2][:], up[1], n, xT_hi[:], xT_lo[:], True, True).then_inc(up_made, 1)
                    else:
                        if exists(g - 1, NM) or n >= 4:
                            pe.wait_ge(hidden_ready, N * g + n - 3)
                        split_product(p_hidden[n % 4][:], up[0], n, xT_hi[:], xT_lo[:], True, True).then_inc(up_made, 1)
                    if c == BROADCAST:
                        if e == 0:
                            pe.wait_ge(gatesT_ready, g + 1)
                        if exists(g - 1, NM) or e:
                            pe.wait_ge(gate_rows_ready, n_exp * g + e)
                        nc.tensor.matmul(p_gate[:], picks_r[:, e, :], gatesT[:], start=True, stop=True).then_inc(gate_spread, 1)
                gd, nd = chunk_before(g, n, LAG)
                if exists(gd, NM):
                    ed, cd = divmod(nd, n_chunks)
                    pe.wait_ge(lo_ready, N * gd + nd + 1)
                    if cd == 0 and (exists(gd - 1, NM) or ed >= 2):
                        pe.wait_ge(term_ready, n_exp * gd + ed - 1)
                    split_product(p_out[ed % 2][:], down, nd, hidden_hi[nd % 4][:], hidden_lo[nd % 4][:],
                                  cd == 0, cd == n_chunks - 1).then_inc(down_made, 1)
                if n == OUT_TURN and exists(g - 1, NM):
                    pe.wait_ge(added, (n_exp - 1) * g)
                    if exists(g, NM):
                        pe.wait_ge(gatesT_ready, g + 1)
                    else:
                        pe.wait_ge(gatesT_ready, g)
                    for t in range(TT):
                        last = nc.tensor.transpose(p_turn[:, t * P:(t + 1) * P], acc[:, t * P:(t + 1) * P], ident[:])
                    last.then_inc(acc_turned, 1)
                if n == ROWS_TURN and exists(g + 1, NM):
                    pe.wait_ge(normed_ready, g + 2)
                    if exists(g - 1, NM):
                        pe.wait_ge(stream_ready, g)
                    elif exists(g, NM):
                        pe.wait_ge(gatesT_ready, g + 1)
                    for t in range(TT):
                        last = nc.tensor.transpose(p_turn[:, t * P:(t + 1) * P], normed[:, t, :], ident[:])
                    last.then_inc(rows_turned, 1)
                if n == LOGITS and exists(g + 1, NM):
                    pe.wait_ge(xT_ready, g + 2)
                    for t in range(TT):
                        last = nc.tensor.matmul(p_turn[:, t * n_exp:(t + 1) * n_exp], xT[:, t * P:(t + 1) * P], router[:],
                                                start=True, stop=True)
                    last.then_inc(logits_made, 1)
                if n == N - 1 and exists(g + 1, NM):
                    pe.wait_ge(gate_step, STEPS * (g + 2))
                    for t in range(TT):
                        last = nc.tensor.transpose(p_turn[0:n_exp, t * P:(t + 1) * P], small["weights"][:, t, :], ident[:])
                    last.then_inc(weights_turned, 1)

        over_groups(pe, steps)

    @block.scalar
    def _(act):
        def steps(g):
            for n in range(N):
                e, c = divmod(n, n_chunks)
                if exists(g, NM):
                    act.wait_ge(up_made, N * g + n + 1)
                    if gated:
                        if exists(g - 1, NM) or n >= 2:
                            act.wait_ge(hidden_ready, N * g + n - 1)
                        nc.scalar.activation(silu[n % 2][:], p_hidden[n % 2][:], ACT.Silu).then_inc(silu_ready, 1)
                    else:
                        if exists(g - 1, NM) or n >= 4:
                            act.wait_ge(lo_ready, N * g + n - 3)
                        nc.scalar.activation(hidden[n % 4][:], p_hidden[n % 4][:], ACT.Gelu_apprx_tanh,
                                             bias=up_b[:, e, c:c + 1]).then_inc(hidden_ready, 1)
                    if c == BROADCAST:
                        act.wait_ge(gate_spread, n_exp * g + e + 1)
                        if exists(g - 1, NM) or e >= 2:
                            act.wait_ge(term_ready, n_exp * g + e - 1)
                        nc.scalar.copy(gate_rows[e % 2][:], p_gate[:]).then_inc(gate_rows_ready, 1)
                if n == ROWS_TURN + 1 and exists(g + 1, NM):
                    act.wait_ge(rows_turned, g + 2)
                    if exists(g, NM):
                        act.wait_ge(split_ready, g + 1)
                        act.wait_ge(logits_made, g + 1)
                    nc.scalar.copy(xT[:], p_turn[:]).then_inc(xT_ready, 1)
                if n == GATE_A + 1 and exists(g + 1, NM):
                    act.wait_ge(gate_step, STEPS * (g + 1) + STEPS_A)
                    nc.scalar.activation(small["exps"][:], small["shifted"][:], ACT.Exp).then_inc(exps_ready, 1)

        over_groups(act, steps)

    @block.gpsimd
    def _(pool):
        nc.gpsimd.memset(earlier[:], 1.0).then_inc(const_step, 1)
        nc.gpsimd.memset(picks[:], 0.0).then_inc(const_step, 1)
        nc.gpsimd.memset(ones[:], 1.0).then_inc(const_step, 1)
        nc.gpsimd.memset(gatesT[:].bitcast(F32), 0.0).then_inc(const_ready, 1)
        pool.wait_ge(const_step, 3)
        nc.gpsimd.affine_select(out=earlier[:], in_=earlier[:], compare_op=ALU.is_gt, fill=0.0, base=0,
                                pattern=[[1, n_exp], [-1, n_exp]], channel_multiplier=0).then_inc(const_ready, 1)
        nc.gpsimd.affine_select(out=picks[:], in_=picks[:], compare_op=ALU.not_equal, fill=1.0, base=0,
                                pattern=[[-1, n_exp], [0, P]], channel_multiplier=1).then_inc(const_step, 1)
        pool.wait_ge(const_step, 4)
        nc.gpsimd.affine_select(out=picks[:], in_=picks[:], compare_op=ALU.not_equal, fill=1.0, base=-32,
                                pattern=[[-1, n_exp], [0, P]], channel_multiplier=1).then_inc(const_step, 1)
        pool.wait_ge(const_step, 5)
        nc.gpsimd.tensor_copy(picks_r[:], picks[:]).then_inc(const_ready, 1)

        def steps(g):
            for n in range(N):
                if exists(g, NM) and on_pool(n):
                    k = N * g + n
                    pool.wait_ge(hidden_ready, k + 1)
                    if exists(g - 1, NM) or n >= 4:
                        pool.wait_ge(down_made, k - 3)
                    nc.gpsimd.tensor_tensor(hidden_hi[n % 4][:], hidden[n % 4][:], ones[:].broadcast_to([P, MT]),
                                            ALU.mult).then_inc(hi_ready, 1)
                gd, nd = chunk_before(g, n, LAG + 1)
                ed, cd = divmod(nd, n_chunks)
                if exists(gd, NM) and cd == n_chunks - 1 and ed:
                    pool.wait_ge(term_ready, n_exp * gd + ed + 1)
                    if ed > 1:
                        pool.wait_ge(added, (n_exp - 1) * gd + ed - 1)
                    nc.gpsimd.tensor_tensor(acc[:], acc[:], terms[ed % 2][:], ALU.add).then_inc(added, 1)

        over_groups(pool, steps)

    @block.vector
    def _(vec):
        vec.wait_ge(const_ready, 3)

        def split_rows(g):
            vec.wait_ge(xT_ready, g + 1)
            if exists(g - 1, NM):
                vec.wait_ge(up_made, N * g)
            nc.vector.tensor_copy(xT_hi[:], xT[:]).then_inc(xT_hi_ready, 1)
            vec.wait_ge(xT_hi_ready, g + 1)
            nc.vector.tensor_tensor(xT_lo[:], xT[:], xT_hi[:].bitcast(F32), ALU.subtract).then_inc(split_ready, 1)

        def gate_steps(g, part):
            done = (0, STEPS_A, STEPS_A + STEPS_B)[part]

            def step(instruction):
                nonlocal done
                done += 1
                instruction.then_inc(gate_step, 1)
                vec.wait_ge(gate_step, STEPS * g + done)

            def spread(rows):
                return rows[:].unsqueeze(2).broadcast_to([P, TT, n_exp])

            lg = small["logits"][:]
            if part == 0:
                vec.wait_ge(logits_made, g + 1)
                src = p_turn[:, 0:TT * n_exp].rearrange("p (t e) -> p t e", t=TT)
                if router_b is not None:
                    step(nc.vector.tensor_tensor(lg, src, router_b[:].unsqueeze(1).broadcast_to([P, TT, n_exp]), ALU.add))
                else:
                    step(nc.vector.tensor_copy(lg, src))
                step(nc.vector.tensor_reduce(per_row["negmax"][:], lg, AX.X, ALU.max, negate=True))
                step(nc.vector.tensor_tensor(small["shifted"][:], lg, spread(per_row["negmax"]), ALU.add))
            if part == 1:
                of_j = lg.unsqueeze(2).broadcast_to([P, TT, n_exp, n_exp])
                of_i = lg.unsqueeze(3).broadcast_to([P, TT, n_exp, n_exp])
                step(nc.vector.tensor_tensor(above[:], of_j, of_i, ALU.is_gt))
                step(nc.vector.tensor_tensor(equal[:], of_j, of_i, ALU.is_equal))
                step(nc.vector.tensor_tensor(equal[:], equal[:],
                                             earlier[:].unsqueeze(1).broadcast_to([P, TT, n_exp, n_exp]), ALU.mult))
                step(nc.vector.tensor_tensor(above[:], above[:], equal[:], ALU.add))
                step(nc.vector.tensor_reduce(small["rank"][:], above[:], AX.X, ALU.add))
            if part == 2:
                vec.wait_ge(exps_ready, g + 1)
                step(nc.vector.tensor_reduce(per_row["sums"][:], small["exps"][:], AX.X, ALU.add))
                step(nc.vector.reciprocal(per_row["rsums"][:], per_row["sums"][:]))
                step(nc.vector.tensor_tensor(small["soft"][:], small["exps"][:], spread(per_row["rsums"]), ALU.mult))
                step(nc.vector.scalar_tensor_tensor(small["mask"][:], small["rank"][:], 1.5, small["soft"][:],
                                                    ALU.is_lt, ALU.mult))
                step(nc.vector.tensor_reduce(per_row["chosen"][:], small["mask"][:], AX.X, ALU.add))
                step(nc.vector.tensor_scalar(per_row["chosen"][:], per_row["chosen"][:], sum_eps, None, ALU.add))
                step(nc.vector.reciprocal(per_row["rchosen"][:], per_row["chosen"][:]))
                if exists(g - 1, NM):
                    vec.wait_ge(weights_turned, g)
                step(nc.vector.scalar_tensor_tensor(small["weights"][:], small["mask"][:], gates[:, gate_col:gate_col + 1],
                                                    spread(per_row["rchosen"]), ALU.mult, ALU.mult))

        def steps(g):
            for n in range(N):
                if exists(g, NM):
                    k = N * g + n
                    if n == 0:
                        split_rows(g)
                    if gated:
                        vec.wait_ge(silu_ready, k + 1)
                        if exists(g - 1, NM) or n >= 4:
                            vec.wait_ge(lo_ready, k - 3)
                        nc.vector.tensor_tensor(hidden[n % 4][:], silu[n % 2][:], p_hidden[2 + n % 2][:],
                                                ALU.mult).then_inc(hidden_ready, 1)
                gl, nl = chunk_before(g, n, 1)
                if exists(gl, NM):
                    if on_pool(nl):
                        vec.wait_ge(hi_ready, POOL_CHUNKS * gl + nl // SHARE + 1)
                    else:
                        vec.wait_ge(hidden_ready, N * gl + nl + 1)
                        if exists(gl - 1, NM) or nl >= 4:
                            vec.wait_ge(down_made, N * gl + nl - 3)
                        nc.vector.tensor_copy(hidden_hi[nl % 4][:], hidden[nl % 4][:]).then_inc(own_hi_ready, 1)
                        vec.wait_ge(own_hi_ready, (N - POOL_CHUNKS) * gl + nl // SHARE + 1)
                    nc.vector.tensor_tensor(hidden_lo[nl % 4][:], hidden[nl % 4][:], hidden_hi[nl % 4][:].bitcast(F32),
                                            ALU.subtract).then_inc(lo_ready, 1)
                gd, nd = chunk_before(g, n, LAG + 1)
                ed, cd = divmod(nd, n_chunks)
                if exists(gd, NM) and cd == n_chunks - 1:
                    vec.wait_ge(down_made, N * gd + nd + 1)
                    vec.wait_ge(gate_rows_ready, n_exp * gd + ed + 1)
                    if ed == 0:
                        to = acc
                        if exists(gd - 1, NM):
                            vec.wait_ge(acc_turned, gd)
                    else:
                        to = terms[ed % 2]
                        if ed >= 3:
                            vec.wait_ge(added, (n_exp - 1) * gd + ed - 2)
                        elif exists(gd - 1, NM):
                            vec.wait_ge(added, (n_exp - 1) * gd)
                    bias = down_b[:, ed:ed + 1] if down_b is not None else 0.0
                    nc.vector.scalar_tensor_tensor(to[:], p_out[ed % 2][:], bias, gate_rows[ed % 2][:],
                                                   ALU.add, ALU.mult).then_inc(term_ready, 1)
                if n == 1 and exists(g + 1, NM):
                    if exists(g, NM):
                        vec.wait_ge(rows_turned, g + 1)
                    for t in range(TT):
                        tile = TT * (g + 1) + t
                        last = nc.vector.tensor_scalar(normed[:, t, :], x_sb[:, bass.ds(tile, 1), :],
                                                       mean[:, bass.ds(tile, 1)], rstd[:, bass.ds(tile, 1)],
                                                       ALU.subtract, ALU.mult)
                    last.then_inc(normed_ready, 1)
                if n == OUT_TURN and exists(g - 1, NM):
                    vec.wait_ge(acc_turned, g)
                    tiles = x_sb[:, bass.ds(TT * (g - 1), TT), :]
                    nc.vector.tensor_tensor(tiles, p_turn[:].rearrange("p (t d) -> p t d", t=TT), tiles,
                                            ALU.add).then_inc(stream_ready, 1)
                if n == OUT_TURN + 2 and exists(g - 1, NM) and out is None:
                    vec.wait_ge(stream_ready, g)
                    for t in range(TT):
                        tile = TT * (g - 1) + t
                        last = nc.vector.bn_stats(stats[:, bass.ds(tile, 1), :], x_sb[:, bass.ds(tile, 1), :])
                    last.then_inc(stats_written, 1)
                if n == GATE_A and exists(g + 1, NM):
                    gate_steps(g + 1, 0)
                if n == GATE_B and exists(g + 1, NM):
                    gate_steps(g + 1, 1)
                if n == GATE_C and exists(g + 1, NM):
                    gate_steps(g + 1, 2)
                if n == N - 1 and exists(g + 1, NM):
                    vec.wait_ge(weights_turned, g + 2)
                    if exists(g, NM):
                        vec.wait_ge(gate_spread, n_exp * (g + 1))
                    nc.vector.tensor_copy(gatesT[0:n_exp, :], p_turn[0:n_exp, :]).then_inc(gatesT_hi_ready, 1)
                    vec.wait_ge(gatesT_hi_ready, g + 2)
                    nc.vector.tensor_tensor(gatesT[32:32 + n_exp, :], p_turn[0:n_exp, :],
                                            gatesT[0:n_exp, :].bitcast(F32), ALU.subtract).then_inc(gatesT_ready, 1)

        over_groups(vec, steps)


def experts_0(nc, stack, new_sem, gate0, gate0_b, w1_0, b1_0, w2_0, b2_0, x_sb, ident, gates, stats, mean, rstd, tmp):
    up, down, router, router_b, up_b, down_b = expert_weights_0(
        nc, stack, new_sem, gate0, gate0_b, w1_0, b1_0, w2_0, b2_0, stats, mean, rstd, tmp)
    experts(nc, stack, new_sem, "m0", up, down, router, router_b, up_b, down_b, 1e-8, 2, x_sb, ident, gates, stats, mean, rstd, None)


def experts_1(nc, stack, new_sem, gate1, w1_1, w3_1, w2_1, x_sb, ident, gates, stats, mean, rstd, tmp, out):
    up, down, router = expert_weights_1(nc, stack, new_sem, gate1, w1_1, w3_1, w2_1, ident, stats, mean, rstd, tmp)
    experts(nc, stack, new_sem, "m1", up, down, router, None, None, None, 0.0, 3, x_sb, ident, gates, stats, mean, rstd, out)


def attention_1(nc, stack, new_sem, wq1, bq1, wk1, bk1, wv1, bv1, wo1, bo1, x_sb, ctx_sb, ident, gates, stats, mean, rstd, tmp):
    GU = MT // S
    TT = MT // P
    HH = H1 // 2
    VW = 2 * 2 * DH1 + 2

    def sb(name, shape, dt=F32):
        return stack.enter_context(nc.sbuf_tensor("a1_" + name, shape, dt))

    def sem(name):
        return new_sem("a1_" + name)

    def ps(name, shape):
        return stack.enter_context(nc.psum_tensor("a1_" + name, shape, F32))

    w_query, w_key, w_value, w_out = sb("w_query", [P, P]), sb("w_key", [P, P]), sb("w_value", [P, P]), sb("w_out", [P, P])
    b_query, b_key, b_value = sb("b_query", [P, 1]), sb("b_key", [P, 1]), sb("b_value", [P, P])
    b_out, one_row = sb("b_out", [1, P]), sb("one_row", [1, P])
    fold = sb("fold", [P, S])
    head_mask = sb("head_mask", [P, HH])
    normed, ctx_rows = sb("normed", [P, TT, D]), sb("ctx_rows", [P, TT, D])
    xT, ctxT = sb("xT", [P, MT]), sb("ctxT", [P, GU, 2, S])
    queries = [sb(f"queries{j}", [P, GU, 2, S]) for j in range(2)]
    keys = [sb(f"keys{j}", [P, GU, S]) for j in range(2)]
    values = [sb(f"values{j}", [P, GU, 4, VW]) for j in range(2)]
    key_heads = [sb(f"key_heads{i}", [P, HH, S]) for i in range(2)]
    negmax = [sb(f"negmax{i}", [P, HH]) for i in range(2)]
    shifted = [sb(f"shifted{i}", [P, HH, S]) for i in range(2)]
    exps = [sb(f"exps{i}", [P, 4, P]) for i in range(4)]
    expsT = [sb(f"expsT{i}", [P, 4, P]) for i in range(2)]
    rsums = [sb(f"rsums{i}", [P, 4, 2]) for i in range(2)]
    heads = [sb(f"heads{i}", [P, P]) for i in range(2)]
    headsT = sb("headsT", [P, MT])

    p_scores = [ps(f"p_scores{i}", [P, HH, S]) for i in range(2)]
    p_expsT = [ps(f"p_expsT{i}", [P, 4, P]) for i in range(2)]
    p_heads = ps("p_heads", [P, 4, VW])
    p_headsT = ps("p_headsT", [P, MT])
    p_turn = ps("p_turn", [P, MT])
    p_values = ps("p_values", [P, 4, 4 * 4 * DH1])

    with ExitStack() as setup:
        weights_in = new_sem("a1_weights_in")
        cleared = new_sem("a1_cleared")
        step_ready = new_sem("a1_setup_step")
        factors_vector, factors_scalar = new_factors(nc, new_sem, "a1", stats, mean, rstd, tmp)
        block = setup.enter_context(nc.Block())
        loads = [(w_query, wq1), (w_key, wk1), (w_value, wv1), (w_out, wo1),
                 (b_query, bq1.rearrange("(p a) -> p a", a=1)), (b_key, bk1.rearrange("(p a) -> p a", a=1)),
                 (b_value, bv1.rearrange("(a n) -> a n", a=1).broadcast_to([P, P])), (b_out, bo1.rearrange("(a n) -> a n", a=1))]

        @block.sync
        def _(sp):
            for dst, src in loads:
                sp.dma_start(dst[:], src).then_inc(weights_in, 16)

        @block.gpsimd
        def _(pool):
            nc.gpsimd.memset(one_row[:], 1.0)
            for j in range(2):
                nc.gpsimd.memset(queries[j][:], 0.0)
                nc.gpsimd.memset(heads[j][:], 0.0)
                nc.gpsimd.memset(values[j][:], 0.0).then_inc(cleared, 1)
            pool.wait_ge(cleared, 2)
            for j in range(2):
                for jj in range(2):
                    nc.gpsimd.memset(values[j][S * jj:S * jj + S, :, :, VW - 2 + jj], 1.0)

        @block.scalar
        def _(act):
            factors_scalar(act)

        @block.vector
        def _(vec):
            factors_vector(vec)
            nc.vector.tensor_tensor(fold[:], ident[:, 0:S], ident[:, S:P], ALU.add).then_inc(step_ready, 1)
            vec.wait_ge(step_ready, 1)
            nc.vector.tensor_reduce(head_mask[:], fold[:].rearrange("p (j d) -> p j d", d=DH1), AX.X, ALU.add)
            vec.wait_ge(weights_in, 16 * len(loads))
            nc.vector.tensor_scalar(w_out[:], w_out[:], gates[:, 1:2], None, ALU.mult)
            nc.vector.tensor_scalar(b_out[:], b_out[:], gates[0:1, 1:2], None, ALU.mult)

    normed_ready, rows_turned, xT_ready = sem("normed_ready"), sem("rows_turned"), sem("xT_ready")
    ctx_turned, ctxT_ready = sem("ctx_turned"), sem("ctxT_ready")
    queries_made, queries_ready, keys_made, keys_ready = sem("queries_made"), sem("queries_ready"), sem("keys_made"), sem("keys_ready")
    values_made, values_ready = sem("values_made"), sem("values_ready")
    key_heads_ready, scores_made, max_ready = sem("key_heads_ready"), sem("scores_made"), sem("max_ready")
    shifted_ready, exps_ready, exps_turned, expsT_ready = sem("shifted_ready"), sem("exps_ready"), sem("exps_turned"), sem("expsT_ready")
    heads_made, rsums_ready, heads_ready, headsT_made = sem("heads_made"), sem("rsums_ready"), sem("heads_ready"), sem("headsT_made")
    headsT_ready, out_made, stream_ready, stats_written = sem("headsT_ready"), sem("out_made"), sem("stream_ready"), sem("stats_written")
    block = stack.enter_context(nc.Block())

    def unit_before(g, u, lag):
        return (g, u - lag) if u >= lag else (g - 1, u - lag + GU)

    def over_groups(engine, steps):
        for g in range(-2, 2):
            steps(g, g % 2)
        with engine.Fori(1, NM // 2 - 1) as it:
            for j in range(2):
                steps(2 * it + j, j)
        for g in range(NM - 2, NM + 1):
            steps(g, g % 2)

    @block.tensor
    def _(pe):
        def steps(g, j):
            nxt = exists(g + 1, NM)
            for u in range(GU):
                if exists(g, NM):
                    k = GU * g + u
                    pe.wait_ge(key_heads_ready, k + 1)
                    if u == 0:
                        pe.wait_ge(queries_ready, 2 * (g + 1))
                    if exists(g - 1, NM) or u >= 2:
                        pe.wait_ge(shifted_ready, k - 1)
                    nc.tensor.matmul(p_scores[u % 2][:], queries[j][:, u, :, :], key_heads[u % 2][:],
                                     start=True, stop=True).then_inc(scores_made, 1)
                gt, ut = unit_before(g, u, 2)
                if exists(gt, NM):
                    k = GU * gt + ut
                    pe.wait_ge(exps_ready, k + 1)
                    if exists(gt - 1, NM) or ut >= 2:
                        pe.wait_ge(expsT_ready, k - 1)
                    for i in range(4):
                        last = nc.tensor.transpose(p_expsT[ut % 2][:, i, :], exps[ut % 4][:, i, :], ident[:])
                    last.then_inc(exps_turned, 1)
                gv, uv = unit_before(g, u, 3)
                jv = j if u >= 3 else 1 - j
                if exists(gv, NM):
                    k = GU * gv + uv
                    pe.wait_ge(expsT_ready, k + 1)
                    if uv % 4 == 0:
                        pe.wait_ge(values_ready, 4 * gv + uv // 2 + 2)
                    if exists(gv - 1, NM) or uv >= 1:
                        pe.wait_ge(heads_ready, 2 * k)
                    for i in range(4):
                        last = nc.tensor.matmul(p_heads[:, i, :], expsT[uv % 2][:, i, :], values[jv][:, uv, i, :],
                                                start=True, stop=True)
                    last.then_inc(heads_made, 1)
                if u == 0 and nxt:
                    pe.wait_ge(normed_ready, g + 2)
                    if exists(g - 2, NM):
                        pe.wait_ge(stream_ready, g - 1)
                    for t in range(TT):
                        last = nc.tensor.transpose(p_turn[:, t * P:(t + 1) * P], normed[:, t, :], ident[:])
                    last.then_inc(rows_turned, 1)
                if u == 1 and nxt:
                    pe.wait_ge(xT_ready, g + 2)
                    for t in range(TT):
                        last = nc.tensor.transpose(p_turn[:, t * P:(t + 1) * P], ctx_rows[:, t, :], ident[:])
                    last.then_inc(ctx_turned, 1)
                if u == 2 and nxt:
                    pe.wait_ge(ctxT_ready, g + 2)
                    nc.tensor.matmul(p_turn[:], w_query[:], xT[:], start=True, stop=True).then_inc(queries_made, 1)
                if u == 3 and nxt:
                    pe.wait_ge(queries_ready, 2 * (g + 2))
                    nc.tensor.matmul(p_turn[:], w_key[:], ctxT[:, :, 0, :], start=True, stop=True).then_inc(keys_made, 1)
                if u in (4, 6) and nxt:
                    if u == 6 or exists(g, NM):
                        pe.wait_ge(values_ready, 4 * (g + 1) + u - 4)
                    for b in range(4):
                        last = nc.tensor.matmul(p_values[:, b, :], ctxT[:, 2 * (u - 4) + b, :, :], w_value[:],
                                                start=True, stop=True)
                    last.then_inc(values_made, 1)
                if u == 5 and exists(g - 1, NM):
                    pe.wait_ge(headsT_ready, g)
                    if nxt:
                        pe.wait_ge(keys_ready, g + 2)
                    elif exists(g - 2, NM):
                        pe.wait_ge(stream_ready, g - 1)
                    for t in range(TT):
                        o = p_turn[:, t * P:(t + 1) * P]
                        nc.tensor.matmul(o, headsT[:, t * P:(t + 1) * P], w_out[:], start=True, stop=False)
                        last = nc.tensor.matmul(o, one_row[:], b_out[:], start=False, stop=True)
                    last.then_inc(out_made, 1)
                gc, uc = unit_before(g, u, 4)
                if exists(gc, NM):
                    pe.wait_ge(heads_ready, 2 * (GU * gc + uc + 1))
                    if uc == 0 and exists(gc - 1, NM):
                        pe.wait_ge(headsT_ready, gc)
                    nc.tensor.matmul(p_headsT[:, S * uc:S * uc + S], heads[uc % 2][:], fold[:],
                                     start=True, stop=True).then_inc(headsT_made, 1)

        over_groups(pe, steps)

    @block.scalar
    def _(act):
        def steps(g, j):
            nxt = exists(g + 1, NM)
            for u in range(GU):
                if u == 4 and exists(g - 1, NM):
                    act.wait_ge(headsT_made, GU * g)
                    if exists(g - 2, NM):
                        act.wait_ge(out_made, g - 1)
                    nc.scalar.copy(headsT[:], p_headsT[:]).then_inc(headsT_ready, 1)
                if exists(g, NM):
                    k = GU * g + u
                    act.wait_ge(shifted_ready, k + 1)
                    if exists(g - 1, NM) or u >= 4:
                        act.wait_ge(exps_turned, k - 3)
                    nc.scalar.activation(exps[u % 4][:], shifted[u % 2][:], ACT.Exp).then_inc(exps_ready, 1)
                gt, ut = unit_before(g, u, 2)
                if exists(gt, NM):
                    k = GU * gt + ut
                    act.wait_ge(exps_turned, k + 1)
                    if exists(gt - 1, NM) or ut >= 2:
                        act.wait_ge(heads_made, k - 1)
                    nc.scalar.copy(expsT[ut % 2][:], p_expsT[ut % 2][:]).then_inc(expsT_ready, 1)
                if u == 0 and nxt:
                    act.wait_ge(rows_turned, g + 2)
                    if exists(g, NM):
                        act.wait_ge(queries_made, g + 1)
                    nc.scalar.copy(xT[:], p_turn[:]).then_inc(xT_ready, 1)
                if u == 1 and nxt:
                    act.wait_ge(ctx_turned, g + 2)
                    if exists(g, NM):
                        act.wait_ge(values_made, 2 * (g + 1))
                    nc.scalar.copy(ctxT[:], p_turn[:].rearrange("p (b s) -> p b s", s=S).unsqueeze(2)
                                   .broadcast_to([P, GU, 2, S])).then_inc(ctxT_ready, 1)
                if u == 2 and nxt:
                    act.wait_ge(queries_made, g + 2)
                    if exists(g - 1, NM):
                        act.wait_ge(scores_made, GU * g)
                    for half in range(2):
                        rows = slice(half * S, half * S + S)
                        nc.scalar.activation(queries[1 - j][rows, :, half, :], p_turn[rows, :], ACT.Identity,
                                             bias=b_query[rows, :]).then_inc(queries_ready, 1)
                if u == 3 and nxt:
                    act.wait_ge(keys_made, g + 2)
                    if exists(g - 1, NM):
                        act.wait_ge(key_heads_ready, GU * g)
                    nc.scalar.activation(keys[1 - j][:], p_turn[:], ACT.Identity, bias=b_key[:]).then_inc(keys_ready, 1)

        over_groups(act, steps)

    @block.gpsimd
    def _(pool):
        def steps(g, j):
            for u in range(GU):
                gk, uk = (g, u + 1) if u + 1 < GU else (g + 1, 0)
                jk = j if u + 1 < GU else 1 - j
                if exists(gk, NM):
                    k = GU * gk + uk
                    if uk == 0:
                        pool.wait_ge(keys_ready, gk + 1)
                    if exists(gk - 1, NM) or uk >= 2:
                        pool.wait_ge(scores_made, k - 1)
                    nc.gpsimd.tensor_tensor(key_heads[uk % 2][:],
                                            keys[jk][:, uk, :].unsqueeze(1).broadcast_to([P, HH, S]),
                                            head_mask[:].unsqueeze(2).broadcast_to([P, HH, S]),
                                            ALU.mult).then_inc(key_heads_ready, 1)

        over_groups(pool, steps)

    @block.vector
    def _(vec):
        def steps(g, j):
            nxt = exists(g + 1, NM)
            for u in range(GU):
                if exists(g, NM):
                    k = GU * g + u
                    vec.wait_ge(scores_made, k + 1)
                    nc.vector.tensor_reduce(negmax[u % 2][:], p_scores[u % 2][:], AX.X, ALU.max,
                                            negate=True).then_inc(max_ready, 1)
                    vec.wait_ge(max_ready, k + 1)
                    if exists(g - 1, NM) or u >= 2:
                        vec.wait_ge(exps_ready, k - 1)
                    nc.vector.tensor_tensor(shifted[u % 2][:], p_scores[u % 2][:],
                                            negmax[u % 2][:].unsqueeze(2).broadcast_to([P, HH, S]),
                                            ALU.add).then_inc(shifted_ready, 1)
                gv, uv = unit_before(g, u, 3)
                if exists(gv, NM):
                    k = GU * gv + uv
                    vec.wait_ge(heads_made, k + 1)
                    nc.vector.reciprocal(rsums[uv % 2][:], p_heads[:, :, VW - 2:VW]).then_inc(rsums_ready, 1)
                    vec.wait_ge(rsums_ready, k + 1)
                    if exists(gv - 1, NM) or uv >= 2:
                        vec.wait_ge(headsT_made, k - 1)
                    for half in range(2):
                        rows = slice(half * S, half * S + S)
                        w = 2 * DH1
                        nc.vector.tensor_tensor(
                            heads[uv % 2][rows, half * S:half * S + S].rearrange("p (i jj d) -> p i jj d", i=4, jj=2),
                            p_heads[rows, :, half * w:half * w + w].rearrange("p i (jj d) -> p i jj d", jj=2),
                            rsums[uv % 2][rows, :, :].unsqueeze(3).broadcast_to([S, 4, 2, DH1]),
                            ALU.mult).then_inc(heads_ready, 1)
                if u in (4, 6) and nxt:
                    n = 2 * (g + 1) + (u - 4) // 2
                    vec.wait_ge(values_made, n + 1)
                    if exists(g - 1, NM):
                        vec.wait_ge(heads_made, GU * g)
                    for jj in range(2):
                        rows = slice(jj * S, jj * S + S)
                        for half in range(2):
                            cut = slice(half * S, half * S + S)
                            src = p_values[rows, :, cut].rearrange("p b (i jj d) -> p b i jj d", i=4, jj=2)[:, :, :, jj, :]
                            bias = b_value[rows, cut].rearrange("p (i jj d) -> p i jj d", i=4, jj=2)[:, :, jj, :]
                            at = half * 2 * DH1 + jj * DH1
                            last = nc.vector.tensor_tensor(values[1 - j][rows, 2 * (u - 4):2 * (u - 4) + 4, :, at:at + DH1], src,
                                                           bias.unsqueeze(1).broadcast_to([S, 4, 4, DH1]), ALU.add)
                            if half:
                                last.then_inc(values_ready, 1)
                if u == 5 and exists(g - 1, NM):
                    vec.wait_ge(out_made, g)
                    tiles = x_sb[:, bass.ds(TT * (g - 1), TT), :]
                    nc.vector.tensor_tensor(tiles, p_turn[:].rearrange("p (t d) -> p t d", t=TT), tiles,
                                            ALU.add).then_inc(stream_ready, 1)
                if u == 3 and exists(g + 2, NM):
                    if exists(g + 1, NM):
                        vec.wait_ge(ctx_turned, g + 2)
                    for t in range(TT):
                        tile = TT * (g + 2) + t
                        nc.vector.tensor_scalar(normed[:, t, :], x_sb[:, bass.ds(tile, 1), :],
                                                mean[:, bass.ds(tile, 1)], rstd[:, bass.ds(tile, 1)],
                                                ALU.subtract, ALU.mult)
                    nc.vector.tensor_copy(ctx_rows[:], ctx_sb[:, bass.ds(TT * (g + 2), TT), :]).then_inc(normed_ready, 1)
                if u == 7 and exists(g - 1, NM):
                    vec.wait_ge(stream_ready, g)
                    for t in range(TT):
                        tile = TT * (g - 1) + t
                        last = nc.vector.bn_stats(stats[:, bass.ds(tile, 1), :], x_sb[:, bass.ds(tile, 1), :])
                    last.then_inc(stats_written, 1)

        over_groups(vec, steps)


_INS = ['x', 'ctx_1024', 'g_xattn', 'g_ffn', 'L0_xattn_ln1_g', 'L0_xattn_ln1_b', 'L0_xattn_ln2_g', 'L0_xattn_ln2_b',
        'L0_xattn_Wq', 'L0_xattn_Wkv', 'L0_xattn_Wo', 'L0_ffn_Wg', 'L0_ffn_bg', 'L0_ffn_W1', 'L0_ffn_b1', 'L0_ffn_W2',
        'L0_ffn_b2', 'L1_xattn_wq', 'L1_xattn_bq', 'L1_xattn_wk', 'L1_xattn_bk', 'L1_xattn_wv', 'L1_xattn_bv',
        'L1_xattn_wo', 'L1_xattn_bo', 'L1_ffn_wg', 'L1_ffn_w1', 'L1_ffn_w3', 'L1_ffn_w2']


def kernel(**inputs):
    import numpy as np
    import concourse.bacc as bacc
    from concourse.bass_utils import run_bass_kernel_spmd

    nc = bacc.Bacc("TRN2", target_bir_lowering=False, num_devices=1)
    arrays, args = {}, []
    for name in _INS:
        a = np.ascontiguousarray(inputs[name])
        arrays[f"in_{name}_dram"] = a
        args.append(nc.dram_tensor(f"in_{name}_dram", a.shape, mybir.dt.from_np(a.dtype), kind="ExternalInput").ap())
    args.append(nc.dram_tensor("out_0_dram", (B, S, D), F32, kind="ExternalOutput").ap())
    build(nc, *args)
    r = run_bass_kernel_spmd(nc, [arrays], core_ids=[0])
    return r.results[0]["out_0_dram"]
```

```python
from contextlib import ExitStack

import concourse.bass as bass
from concourse import mybir
from concourse.alu_op_type import AluOpType as ALU

F32 = mybir.dt.float32
F32R = mybir.dt.float32r
ACT = mybir.ActivationFunctionType
AX = mybir.AxisListType

P = 128
B, S, D = 128, 64, 128
TOK = B * S
NT = TOK // P
EPS = 1e-5
H0, DH0 = 16, 64
INNER = H0 * DH0
SCALE0 = 1.0 / 8.0
GB = 4
GT = GB * S
NG = B // GB
UN = 2 * GB
E0, F0 = 8, 512
H1, DH1 = 16, 8
E1, I1 = 8, 256
MT = 512
NM = TOK // MT


def exists(g, n):
    return (0 <= g < n) if isinstance(g, int) else True


ROOT_AT = 8
ROOTS_AT = (8, 12)
LN_STEPS = 9


def layer_norm_factors(nc, vec, stats, mean, rstd, tmp, step_done, sqrt_ready, steps, roots, twice):
    m_even, v_even, m_odd, v_odd = stats[:, :, 1], stats[:, :, 2], stats[:, :, 4], stats[:, :, 5]
    arg, var, root = tmp[:, 0, :], tmp[:, 1, :], tmp[:, 2, :]

    def step(instruction):
        nonlocal steps
        steps += 1
        instruction.then_inc(step_done, 1)
        vec.wait_ge(step_done, steps)

    def rsqrt(to):
        nonlocal roots
        roots += 1
        vec.wait_ge(sqrt_ready, roots)
        step(nc.vector.reciprocal(to, root))

    step(nc.vector.tensor_tensor(mean[:], m_even, m_odd, ALU.add))
    step(nc.vector.tensor_scalar(mean[:], mean[:], 0.5, None, ALU.mult))
    step(nc.vector.tensor_tensor(arg, m_even, m_odd, ALU.subtract))
    step(nc.vector.tensor_tensor(arg, arg, arg, ALU.mult))
    step(nc.vector.tensor_tensor(var, v_even, v_odd, ALU.add))
    step(nc.vector.tensor_scalar(var, var, 1.0 / P, None, ALU.mult))
    step(nc.vector.scalar_tensor_tensor(var, arg, 0.25, var, ALU.mult, ALU.add))
    step(nc.vector.tensor_scalar(arg, var, EPS, None, ALU.add))
    rsqrt(rstd[:])
    if twice:
        step(nc.vector.tensor_tensor(arg, rstd[:], rstd[:], ALU.mult))
        step(nc.vector.tensor_tensor(arg, arg, var, ALU.mult))
        step(nc.vector.tensor_scalar(arg, arg, EPS, None, ALU.add))
        rsqrt(var)
        step(nc.vector.tensor_tensor(rstd[:], rstd[:], var, ALU.mult))
    return steps


def build(nc, x, ctx_in, g_xattn, g_ffn, ln1_g, ln1_b, ln2_g, ln2_b, wq0, wkv0, wo0,
          gate0, gate0_b, w1_0, b1_0, w2_0, b2_0, wq1, bq1, wk1, bk1, wv1, bv1, wo1, bo1,
          gate1, w1_1, w3_1, w2_1, out):
    with ExitStack() as stack:
        def sem(name):
            return stack.enter_context(nc.semaphore(name))

        def sb(name, shape, dt=F32):
            return stack.enter_context(nc.sbuf_tensor(name, shape, dt))

        x_sb = sb("x_sb", [P, NT, D])
        ctx_sb = sb("ctx_sb", [P, NT, D])
        ident = sb("ident", [P, P])
        gates = sb("gates", [P, 4])
        stats = sb("stats", [P, NT, 6])
        mean = sb("mean", [P, NT])
        rstd = sb("rstd", [P, NT])
        cmean = sb("cmean", [P, NT])
        crstd = sb("crstd", [P, NT])
        tmp = sb("ln_tmp", [P, 3, NT])
        cols = sb("cols", [P, 4])

        with ExitStack() as inner:
            attention_0(nc, inner, sem, x, ctx_in, g_xattn, g_ffn, ln1_g, ln1_b, ln2_g, ln2_b, wq0, wkv0, wo0,
                        x_sb, ctx_sb, ident, gates, stats, mean, rstd, cmean, crstd, tmp, cols)
        with ExitStack() as inner:
            experts_0(nc, inner, sem, gate0, gate0_b, w1_0, b1_0, w2_0, b2_0,
                      x_sb, ident, gates, stats, mean, rstd, tmp)
        with ExitStack() as inner:
            attention_1(nc, inner, sem, wq1, bq1, wk1, bk1, wv1, bv1, wo1, bo1,
                        x_sb, ctx_sb, ident, gates, stats, mean, rstd, tmp)
        with ExitStack() as inner:
            experts_1(nc, inner, sem, gate1, w1_1, w3_1, w2_1,
                      x_sb, ident, gates, stats, mean, rstd, tmp, out)


def attention_0(nc, stack, new_sem, x, ctx_in, g_xattn, g_ffn, ln1_g, ln1_b, ln2_g, ln2_b, wq0, wkv0, wo0,
                x_sb, ctx_sb, ident, gates, stats, mean, rstd, cmean, crstd, tmp, cols):
    def sb(name, shape, dt=F32):
        return stack.enter_context(nc.sbuf_tensor(name, shape, dt))

    def sem(name):
        return new_sem("a0_" + name)

    score_hi = sb("score_hi", [P, H0, P], F32R)
    score_lo = sb("score_lo", [P, H0, P], F32R)
    value_w = sb("value_w", [P, H0, P])

    with ExitStack() as setup:
        def ssb(name, shape, dt=F32):
            return setup.enter_context(nc.sbuf_tensor(name, shape, dt))

        def ssem(name):
            return new_sem("s_" + name)

        wq_sb = ssb("wq_sb", [P, INNER])
        wkv_sb = ssb("wkv_sb", [P, 2 * INNER])
        wo_sb = ssb("wo_sb", [DH0, H0, P])
        wT = ssb("wT", [DH0, 3, 4, P])
        scaled = ssb("scaled", [P, 4, P])
        cstats = ssb("cstats", [P, NT, 6])
        g_row = ssb("g_row", [P, 4])
        pT = [setup.enter_context(nc.psum_tensor(f"s_pT{i}", [DH0, 4, P], F32)) for i in range(3)]
        pA = setup.enter_context(nc.psum_tensor("s_pA", [P, 4, P], F32))
        pB = setup.enter_context(nc.psum_tensor("s_pB", [P, 4, P], F32))
        NL = 8
        LT = NT // NL
        rows_in = [ssem(f"rows_in{i}") for i in range(NL)]
        weights_in, small_in = ssem("weights_in"), ssem("small_in")
        ident_zero, ident_ready = ssem("ident_zero"), ssem("ident_ready")
        gates_ready = ssem("gates_ready")
        stats_done, ln_step, sqrt_ready = ssem("stats_done"), ssem("ln_step"), ssem("sqrt_ready")
        wT_filled, wT_taken = ssem("wT_filled"), ssem("wT_taken")
        ab_filled, score_hi_ready, scaled_ready, ab_taken = ssem("ab_filled"), ssem("score_hi_ready"), ssem("scaled_ready"), ssem("ab_taken")
        block = setup.enter_context(nc.Block())
        xv = x.rearrange("(t two) s d -> (two s) t d", two=2)
        cv = ctx_in.rearrange("(t two) s d -> (two s) t d", two=2)

        @block.sync
        def _(sp):
            sp.dma_start(wq_sb[:], wq0).then_inc(weights_in, 16)
            sp.dma_start(wkv_sb[:], wkv0).then_inc(weights_in, 16)
            sp.dma_start(wo_sb[:], wo0.rearrange("(h e) f -> e h f", h=H0)).then_inc(weights_in, 16)
            for i in range(NL):
                sp.dma_start(x_sb[:, i * LT:(i + 1) * LT, :], xv[:, i * LT:(i + 1) * LT, :]).then_inc(rows_in[i], 16)

        @block.gpsimd
        def _(pool):
            for i, v in enumerate((ln1_g, ln1_b, ln2_g, ln2_b)):
                pool.dma_start(cols[:, i:i + 1], v.rearrange("(p a) -> p a", a=1)).then_inc(small_in, 16)
            for i, v in enumerate((g_xattn, g_ffn)):
                pool.dma_start(g_row[:, 2 * i:2 * i + 2],
                               v.rearrange("(a n) -> a n", a=1).broadcast_to([P, 2])).then_inc(small_in, 16)
            nc.gpsimd.memset(ident[:], 0.0).then_inc(ident_zero, 1)
            pool.wait_ge(ident_zero, 1)
            nc.gpsimd.affine_select(out=ident[:], in_=ident[:], compare_op=ALU.not_equal, fill=1.0, base=0,
                                    pattern=[[-1, P]], channel_multiplier=1).then_inc(ident_ready, 1)

        @block.scalar
        def _(act):
            for i in range(NL):
                act.dma_start(ctx_sb[:, i * LT:(i + 1) * LT, :], cv[:, i * LT:(i + 1) * LT, :]).then_inc(rows_in[i], 16)
            act.wait_ge(small_in, 16 * 6)
            nc.scalar.activation(gates[:], g_row[:], ACT.Tanh).then_inc(gates_ready, 1)
            for c in range(4):
                for i in range(3):
                    act.wait_ge(wT_filled, 3 * c + i + 1)
                    if c:
                        act.wait_ge(ab_filled, c)
                    nc.scalar.copy(wT[:, i, :, :], pT[i][:]).then_inc(wT_taken, 1)
                act.wait_ge(ab_filled, c + 1)
                if c == 0:
                    act.wait_ge(gates_ready, 1)
                nc.scalar.activation(value_w[:, 4 * c:4 * c + 4, :], pB[:], ACT.Copy,
                                     scale=gates[:, 0:1]).then_inc(ab_taken, 1)
            for n in (ROOT_AT, LN_STEPS + ROOTS_AT[0], LN_STEPS + ROOTS_AT[1]):
                act.wait_ge(ln_step, n)
                nc.scalar.activation(tmp[:, 2, :], tmp[:, 0, :], ACT.Sqrt).then_inc(sqrt_ready, 1)

        @block.tensor
        def _(pe):
            pe.wait_ge(ident_ready, 1)
            pe.wait_ge(weights_in, 48)
            for c in range(4):
                for i in range(3):
                    if c:
                        pe.wait_ge(wT_taken, 3 * (c - 1) + i + 1)
                    for h in range(4):
                        col = (4 * c + h) * DH0
                        src = (wq_sb, wkv_sb, wkv_sb)[i][:, (0, 0, INNER)[i] + col:(0, 0, INNER)[i] + col + DH0]
                        last = nc.tensor.transpose(pT[i][:, h, :], src, ident[:])
                    last.then_inc(wT_filled, 1)
                pe.wait_ge(wT_taken, 3 * c + 3)
                if c:
                    pe.wait_ge(ab_taken, 2 * c)
                for h in range(4):
                    nc.tensor.matmul(pA[:, h, :], wT[:, 0, h, :], wT[:, 1, h, :], start=True, stop=True)
                    last = nc.tensor.matmul(pB[:, h, :], wT[:, 2, h, :], wo_sb[:, 4 * c + h, :], start=True, stop=True)
                last.then_inc(ab_filled, 1)

        @block.vector
        def _(vec):
            for c in range(4):
                hs = slice(4 * c, 4 * c + 4)
                vec.wait_ge(ab_filled, c + 1)
                nc.vector.tensor_scalar(scaled[:], pA[:], SCALE0, None, ALU.mult).then_inc(scaled_ready, 1)
                vec.wait_ge(scaled_ready, c + 1)
                nc.vector.tensor_copy(score_hi[:, hs, :], scaled[:]).then_inc(score_hi_ready, 1)
                vec.wait_ge(score_hi_ready, c + 1)
                nc.vector.tensor_tensor(score_lo[:, hs, :], scaled[:], score_hi[:, hs, :].bitcast(F32),
                                        ALU.subtract).then_inc(ab_taken, 1)
            for i in range(NL):
                vec.wait_ge(rows_in[i], 32)
                for t in range(i * LT, (i + 1) * LT):
                    nc.vector.bn_stats(stats[:, t, :], x_sb[:, t, :])
                    last = nc.vector.bn_stats(cstats[:, t, :], ctx_sb[:, t, :])
            last.then_inc(stats_done, 1)
            vec.wait_ge(stats_done, 1)
            steps = layer_norm_factors(nc, vec, cstats, cmean, crstd, tmp, ln_step, sqrt_ready, 0, 0, False)
            layer_norm_factors(nc, vec, stats, mean, rstd, tmp, ln_step, sqrt_ready, steps, 1, True)

    normed = sb("a0_normed", [P, 4, D])
    kvT = [sb(f"a0_kvT{j}", [P, GB, 2, S]) for j in range(2)]
    latT_hi = [sb(f"a0_latT_hi{j}", [P, GB, S], F32R) for j in range(2)]
    latT_lo = [sb(f"a0_latT_lo{j}", [P, GB, S], F32R) for j in range(2)]
    kv_rows = [sb(f"a0_kv_rows{j}", [P, GB, D]) for j in range(2)]
    queries = [sb(f"a0_queries{j}", [P, H0 // 2, GB, 2, S]) for j in range(2)]
    attended = [sb(f"a0_attended{j}", [P, H0, GB, S]) for j in range(2)]
    shifted = [sb(f"a0_shifted{i}", [P, 4, P]) for i in range(2)]
    exps = [sb(f"a0_exps{i}", [P, 4, P]) for i in range(2)]
    probs = [sb(f"a0_probs{i}", [P, 4, P]) for i in range(2)]
    probsT = [sb(f"a0_probsT{i}", [P, 4 * P]) for i in range(2)]
    negmax = [sb(f"a0_negmax{i}", [P, 4]) for i in range(2)]
    sums = [sb(f"a0_sums{i}", [P, 4]) for i in range(2)]
    rsums = [sb(f"a0_rsums{i}", [P, 4]) for i in range(2)]
    projT = sb("a0_projT", [P, GT])

    def ps(name, shape):
        return stack.enter_context(nc.psum_tensor("a0_" + name, shape, F32))

    p_scores = [ps(f"p_scores{i}", [P, 4, P]) for i in range(2)]
    p_probsT = [ps(f"p_probsT{i}", [P, 4 * P]) for i in range(2)]
    p_attended = ps("p_attended", [P, UN, S])
    p_queries = ps("p_queries", [P, 2, GB, S])
    p_turn = ps("p_turn", [P, 4, P])
    p_proj = ps("p_proj", [P, GT])

    normed_ready = sem("normed_ready")
    rows_turned = sem("rows_turned")
    kvT_ready = sem("kvT_ready")
    lat_hi_ready, lat_ready = sem("lat_hi_ready"), sem("lat_ready")
    keys_turned = sem("keys_turned")
    kv_rows_ready = sem("kv_rows_ready")
    queries_made, queries_ready = sem("queries_made"), sem("queries_ready")
    scores_made = sem("scores_made")
    max_ready, shifted_ready, exps_ready = sem("max_ready"), sem("shifted_ready"), sem("exps_ready")
    sums_ready, rsums_ready, probs_ready = sem("sums_ready"), sem("rsums_ready"), sem("probs_ready")
    probs_turned, probsT_ready = sem("probs_turned"), sem("probsT_ready")
    attended_made, attended_ready = sem("attended_made"), sem("attended_ready")
    proj_made, proj_ready = sem("proj_made"), sem("proj_ready")
    proj_turned, stream_ready = sem("proj_turned"), sem("stream_ready")
    stats_written = sem("stats_written")
    block = stack.enter_context(nc.Block())


    def query_chunk_of(g, j, u):
        return (g + 1, 1 - j, u - 2) if u >= 2 else (g, j, u + 6)

    def projected_by(g, j, u):
        return (g - 1, 1 - j, u - 3) if u >= 3 else (g - 2, j, u + 5)

    def unit_before(g, u, lag):
        return (g, u - lag) if u >= lag else (g - 1, u - lag + UN)

    def over_groups(engine, steps):
        for g in range(-2, 2):
            steps(g, g % 2)
        with engine.Fori(1, NG // 2 - 1) as it:
            for j in range(2):
                steps(2 * it + j, j)
        for g in range(NG - 2, NG + 2):
            steps(g, g % 2)

    @block.tensor
    def _(pe):
        def query_chunk(g, j, c):
            pe.wait_ge(lat_ready, g + 1)
            if exists(g - 1, NG) or c:
                pe.wait_ge(queries_ready, 8 * g + c)
            for h in range(2):
                o = p_queries[:, h, :, :]
                w_hi, w_lo = score_hi[:, 2 * c + h, :], score_lo[:, 2 * c + h, :]
                nc.tensor.matmul(o, w_hi, latT_hi[j][:], start=True, stop=False)
                nc.tensor.matmul(o, w_hi, latT_lo[j][:], start=False, stop=False)
                last = nc.tensor.matmul(o, w_lo, latT_hi[j][:], start=False, stop=True)
            last.then_inc(queries_made, 1)

        def project(g, j, r):
            if r == 0:
                pe.wait_ge(attended_ready, UN * (g + 1))
                if exists(g - 1, NG):
                    pe.wait_ge(proj_ready, g)
            for h in (2 * r, 2 * r + 1):
                last = nc.tensor.matmul(p_proj[:], value_w[:, h, :], attended[j][:, h, :, :],
                                        start=h == 0, stop=h == H0 - 1)
            if r == H0 // 2 - 1:
                last.then_inc(proj_made, 1)

        def steps(g, j):
            for u in range(UN):
                if exists(g, NG):
                    half, b = divmod(u, GB)
                    if b == 0:
                        pe.wait_ge(queries_ready, 8 * g + 4 * half + 4)
                    if exists(g - 1, NG) or u >= 2:
                        pe.wait_ge(shifted_ready, UN * g + u - 1)
                    for i in range(4):
                        last = nc.tensor.matmul(p_scores[u % 2][:, i, :], queries[j][:, 4 * half + i, b, :, :],
                                                kvT[j][:, b, :, :], start=True, stop=True)
                    last.then_inc(scores_made, 1)
                gt, ut = unit_before(g, u, 2)
                if exists(gt, NG):
                    pe.wait_ge(probs_ready, UN * gt + ut + 1)
                    if exists(gt - 1, NG) or ut >= 2:
                        pe.wait_ge(probsT_ready, UN * gt + ut - 1)
                    for i in range(4):
                        last = nc.tensor.transpose(p_probsT[u % 2][:, i * P:(i + 1) * P], probs[u % 2][:, i, :], ident[:])
                    last.then_inc(probs_turned, 1)
                ga, ua = unit_before(g, u, 3)
                ja = j if u >= 3 else 1 - j
                if exists(ga, NG):
                    pe.wait_ge(probsT_ready, UN * ga + ua + 1)
                    if ua == 0:
                        pe.wait_ge(kv_rows_ready, ga + 1)
                    if exists(ga - 1, NG) or ua >= 1:
                        pe.wait_ge(attended_ready, UN * ga + ua)
                    nc.tensor.matmul(p_attended[:], kv_rows[ja][:, ua % GB, :], probsT[ua % 2][:],
                                     start=True, stop=True).then_inc(attended_made, 1)
                if u == 0 and exists(g + 1, NG):
                    pe.wait_ge(normed_ready, g + 2)
                    if exists(g - 3, NG):
                        pe.wait_ge(stream_ready, g - 2)
                    for i in range(4):
                        last = nc.tensor.transpose(p_turn[:, i, :], normed[:, i, :], ident[:])
                    last.then_inc(rows_turned, 1)
                if u == 1 and exists(g + 1, NG):
                    pe.wait_ge(kvT_ready, 2 * (g + 2))
                    for b in range(GB):
                        last = nc.tensor.transpose(p_turn[:, b, :], kvT[1 - j][:, b, :, :], ident[:])
                    last.then_inc(keys_turned, 1)
                if u == 4 and exists(g - 2, NG):
                    if exists(g + 1, NG):
                        pe.wait_ge(kv_rows_ready, g + 2)
                    elif exists(g - 3, NG):
                        pe.wait_ge(stream_ready, g - 2)
                    pe.wait_ge(proj_ready, g - 1)
                    for t in range(2):
                        last = nc.tensor.transpose(p_turn[:, t, :], projT[:, t * P:(t + 1) * P], ident[:])
                    last.then_inc(proj_turned, 1)
                gq, jq, c = query_chunk_of(g, j, u)
                if exists(gq, NG):
                    query_chunk(gq, jq, c)
                gp, jp, r = projected_by(g, j, u)
                if exists(gp, NG):
                    project(gp, jp, r)

        over_groups(pe, steps)

    @block.scalar
    def _(act):
        def take_projection(g):
            act.wait_ge(proj_made, g + 1)
            if exists(g - 1, NG):
                act.wait_ge(proj_turned, g)
            nc.scalar.copy(projT[:], p_proj[:]).then_inc(proj_ready, 1)

        def take_queries(g, j, c):
            act.wait_ge(queries_made, 8 * g + c + 1)
            if c == 0 and exists(g - 2, NG):
                act.wait_ge(scores_made, UN * (g - 1))
            nc.scalar.copy(queries[j][:, c, :, :, :].rearrange("p b h s -> p h b s"), p_queries[:]).then_inc(queries_ready, 1)

        def steps(g, j):
            for u in range(UN):
                if u == 3 and exists(g - 2, NG):
                    take_projection(g - 2)
                if exists(g, NG):
                    act.wait_ge(shifted_ready, UN * g + u + 1)
                    if exists(g - 1, NG) or u >= 2:
                        act.wait_ge(probs_ready, UN * g + u - 1)
                    nc.scalar.activation(exps[u % 2][:], shifted[u % 2][:], ACT.Exp).then_inc(exps_ready, 1)
                gt, ut = unit_before(g, u, 2)
                if exists(gt, NG):
                    act.wait_ge(probs_turned, UN * gt + ut + 1)
                    if exists(gt - 1, NG) or ut >= 2:
                        act.wait_ge(attended_made, UN * gt + ut - 1)
                    nc.scalar.copy(probsT[u % 2][:], p_probsT[u % 2][:]).then_inc(probsT_ready, 1)
                ga, ua = unit_before(g, u, 3)
                ja = j if u >= 3 else 1 - j
                if exists(ga, NG):
                    act.wait_ge(attended_made, UN * ga + ua + 1)
                    if ua == 0 and exists(ga - 2, NG):
                        act.wait_ge(proj_made, ga - 1)
                    half, b = divmod(ua, GB)
                    nc.scalar.copy(attended[ja][:, UN * half:UN * half + UN, b, :],
                                   p_attended[:]).then_inc(attended_ready, 1)
                if u == 0 and exists(g + 1, NG):
                    act.wait_ge(rows_turned, g + 2)
                    if exists(g - 1, NG):
                        act.wait_ge(scores_made, UN * g)
                    for kind in range(2):
                        src = p_turn[:, 2 * kind:2 * kind + 2, :].rearrange("p t (two s) -> p (t two) s", two=2)
                        nc.scalar.activation(kvT[1 - j][:, :, kind, :], src, ACT.Identity,
                                             scale=cols[:, 2 * kind:2 * kind + 1],
                                             bias=cols[:, 2 * kind + 1:2 * kind + 2]).then_inc(kvT_ready, 1)
                gq, jq, c = query_chunk_of(g, j, u)
                if exists(gq, NG):
                    take_queries(gq, jq, c)

        over_groups(act, steps)

    @block.vector
    def _(vec):
        def steps(g, j):
            for u in range(UN):
                if u == 1 and exists(g + 1, NG):
                    vec.wait_ge(kvT_ready, 2 * (g + 2))
                    if exists(g - 1, NG):
                        vec.wait_ge(queries_made, 8 * g)
                    nc.vector.tensor_copy(latT_hi[1 - j][:], kvT[1 - j][:, :, 1, :]).then_inc(lat_hi_ready, 1)
                    vec.wait_ge(lat_hi_ready, g + 2)
                    nc.vector.tensor_tensor(latT_lo[1 - j][:], kvT[1 - j][:, :, 1, :], latT_hi[1 - j][:].bitcast(F32),
                                            ALU.subtract).then_inc(lat_ready, 1)
                if exists(g, NG):
                    k = UN * g + u
                    vec.wait_ge(scores_made, k + 1)
                    if exists(g - 1, NG) or u >= 2:
                        vec.wait_ge(shifted_ready, k - 1)
                    nc.vector.tensor_reduce(negmax[u % 2][:], p_scores[u % 2][:], AX.X, ALU.max,
                                            negate=True).then_inc(max_ready, 1)
                    vec.wait_ge(max_ready, k + 1)
                    if exists(g - 1, NG) or u >= 2:
                        vec.wait_ge(exps_ready, k - 1)
                    nc.vector.tensor_tensor(shifted[u % 2][:], p_scores[u % 2][:],
                                            negmax[u % 2][:].unsqueeze(2).broadcast_to([P, 4, P]),
                                            ALU.add).then_inc(shifted_ready, 1)
                gs, us = unit_before(g, u, 1)
                if exists(gs, NG):
                    k = UN * gs + us
                    vec.wait_ge(exps_ready, k + 1)
                    if exists(gs - 1, NG) or us >= 2:
                        vec.wait_ge(probs_ready, k - 1)
                    nc.vector.tensor_reduce(sums[us % 2][:], exps[us % 2][:], AX.X, ALU.add).then_inc(sums_ready, 1)
                    vec.wait_ge(sums_ready, k + 1)
                    nc.vector.reciprocal(rsums[us % 2][:], sums[us % 2][:]).then_inc(rsums_ready, 1)
                if u == 1 and exists(g + 1, NG):
                    vec.wait_ge(keys_turned, g + 2)
                    if exists(g - 1, NG):
                        vec.wait_ge(attended_made, UN * g)
                    nc.vector.tensor_copy(kv_rows[1 - j][:], p_turn[:]).then_inc(kv_rows_ready, 1)
                if u == 5 and exists(g - 2, NG):
                    vec.wait_ge(proj_turned, g - 1)
                    tiles = x_sb[:, bass.ds(2 * (g - 2), 2), :]
                    nc.vector.tensor_tensor(tiles, p_turn[:, 0:2, :], tiles, ALU.add).then_inc(stream_ready, 1)
                if u == 4 and exists(g + 2, NG):
                    if exists(g + 1, NG):
                        vec.wait_ge(rows_turned, g + 2)
                    for kind, (rows, m, r) in enumerate(((ctx_sb, cmean, crstd), (x_sb, mean, rstd))):
                        for t in range(2):
                            tile = 2 * (g + 2) + t
                            last = nc.vector.tensor_scalar(normed[:, 2 * kind + t, :], rows[:, bass.ds(tile, 1), :],
                                                           m[:, bass.ds(tile, 1)], r[:, bass.ds(tile, 1)],
                                                           ALU.subtract, ALU.mult)
                    last.then_inc(normed_ready, 1)
                if u == 6 and exists(g - 2, NG):
                    vec.wait_ge(stream_ready, g - 1)
                    for t in range(2):
                        tile = 2 * (g - 2) + t
                        last = nc.vector.bn_stats(stats[:, bass.ds(tile, 1), :], x_sb[:, bass.ds(tile, 1), :])
                    last.then_inc(stats_written, 1)

        over_groups(vec, steps)
        vec.wait_ge(stats_written, NG)

    @block.gpsimd
    def _(pool):
        def steps(g, j):
            for u in range(UN):
                gs, us = unit_before(g, u, 1)
                if exists(gs, NG):
                    k = UN * gs + us
                    pool.wait_ge(rsums_ready, k + 1)
                    if exists(gs - 1, NG) or us >= 2:
                        pool.wait_ge(probs_turned, k - 1)
                    nc.gpsimd.tensor_tensor(probs[us % 2][:], exps[us % 2][:],
                                            rsums[us % 2][:].unsqueeze(2).broadcast_to([P, 4, P]),
                                            ALU.mult).then_inc(probs_ready, 1)

        over_groups(pool, steps)


def new_factors(nc, new_sem, tag, stats, mean, rstd, tmp):
    step_done = new_sem(tag + "_ln_step")
    sqrt_ready = new_sem(tag + "_sqrt_ready")

    def on_vector(vec):
        layer_norm_factors(nc, vec, stats, mean, rstd, tmp, step_done, sqrt_ready, 0, 0, False)

    def on_scalar(act):
        act.wait_ge(step_done, ROOT_AT)
        nc.scalar.activation(tmp[:, 2, :], tmp[:, 0, :], ACT.Sqrt).then_inc(sqrt_ready, 1)

    return on_vector, on_scalar


def expert_weights_0(nc, stack, new_sem, gate0, gate0_b, w1_0, b1_0, w2_0, b2_0, stats, mean, rstd, tmp):
    def sb(name, shape, dt=F32):
        return stack.enter_context(nc.sbuf_tensor("m0_" + name, shape, dt))

    n_chunks = F0 // P
    up = [(sb("up_hi", [P, E0 * n_chunks, P], F32R), sb("up_lo", [P, E0 * n_chunks, P], F32R))]
    down = (sb("down_hi", [P, E0 * n_chunks, P], F32R), sb("down_lo", [P, E0 * n_chunks, P], F32R))
    router, router_b = sb("router", [P, E0]), sb("router_b", [P, E0])
    up_b, down_b = sb("up_b", [P, E0, n_chunks]), sb("down_b", [P, E0])
    with ExitStack() as setup:
        raw = [setup.enter_context(nc.sbuf_tensor(f"m0_raw{i}", [P, E0 * n_chunks, P], F32)) for i in range(2)]
        weights_in = [new_sem(f"m0_in{i}") for i in range(4)]
        small_in = new_sem("m0_small_in")
        hi_ready = new_sem("m0_weights_hi")
        factors_vector, factors_scalar = new_factors(nc, new_sem, "m0", stats, mean, rstd, tmp)
        block = setup.enter_context(nc.Block())
        half = E0 // 2
        views = [(raw[0], w1_0.rearrange("e d (c m) -> d e c m", m=P)), (raw[1], w2_0.rearrange("e (c p) f -> p e c f", p=P))]
        parts = [(i, s) for s in range(2) for i in range(2)]

        @block.sync
        def _(sp):
            for n, (i, s) in enumerate(parts):
                dst = views[i][0][:].rearrange("p (e c) m -> p e c m", e=E0)
                for e in range(s * half, (s + 1) * half):
                    sp.dma_start(dst[:, e, :, :], views[i][1][:, e, :, :]).then_inc(weights_in[n], 16)

        @block.gpsimd
        def _(pool):
            pool.dma_start(router[:], gate0).then_inc(small_in, 16)
            pool.dma_start(router_b[:], gate0_b.rearrange("(a n) -> a n", a=1).broadcast_to([P, E0])).then_inc(small_in, 16)
            for e in range(E0):
                pool.dma_start(up_b[:, e, :], b1_0[e, :].rearrange("(c p) -> p c", p=P),
                               allow_slow_non_contiguous=True).then_inc(small_in, 16)
            pool.dma_start(down_b[:], b2_0.rearrange("e f -> f e"), allow_slow_non_contiguous=True).then_inc(small_in, 16)
            pool.wait_ge(small_in, 16 * (E0 + 3))

        @block.scalar
        def _(act):
            factors_scalar(act)
            for n, (i, s) in enumerate(parts):
                rows = slice(s * half * n_chunks, (s + 1) * half * n_chunks)
                act.wait_ge(weights_in[n], 16 * half)
                nc.scalar.copy((up[0], down)[i][0][:, rows, :], raw[i][:, rows, :]).then_inc(hi_ready, 1)

        @block.vector
        def _(vec):
            factors_vector(vec)
            for n, (i, s) in enumerate(parts):
                rows = slice(s * half * n_chunks, (s + 1) * half * n_chunks)
                hi, lo = (up[0], down)[i]
                vec.wait_ge(hi_ready, n + 1)
                nc.vector.tensor_tensor(lo[:, rows, :], raw[i][:, rows, :], hi[:, rows, :].bitcast(F32), ALU.subtract)

    return up, down, router, router_b, up_b, down_b


def expert_weights_1(nc, stack, new_sem, gate1, w1_1, w3_1, w2_1, ident, stats, mean, rstd, tmp):
    def sb(name, shape, dt=F32):
        return stack.enter_context(nc.sbuf_tensor("m1_" + name, shape, dt))

    n_chunks = I1 // P
    up = [(sb(f"up_hi{i}", [P, E1 * n_chunks, P], F32R), sb(f"up_lo{i}", [P, E1 * n_chunks, P], F32R)) for i in range(2)]
    down = (sb("down_hi", [P, E1 * n_chunks, P], F32R), sb("down_lo", [P, E1 * n_chunks, P], F32R))
    router = sb("router", [P, E1])
    with ExitStack() as setup:
        raw = [setup.enter_context(nc.sbuf_tensor(f"m1_raw{i}", [P, E1 * n_chunks, P], F32)) for i in range(3)]
        raw_router = setup.enter_context(nc.sbuf_tensor("m1_raw_router", [E1, P], F32))
        banks = [setup.enter_context(nc.psum_tensor(f"m1_bank{i}", [P, 4, P], F32)) for i in range(4)]
        weights_in = [new_sem(f"m1_in{i}") for i in range(4)]
        turned = new_sem("m1_turned")
        hi_ready = new_sem("m1_weights_hi")
        lo_ready = new_sem("m1_weights_lo")
        router_turned = new_sem("m1_router_turned")
        factors_vector, factors_scalar = new_factors(nc, new_sem, "m1", stats, mean, rstd, tmp)
        block = setup.enter_context(nc.Block())
        quads = E1 * n_chunks // 4
        hi_lo = [up[0], up[1], down]

        @block.sync
        def _(sp):
            sp.dma_start(raw_router[:], gate1).then_inc(weights_in[3], 16)
            for i, w in enumerate((w1_1, w3_1)):
                sp.dma_start(raw[i][:].rearrange("p (e c) h -> p e c h", e=E1),
                             w.rearrange("e (c p) h -> p e c h", p=P)).then_inc(weights_in[i], 16)
            sp.dma_start(raw[2][:].rearrange("p (e c) i -> p e (c i)", e=E1),
                         w2_1.rearrange("e h i -> h e i")).then_inc(weights_in[2], 16)

        @block.tensor
        def _(pe):
            for i in range(3):
                pe.wait_ge(weights_in[i], 16)
                for q in range(quads):
                    n = quads * i + q
                    if n >= 4:
                        pe.wait_ge(lo_ready, n - 3)
                    for b in range(4):
                        last = nc.tensor.transpose(banks[n % 4][:, b, :], raw[i][:, 4 * q + b, :], ident[:])
                    last.then_inc(turned, 1)
            pe.wait_ge(weights_in[3], 16)
            pe.wait_ge(lo_ready, 3 * quads - 3)
            nc.tensor.transpose(banks[0][:, 0, 0:E1], raw_router[:], ident[0:E1, 0:E1]).then_inc(router_turned, 1)

        @block.scalar
        def _(act):
            factors_scalar(act)
            for n in range(3 * quads):
                i, q = divmod(n, quads)
                act.wait_ge(turned, n + 1)
                nc.scalar.copy(hi_lo[i][0][:, 4 * q:4 * q + 4, :], banks[n % 4][:]).then_inc(hi_ready, 1)

        @block.vector
        def _(vec):
            factors_vector(vec)
            for n in range(3 * quads):
                i, q = divmod(n, quads)
                hi, lo = hi_lo[i]
                vec.wait_ge(hi_ready, n + 1)
                nc.vector.tensor_tensor(lo[:, 4 * q:4 * q + 4, :], banks[n % 4][:], hi[:, 4 * q:4 * q + 4, :].bitcast(F32),
                                        ALU.subtract).then_inc(lo_ready, 1)
            vec.wait_ge(router_turned, 1)
            nc.vector.tensor_copy(router[:], banks[0][:, 0, 0:E1])

    return up, down, router


def experts(nc, stack, new_sem, tag, up, down, router, router_b, up_b, down_b, sum_eps, gate_col,
            x_sb, ident, gates, stats, mean, rstd, out):
    n_exp = 8
    n_chunks = down[0].shape[1] // n_exp
    gated = up_b is None
    N = n_exp * n_chunks
    LAG = 4 if gated else 5
    ROWS_TURN, LOGITS, SPLIT = (1, 3, 5) if gated else (2, 5, 6)
    GATE_A, GATE_B, GATE_C = (4, 6, 8) if gated else (7, 10, 13)
    GATES_TURN, OUT_TURN, NORM = (11, 13, 15) if gated else (18, 23, 28)
    TT = MT // P

    def sb(name, shape, dt=F32):
        return stack.enter_context(nc.sbuf_tensor(f"{tag}_{name}", shape, dt))

    def sem(name):
        return new_sem(f"{tag}_{name}")

    def ps(name, shape):
        return stack.enter_context(nc.psum_tensor(f"{tag}_{name}", shape, F32))

    normed = sb("normed", [P, TT, D])
    xT = sb("xT", [P, MT])
    xT_hi = [sb(f"xT_hi{j}", [P, MT], F32R) for j in range(2)]
    xT_lo = [sb(f"xT_lo{j}", [P, MT], F32R) for j in range(2)]
    silu = [sb(f"silu{i}", [P, MT]) for i in range(4)] if gated else None
    linear = [sb(f"linear{i}", [P, MT]) for i in range(4)] if gated else None
    hidden = [sb(f"hidden{i}", [P, MT]) for i in range(4)]
    RING = 8
    hidden_hi = [sb(f"hidden_hi{i}", [P, MT], F32R) for i in range(RING)]
    hidden_lo = [sb(f"hidden_lo{i}", [P, MT], F32R) for i in range(RING)]
    gate_rows = [sb(f"gate_rows{i}", [P, MT]) for i in range(2)]
    terms = [sb(f"terms{i}", [P, MT]) for i in range(2)]
    acc = [sb(f"acc{j}", [P, MT]) for j in range(2)]
    small = {name: sb(name, [P, TT, n_exp]) for name in ("logits", "shifted", "exps", "soft", "rank", "mask", "weights")}
    per_row = {name: sb(name, [P, TT]) for name in ("negmax", "sums", "rsums", "chosen", "rchosen")}
    above, equal = sb("above", [P, TT, n_exp, n_exp]), sb("equal", [P, TT, n_exp, n_exp])
    earlier = sb("earlier", [P, n_exp, n_exp])
    ones = sb("ones", [P, 1])
    picks_r = sb("picks_r", [64, n_exp, P], F32R)
    gatesT = [sb(f"gatesT{j}", [64, MT], F32R) for j in range(2)]

    p_hidden = [ps(f"p_hidden{i}", [P, MT]) for i in range(4)]
    p_out = [ps(f"p_out{i}", [P, MT]) for i in range(2)]
    p_turn = ps("p_turn", [P, MT])
    p_gate = ps("p_gate", [P, MT])

    const_step, const_ready = sem("const_step"), sem("const_ready")
    normed_ready, rows_turned, xT_ready = sem("normed_ready"), sem("rows_turned"), sem("xT_ready")
    xT_hi_ready, split_ready = sem("xT_hi_ready"), sem("split_ready")
    logits_made, gate_step, exps_ready = sem("logits_made"), sem("gate_step"), sem("exps_ready")
    weights_turned, gatesT_hi_ready, gatesT_ready = sem("weights_turned"), sem("gatesT_hi_ready"), sem("gatesT_ready")
    gate_spread, gate_rows_ready = sem("gate_spread"), sem("gate_rows_ready")
    up_made, linear_ready, hidden_ready = sem("up_made"), sem("linear_ready") if gated else None, sem("hidden_ready")
    own_hi_ready = sem("own_hi_ready") if not gated else None
    act_hi_ready = sem("act_hi_ready") if not gated else None
    hi_ready, lo_ready, down_made = sem("hi_ready"), sem("lo_ready"), sem("down_made")
    term_ready, added = sem("term_ready"), sem("added")
    acc_turned, stream_ready, stats_written = sem("acc_turned"), sem("stream_ready"), sem("stats_written")
    stored = sem("stored") if out is not None else None
    block = stack.enter_context(nc.Block())
    STEPS_A, STEPS_B, STEPS_C = 3, 5, 8
    STEPS = STEPS_A + STEPS_B + STEPS_C

    def on_pool(n):
        return gated or n % 2 == 0

    def on_scalar(n):
        return not gated and n % 4 == 1

    def chunk_before(g, n, lag):
        return (g, n - lag) if n >= lag else (g - 1, n - lag + N)

    def over_groups(engine, steps):
        for g in (-2, -1, 0, 1):
            steps(g, g % 2)
        with engine.Fori(1, NM // 2 - 1) as it:
            for j in range(2):
                steps(2 * it + j, j)
        for g in (NM - 2, NM - 1, NM):
            steps(g, g % 2)

    @block.sync
    def _(sp):
        if out is not None:
            view = out.rearrange("(t two) s d -> (two s) t d", two=2)
            with sp.Fori(0, NM) as g:
                sp.wait_ge(stream_ready, g + 1)
                sp.dma_start(view[:, bass.ds(TT * g, TT), :], x_sb[:, bass.ds(TT * g, TT), :]).then_inc(stored, 16)
            sp.wait_ge(stored, 16 * NM)

    @block.tensor
    def _(pe):
        pe.wait_ge(const_ready, 4)

        def split_product(o, w, row, hi, lo, first, last_one):
            nc.tensor.matmul(o, w[0][:, row, :], hi, start=first, stop=False)
            nc.tensor.matmul(o, w[0][:, row, :], lo, start=False, stop=False)
            return nc.tensor.matmul(o, w[1][:, row, :], hi, start=False, stop=last_one)

        def steps(g, j):
            for n in range(N):
                e, c = divmod(n, n_chunks)
                if exists(g, NM):
                    if n == 0:
                        pe.wait_ge(split_ready, g + 1)
                    if gated:
                        if exists(g - 1, NM) or n >= 2:
                            pe.wait_ge(linear_ready, N * g + n - 1)
                        split_product(p_hidden[n % 2][:], up[0], n, xT_hi[j][:], xT_lo[j][:], True, True)
                        split_product(p_hidden[2 + n % 2][:], up[1], n, xT_hi[j][:], xT_lo[j][:], True, True).then_inc(up_made, 1)
                    else:
                        if exists(g - 1, NM) or n >= 4:
                            pe.wait_ge(hidden_ready, N * g + n - 3)
                        split_product(p_hidden[n % 4][:], up[0], n, xT_hi[j][:], xT_lo[j][:], True, True).then_inc(up_made, 1)
                gd, nd = chunk_before(g, n, LAG)
                if exists(gd, NM):
                    ed, cd = divmod(nd, n_chunks)
                    if cd == 0:
                        if ed == 0:
                            pe.wait_ge(gatesT_ready, gd + 1)
                        if exists(gd - 1, NM) or ed:
                            pe.wait_ge(gate_rows_ready, n_exp * gd + ed)
                        nc.tensor.matmul(p_gate[:], picks_r[:, ed, :], gatesT[j if n >= LAG else 1 - j][:],
                                         start=True, stop=True).then_inc(gate_spread, 1)
                    pe.wait_ge(lo_ready, N * gd + nd + 1)
                    if cd == 0 and (exists(gd - 1, NM) or ed >= 2):
                        pe.wait_ge(term_ready, n_exp * gd + ed - 1)
                    split_product(p_out[ed % 2][:], down, nd, hidden_hi[nd % RING][:], hidden_lo[nd % RING][:],
                                  cd == 0, cd == n_chunks - 1).then_inc(down_made, 1)
                if n == ROWS_TURN and exists(g + 1, NM):
                    pe.wait_ge(normed_ready, g + 2)
                    if exists(g - 2, NM):
                        pe.wait_ge(stream_ready, g - 1)
                    elif exists(g, NM):
                        pe.wait_ge(gatesT_ready, g + 1)
                    for t in range(TT):
                        last = nc.tensor.transpose(p_turn[:, t * P:(t + 1) * P], normed[:, t, :], ident[:])
                    last.then_inc(rows_turned, 1)
                if n == LOGITS and exists(g + 1, NM):
                    pe.wait_ge(xT_ready, g + 2)
                    for t in range(TT):
                        last = nc.tensor.matmul(p_turn[:, t * n_exp:(t + 1) * n_exp], xT[:, t * P:(t + 1) * P], router[:],
                                                start=True, stop=True)
                    last.then_inc(logits_made, 1)
                if n == GATES_TURN and exists(g + 1, NM):
                    pe.wait_ge(gate_step, STEPS * (g + 2))
                    for t in range(TT):
                        last = nc.tensor.transpose(p_turn[0:n_exp, t * P:(t + 1) * P], small["weights"][:, t, :], ident[:])
                    last.then_inc(weights_turned, 1)
                if n == OUT_TURN and exists(g - 1, NM):
                    pe.wait_ge(added, (n_exp - 1) * g)
                    if exists(g + 1, NM):
                        pe.wait_ge(gatesT_ready, g + 2)
                    else:
                        pe.wait_ge(stream_ready, g - 1)
                    for t in range(TT):
                        last = nc.tensor.transpose(p_turn[:, t * P:(t + 1) * P], acc[1 - j][:, t * P:(t + 1) * P], ident[:])
                    last.then_inc(acc_turned, 1)

        over_groups(pe, steps)

    @block.scalar
    def _(act):
        def steps(g, j):
            for n in range(N):
                e, c = divmod(n, n_chunks)
                if exists(g, NM):
                    act.wait_ge(up_made, N * g + n + 1)
                    if gated:
                        if exists(g - 1, NM) or n >= 4:
                            act.wait_ge(hidden_ready, N * g + n - 3)
                        nc.scalar.activation(silu[n % 4][:], p_hidden[n % 2][:], ACT.Silu)
                        nc.scalar.copy(linear[n % 4][:], p_hidden[2 + n % 2][:]).then_inc(linear_ready, 1)
                    else:
                        if exists(g - 1, NM) or n >= 4:
                            act.wait_ge(lo_ready, N * g + n - 3)
                        nc.scalar.activation(hidden[n % 4][:], p_hidden[n % 4][:], ACT.Gelu_apprx_tanh,
                                             bias=up_b[:, e, c:c + 1]).then_inc(hidden_ready, 1)
                gs, ns = chunk_before(g, n, 1)
                if exists(gs, NM) and on_scalar(ns):
                    act.wait_ge(hidden_ready, N * gs + ns + 1)
                    if exists(gs - 1, NM) or ns >= RING:
                        act.wait_ge(down_made, N * gs + ns + 1 - RING)
                    nc.scalar.copy(hidden_hi[ns % RING][:], hidden[ns % 4][:]).then_inc(act_hi_ready, 1)
                gd, nd = chunk_before(g, n, LAG)
                ed, cd = divmod(nd, n_chunks)
                if exists(gd, NM) and cd == 0:
                    act.wait_ge(gate_spread, n_exp * gd + ed + 1)
                    if exists(gd - 1, NM) or ed >= 2:
                        act.wait_ge(term_ready, n_exp * gd + ed - 1)
                    nc.scalar.copy(gate_rows[ed % 2][:], p_gate[:]).then_inc(gate_rows_ready, 1)
                if n == ROWS_TURN + 1 and exists(g + 1, NM):
                    act.wait_ge(rows_turned, g + 2)
                    if exists(g, NM):
                        act.wait_ge(split_ready, g + 1)
                        act.wait_ge(logits_made, g + 1)
                    nc.scalar.copy(xT[:], p_turn[:]).then_inc(xT_ready, 1)
                if n == GATE_A + 1 and exists(g + 1, NM):
                    act.wait_ge(gate_step, STEPS * (g + 1) + STEPS_A)
                    nc.scalar.activation(small["exps"][:], small["shifted"][:], ACT.Exp).then_inc(exps_ready, 1)

        over_groups(act, steps)

    @block.gpsimd
    def _(pool):
        nc.gpsimd.memset(earlier[:], 1.0).then_inc(const_step, 1)
        nc.gpsimd.memset(picks_r[:].bitcast(F32), 0.0).then_inc(const_step, 1)
        nc.gpsimd.memset(ones[:], 1.0).then_inc(const_step, 1)
        nc.gpsimd.memset(gatesT[0][:].bitcast(F32), 0.0).then_inc(const_ready, 1)
        nc.gpsimd.memset(gatesT[1][:].bitcast(F32), 0.0).then_inc(const_ready, 1)
        pool.wait_ge(const_step, 3)
        nc.gpsimd.affine_select(out=earlier[:], in_=earlier[:], compare_op=ALU.is_gt, fill=0.0, base=0,
                                pattern=[[1, n_exp], [-1, n_exp]], channel_multiplier=0).then_inc(const_ready, 1)
        nc.gpsimd.affine_select(out=picks_r[:], in_=picks_r[:].bitcast(F32), compare_op=ALU.not_equal, fill=1.0, base=0,
                                pattern=[[-1, n_exp], [0, P]], channel_multiplier=1).then_inc(const_step, 1)
        pool.wait_ge(const_step, 4)
        nc.gpsimd.affine_select(out=picks_r[:], in_=picks_r[:].bitcast(F32), compare_op=ALU.not_equal, fill=1.0, base=-32,
                                pattern=[[-1, n_exp], [0, P]], channel_multiplier=1).then_inc(const_ready, 1)

        def steps(g, j):
            for n in range(N):
                if exists(g, NM) and on_pool(n):
                    k = N * g + n
                    pool.wait_ge(hidden_ready, k + 1)
                    if exists(g - 1, NM) or n >= RING:
                        pool.wait_ge(down_made, k + 1 - RING)
                    nc.gpsimd.tensor_tensor(hidden_hi[n % RING][:], hidden[n % 4][:], ones[:].broadcast_to([P, MT]),
                                            ALU.mult).then_inc(hi_ready, 1)
                gd, nd = chunk_before(g, n, LAG + 1)
                jd = j if n > LAG else 1 - j
                ed, cd = divmod(nd, n_chunks)
                if exists(gd, NM) and cd == n_chunks - 1 and ed:
                    pool.wait_ge(term_ready, n_exp * gd + ed + 1)
                    if ed > 1:
                        pool.wait_ge(added, (n_exp - 1) * gd + ed - 1)
                    nc.gpsimd.tensor_tensor(acc[jd][:], acc[jd][:], terms[ed % 2][:], ALU.add).then_inc(added, 1)

        over_groups(pool, steps)

    @block.vector
    def _(vec):
        vec.wait_ge(const_ready, 4)

        def split_rows(g, j):
            vec.wait_ge(xT_ready, g + 1)
            if exists(g - 2, NM):
                vec.wait_ge(up_made, N * (g - 1))
            nc.vector.tensor_copy(xT_hi[j][:], xT[:]).then_inc(xT_hi_ready, 1)
            vec.wait_ge(xT_hi_ready, g + 1)
            nc.vector.tensor_tensor(xT_lo[j][:], xT[:], xT_hi[j][:].bitcast(F32), ALU.subtract).then_inc(split_ready, 1)

        def gate_steps(g, part):
            done = (0, STEPS_A, STEPS_A + STEPS_B)[part]

            def step(instruction):
                nonlocal done
                done += 1
                instruction.then_inc(gate_step, 1)
                vec.wait_ge(gate_step, STEPS * g + done)

            def spread(rows):
                return rows[:].unsqueeze(2).broadcast_to([P, TT, n_exp])

            lg = small["logits"][:]
            if part == 0:
                vec.wait_ge(logits_made, g + 1)
                src = p_turn[:, 0:TT * n_exp].rearrange("p (t e) -> p t e", t=TT)
                if router_b is not None:
                    step(nc.vector.tensor_tensor(lg, src, router_b[:].unsqueeze(1).broadcast_to([P, TT, n_exp]), ALU.add))
                else:
                    step(nc.vector.tensor_copy(lg, src))
                step(nc.vector.tensor_reduce(per_row["negmax"][:], lg, AX.X, ALU.max, negate=True))
                step(nc.vector.tensor_tensor(small["shifted"][:], lg, spread(per_row["negmax"]), ALU.add))
            if part == 1:
                of_j = lg.unsqueeze(2).broadcast_to([P, TT, n_exp, n_exp])
                of_i = lg.unsqueeze(3).broadcast_to([P, TT, n_exp, n_exp])
                step(nc.vector.tensor_tensor(above[:], of_j, of_i, ALU.is_gt))
                step(nc.vector.tensor_tensor(equal[:], of_j, of_i, ALU.is_equal))
                step(nc.vector.tensor_tensor(equal[:], equal[:],
                                             earlier[:].unsqueeze(1).broadcast_to([P, TT, n_exp, n_exp]), ALU.mult))
                step(nc.vector.tensor_tensor(above[:], above[:], equal[:], ALU.add))
                step(nc.vector.tensor_reduce(small["rank"][:], above[:], AX.X, ALU.add))
            if part == 2:
                vec.wait_ge(exps_ready, g + 1)
                step(nc.vector.tensor_reduce(per_row["sums"][:], small["exps"][:], AX.X, ALU.add))
                step(nc.vector.reciprocal(per_row["rsums"][:], per_row["sums"][:]))
                step(nc.vector.tensor_tensor(small["soft"][:], small["exps"][:], spread(per_row["rsums"]), ALU.mult))
                step(nc.vector.scalar_tensor_tensor(small["mask"][:], small["rank"][:], 1.5, small["soft"][:],
                                                    ALU.is_lt, ALU.mult))
                step(nc.vector.tensor_reduce(per_row["chosen"][:], small["mask"][:], AX.X, ALU.add))
                step(nc.vector.tensor_scalar(per_row["chosen"][:], per_row["chosen"][:], sum_eps, None, ALU.add))
                step(nc.vector.reciprocal(per_row["rchosen"][:], per_row["chosen"][:]))
                if exists(g - 1, NM):
                    vec.wait_ge(weights_turned, g)
                step(nc.vector.scalar_tensor_tensor(small["weights"][:], small["mask"][:], gates[:, gate_col:gate_col + 1],
                                                    spread(per_row["rchosen"]), ALU.mult, ALU.mult))

        def steps(g, j):
            for n in range(N):
                gh, nh = chunk_before(g, n, 1)
                if gated and exists(gh, NM):
                    k = N * gh + nh
                    vec.wait_ge(linear_ready, k + 1)
                    if exists(gh - 1, NM) or nh >= 4:
                        vec.wait_ge(lo_ready, k - 3)
                    nc.vector.tensor_tensor(hidden[nh % 4][:], silu[nh % 4][:], linear[nh % 4][:],
                                            ALU.mult).then_inc(hidden_ready, 1)
                gl, nl = chunk_before(g, n, 2)
                if exists(gl, NM):
                    if gated:
                        vec.wait_ge(hi_ready, N * gl + nl + 1)
                    elif on_pool(nl):
                        vec.wait_ge(hi_ready, N // 2 * gl + nl // 2 + 1)
                    elif on_scalar(nl):
                        vec.wait_ge(act_hi_ready, N // 4 * gl + nl // 4 + 1)
                    else:
                        vec.wait_ge(hidden_ready, N * gl + nl + 1)
                        if exists(gl - 1, NM) or nl >= RING:
                            vec.wait_ge(down_made, N * gl + nl + 1 - RING)
                        nc.vector.tensor_copy(hidden_hi[nl % RING][:], hidden[nl % 4][:]).then_inc(own_hi_ready, 1)
                        vec.wait_ge(own_hi_ready, N // 4 * gl + nl // 4 + 1)
                    nc.vector.tensor_tensor(hidden_lo[nl % RING][:], hidden[nl % 4][:], hidden_hi[nl % RING][:].bitcast(F32),
                                            ALU.subtract).then_inc(lo_ready, 1)
                gd, nd = chunk_before(g, n, LAG + 1)
                jd = j if n > LAG else 1 - j
                ed, cd = divmod(nd, n_chunks)
                if exists(gd, NM) and cd == n_chunks - 1:
                    vec.wait_ge(down_made, N * gd + nd + 1)
                    vec.wait_ge(gate_rows_ready, n_exp * gd + ed + 1)
                    if ed == 0:
                        to = acc[jd]
                        if exists(gd - 2, NM):
                            vec.wait_ge(acc_turned, gd - 1)
                    else:
                        to = terms[ed % 2]
                        if ed >= 3:
                            vec.wait_ge(added, (n_exp - 1) * gd + ed - 2)
                        elif exists(gd - 1, NM):
                            vec.wait_ge(added, (n_exp - 1) * gd)
                    bias = down_b[:, ed:ed + 1] if down_b is not None else 0.0
                    nc.vector.scalar_tensor_tensor(to[:], p_out[ed % 2][:], bias, gate_rows[ed % 2][:],
                                                   ALU.add, ALU.mult).then_inc(term_ready, 1)
                if n == NORM and exists(g + 2, NM):
                    if exists(g + 1, NM):
                        vec.wait_ge(rows_turned, g + 2)
                    for t in range(TT):
                        tile = TT * (g + 2) + t
                        last = nc.vector.tensor_scalar(normed[:, t, :], x_sb[:, bass.ds(tile, 1), :],
                                                       mean[:, bass.ds(tile, 1)], rstd[:, bass.ds(tile, 1)],
                                                       ALU.subtract, ALU.mult)
                    last.then_inc(normed_ready, 1)
                if n == OUT_TURN + 1 and exists(g - 1, NM):
                    vec.wait_ge(acc_turned, g)
                    tiles = x_sb[:, bass.ds(TT * (g - 1), TT), :]
                    nc.vector.tensor_tensor(tiles, p_turn[:].rearrange("p (t d) -> p t d", t=TT), tiles,
                                            ALU.add).then_inc(stream_ready, 1)
                if n == OUT_TURN + 3 and exists(g - 1, NM) and out is None:
                    vec.wait_ge(stream_ready, g)
                    for t in range(TT):
                        tile = TT * (g - 1) + t
                        last = nc.vector.bn_stats(stats[:, bass.ds(tile, 1), :], x_sb[:, bass.ds(tile, 1), :])
                    last.then_inc(stats_written, 1)
                if n == SPLIT and exists(g + 1, NM):
                    split_rows(g + 1, 1 - j)
                if n == GATE_A and exists(g + 1, NM):
                    gate_steps(g + 1, 0)
                if n == GATE_B and exists(g + 1, NM):
                    gate_steps(g + 1, 1)
                if n == GATE_C and exists(g + 1, NM):
                    gate_steps(g + 1, 2)
                if n == GATES_TURN + 1 and exists(g + 1, NM):
                    vec.wait_ge(weights_turned, g + 2)
                    if exists(g - 1, NM):
                        vec.wait_ge(gate_spread, n_exp * g)
                    nc.vector.tensor_copy(gatesT[1 - j][0:n_exp, :], p_turn[0:n_exp, :]).then_inc(gatesT_hi_ready, 1)
                    vec.wait_ge(gatesT_hi_ready, g + 2)
                    nc.vector.tensor_tensor(gatesT[1 - j][32:32 + n_exp, :], p_turn[0:n_exp, :],
                                            gatesT[1 - j][0:n_exp, :].bitcast(F32), ALU.subtract).then_inc(gatesT_ready, 1)

        over_groups(vec, steps)


def experts_0(nc, stack, new_sem, gate0, gate0_b, w1_0, b1_0, w2_0, b2_0, x_sb, ident, gates, stats, mean, rstd, tmp):
    up, down, router, router_b, up_b, down_b = expert_weights_0(
        nc, stack, new_sem, gate0, gate0_b, w1_0, b1_0, w2_0, b2_0, stats, mean, rstd, tmp)
    experts(nc, stack, new_sem, "m0", up, down, router, router_b, up_b, down_b, 1e-8, 2, x_sb, ident, gates, stats, mean, rstd, None)


def experts_1(nc, stack, new_sem, gate1, w1_1, w3_1, w2_1, x_sb, ident, gates, stats, mean, rstd, tmp, out):
    up, down, router = expert_weights_1(nc, stack, new_sem, gate1, w1_1, w3_1, w2_1, ident, stats, mean, rstd, tmp)
    experts(nc, stack, new_sem, "m1", up, down, router, None, None, None, 0.0, 3, x_sb, ident, gates, stats, mean, rstd, out)


def attention_1(nc, stack, new_sem, wq1, bq1, wk1, bk1, wv1, bv1, wo1, bo1, x_sb, ctx_sb, ident, gates, stats, mean, rstd, tmp):
    GU = MT // S
    TT = MT // P
    HH = H1 // 2
    VW = 2 * 2 * DH1 + 2

    def sb(name, shape, dt=F32):
        return stack.enter_context(nc.sbuf_tensor("a1_" + name, shape, dt))

    def sem(name):
        return new_sem("a1_" + name)

    def ps(name, shape):
        return stack.enter_context(nc.psum_tensor("a1_" + name, shape, F32))

    w_query, w_key, w_value, w_out = sb("w_query", [P, P]), sb("w_key", [P, P]), sb("w_value", [P, P]), sb("w_out", [P, P])
    b_query, b_key, b_value = sb("b_query", [P, 1]), sb("b_key", [P, 1]), sb("b_value", [P, P])
    b_out, one_row = sb("b_out", [1, P]), sb("one_row", [1, P])
    fold = sb("fold", [P, S])
    head_mask = sb("head_mask", [P, HH])
    normed, ctx_rows = sb("normed", [P, TT, D]), sb("ctx_rows", [P, TT, D])
    xT, ctxT = sb("xT", [P, MT]), sb("ctxT", [P, GU, 2, S])
    queries = [sb(f"queries{j}", [P, GU, 2, S]) for j in range(2)]
    keys = [sb(f"keys{j}", [P, GU, S]) for j in range(2)]
    values = [sb(f"values{j}", [P, GU, 4, VW]) for j in range(2)]
    key_heads = [sb(f"key_heads{i}", [P, HH, S]) for i in range(2)]
    negmax = [sb(f"negmax{i}", [P, HH]) for i in range(2)]
    shifted = [sb(f"shifted{i}", [P, HH, S]) for i in range(2)]
    exps = [sb(f"exps{i}", [P, 4, P]) for i in range(4)]
    expsT = [sb(f"expsT{i}", [P, 4, P]) for i in range(2)]
    rsums = [sb(f"rsums{i}", [P, 4, 2]) for i in range(2)]
    heads = [sb(f"heads{i}", [P, P]) for i in range(2)]
    headsT = sb("headsT", [P, MT])

    p_scores = [ps(f"p_scores{i}", [P, HH, S]) for i in range(2)]
    p_expsT = [ps(f"p_expsT{i}", [P, 4, P]) for i in range(2)]
    p_heads = ps("p_heads", [P, 4, VW])
    p_headsT = ps("p_headsT", [P, MT])
    p_turn = ps("p_turn", [P, MT])
    p_values = ps("p_values", [P, 4, 4 * 4 * DH1])

    with ExitStack() as setup:
        weights_in = new_sem("a1_weights_in")
        cleared = new_sem("a1_cleared")
        step_ready = new_sem("a1_setup_step")
        factors_vector, factors_scalar = new_factors(nc, new_sem, "a1", stats, mean, rstd, tmp)
        block = setup.enter_context(nc.Block())
        loads = [(w_query, wq1), (w_key, wk1), (w_value, wv1), (w_out, wo1),
                 (b_query, bq1.rearrange("(p a) -> p a", a=1)), (b_key, bk1.rearrange("(p a) -> p a", a=1)),
                 (b_value, bv1.rearrange("(a n) -> a n", a=1).broadcast_to([P, P])), (b_out, bo1.rearrange("(a n) -> a n", a=1))]

        @block.sync
        def _(sp):
            for dst, src in loads:
                sp.dma_start(dst[:], src).then_inc(weights_in, 16)

        @block.gpsimd
        def _(pool):
            nc.gpsimd.memset(one_row[:], 1.0)
            for j in range(2):
                nc.gpsimd.memset(queries[j][:], 0.0)
                nc.gpsimd.memset(heads[j][:], 0.0)
                nc.gpsimd.memset(values[j][:], 0.0).then_inc(cleared, 1)
            pool.wait_ge(cleared, 2)
            for j in range(2):
                for jj in range(2):
                    nc.gpsimd.memset(values[j][S * jj:S * jj + S, :, :, VW - 2 + jj], 1.0)

        @block.scalar
        def _(act):
            factors_scalar(act)

        @block.vector
        def _(vec):
            factors_vector(vec)
            nc.vector.tensor_tensor(fold[:], ident[:, 0:S], ident[:, S:P], ALU.add).then_inc(step_ready, 1)
            vec.wait_ge(step_ready, 1)
            nc.vector.tensor_reduce(head_mask[:], fold[:].rearrange("p (j d) -> p j d", d=DH1), AX.X, ALU.add)
            vec.wait_ge(weights_in, 16 * len(loads))
            nc.vector.tensor_scalar(w_out[:], w_out[:], gates[:, 1:2], None, ALU.mult)
            nc.vector.tensor_scalar(b_out[:], b_out[:], gates[0:1, 1:2], None, ALU.mult)

    normed_ready, rows_turned, xT_ready = sem("normed_ready"), sem("rows_turned"), sem("xT_ready")
    ctx_turned, ctxT_ready = sem("ctx_turned"), sem("ctxT_ready")
    queries_made, queries_ready, keys_made, keys_ready = sem("queries_made"), sem("queries_ready"), sem("keys_made"), sem("keys_ready")
    values_made, values_ready = sem("values_made"), sem("values_ready")
    key_heads_ready, scores_made, max_ready = sem("key_heads_ready"), sem("scores_made"), sem("max_ready")
    shifted_ready, exps_ready, exps_turned, expsT_ready = sem("shifted_ready"), sem("exps_ready"), sem("exps_turned"), sem("expsT_ready")
    heads_made, rsums_ready, heads_ready, headsT_made = sem("heads_made"), sem("rsums_ready"), sem("heads_ready"), sem("headsT_made")
    headsT_ready, out_made, stream_ready, stats_written = sem("headsT_ready"), sem("out_made"), sem("stream_ready"), sem("stats_written")
    block = stack.enter_context(nc.Block())

    def unit_before(g, u, lag):
        return (g, u - lag) if u >= lag else (g - 1, u - lag + GU)

    def over_groups(engine, steps):
        for g in range(-2, 2):
            steps(g, g % 2)
        with engine.Fori(1, NM // 2 - 1) as it:
            for j in range(2):
                steps(2 * it + j, j)
        for g in range(NM - 2, NM + 1):
            steps(g, g % 2)

    @block.tensor
    def _(pe):
        def steps(g, j):
            nxt = exists(g + 1, NM)
            for u in range(GU):
                if exists(g, NM):
                    k = GU * g + u
                    pe.wait_ge(key_heads_ready, k + 1)
                    if u == 0:
                        pe.wait_ge(queries_ready, 2 * (g + 1))
                    if exists(g - 1, NM) or u >= 2:
                        pe.wait_ge(shifted_ready, k - 1)
                    nc.tensor.matmul(p_scores[u % 2][:], queries[j][:, u, :, :], key_heads[u % 2][:],
                                     start=True, stop=True).then_inc(scores_made, 1)
                gt, ut = unit_before(g, u, 2)
                if exists(gt, NM):
                    k = GU * gt + ut
                    pe.wait_ge(exps_ready, k + 1)
                    if exists(gt - 1, NM) or ut >= 2:
                        pe.wait_ge(expsT_ready, k - 1)
                    for i in range(4):
                        last = nc.tensor.transpose(p_expsT[ut % 2][:, i, :], exps[ut % 4][:, i, :], ident[:])
                    last.then_inc(exps_turned, 1)
                gv, uv = unit_before(g, u, 3)
                jv = j if u >= 3 else 1 - j
                if exists(gv, NM):
                    k = GU * gv + uv
                    pe.wait_ge(expsT_ready, k + 1)
                    if uv % 4 == 0:
                        pe.wait_ge(values_ready, 4 * gv + uv // 2 + 2)
                    if exists(gv - 1, NM) or uv >= 1:
                        pe.wait_ge(heads_ready, 2 * k)
                    for i in range(4):
                        last = nc.tensor.matmul(p_heads[:, i, :], expsT[uv % 2][:, i, :], values[jv][:, uv, i, :],
                                                start=True, stop=True)
                    last.then_inc(heads_made, 1)
                if u == 0 and nxt:
                    pe.wait_ge(normed_ready, g + 2)
                    if exists(g - 2, NM):
                        pe.wait_ge(stream_ready, g - 1)
                    for t in range(TT):
                        last = nc.tensor.transpose(p_turn[:, t * P:(t + 1) * P], normed[:, t, :], ident[:])
                    last.then_inc(rows_turned, 1)
                if u == 1 and nxt:
                    pe.wait_ge(xT_ready, g + 2)
                    for t in range(TT):
                        last = nc.tensor.transpose(p_turn[:, t * P:(t + 1) * P], ctx_rows[:, t, :], ident[:])
                    last.then_inc(ctx_turned, 1)
                if u == 2 and nxt:
                    pe.wait_ge(ctxT_ready, g + 2)
                    nc.tensor.matmul(p_turn[:], w_query[:], xT[:], start=True, stop=True).then_inc(queries_made, 1)
                if u == 3 and nxt:
                    pe.wait_ge(queries_ready, 2 * (g + 2))
                    nc.tensor.matmul(p_turn[:], w_key[:], ctxT[:, :, 0, :], start=True, stop=True).then_inc(keys_made, 1)
                if u in (4, 6) and nxt:
                    if u == 6 or exists(g, NM):
                        pe.wait_ge(values_ready, 4 * (g + 1) + u - 4)
                    for b in range(4):
                        last = nc.tensor.matmul(p_values[:, b, :], ctxT[:, 2 * (u - 4) + b, :, :], w_value[:],
                                                start=True, stop=True)
                    last.then_inc(values_made, 1)
                if u == 5 and exists(g - 1, NM):
                    pe.wait_ge(headsT_ready, g)
                    if nxt:
                        pe.wait_ge(keys_ready, g + 2)
                    elif exists(g - 2, NM):
                        pe.wait_ge(stream_ready, g - 1)
                    for t in range(TT):
                        o = p_turn[:, t * P:(t + 1) * P]
                        nc.tensor.matmul(o, headsT[:, t * P:(t + 1) * P], w_out[:], start=True, stop=False)
                        last = nc.tensor.matmul(o, one_row[:], b_out[:], start=False, stop=True)
                    last.then_inc(out_made, 1)
                gc, uc = unit_before(g, u, 4)
                if exists(gc, NM):
                    pe.wait_ge(heads_ready, 2 * (GU * gc + uc + 1))
                    if uc == 0 and exists(gc - 1, NM):
                        pe.wait_ge(headsT_ready, gc)
                    nc.tensor.matmul(p_headsT[:, S * uc:S * uc + S], heads[uc % 2][:], fold[:],
                                     start=True, stop=True).then_inc(headsT_made, 1)

        over_groups(pe, steps)

    @block.scalar
    def _(act):
        def steps(g, j):
            nxt = exists(g + 1, NM)
            for u in range(GU):
                if u == 4 and exists(g - 1, NM):
                    act.wait_ge(headsT_made, GU * g)
                    if exists(g - 2, NM):
                        act.wait_ge(out_made, g - 1)
                    nc.scalar.copy(headsT[:], p_headsT[:]).then_inc(headsT_ready, 1)
                if exists(g, NM):
                    k = GU * g + u
                    act.wait_ge(shifted_ready, k + 1)
                    if exists(g - 1, NM) or u >= 4:
                        act.wait_ge(exps_turned, k - 3)
                    nc.scalar.activation(exps[u % 4][:], shifted[u % 2][:], ACT.Exp).then_inc(exps_ready, 1)
                gt, ut = unit_before(g, u, 2)
                if exists(gt, NM):
                    k = GU * gt + ut
                    act.wait_ge(exps_turned, k + 1)
                    if exists(gt - 1, NM) or ut >= 2:
                        act.wait_ge(heads_made, k - 1)
                    nc.scalar.copy(expsT[ut % 2][:], p_expsT[ut % 2][:]).then_inc(expsT_ready, 1)
                if u == 0 and nxt:
                    act.wait_ge(rows_turned, g + 2)
                    if exists(g, NM):
                        act.wait_ge(queries_made, g + 1)
                    nc.scalar.copy(xT[:], p_turn[:]).then_inc(xT_ready, 1)
                if u == 1 and nxt:
                    act.wait_ge(ctx_turned, g + 2)
                    if exists(g, NM):
                        act.wait_ge(values_made, 2 * (g + 1))
                    nc.scalar.copy(ctxT[:], p_turn[:].rearrange("p (b s) -> p b s", s=S).unsqueeze(2)
                                   .broadcast_to([P, GU, 2, S])).then_inc(ctxT_ready, 1)
                if u == 2 and nxt:
                    act.wait_ge(queries_made, g + 2)
                    if exists(g - 1, NM):
                        act.wait_ge(scores_made, GU * g)
                    for half in range(2):
                        rows = slice(half * S, half * S + S)
                        nc.scalar.activation(queries[1 - j][rows, :, half, :], p_turn[rows, :], ACT.Identity,
                                             bias=b_query[rows, :]).then_inc(queries_ready, 1)
                if u == 3 and nxt:
                    act.wait_ge(keys_made, g + 2)
                    if exists(g - 1, NM):
                        act.wait_ge(key_heads_ready, GU * g)
                    nc.scalar.activation(keys[1 - j][:], p_turn[:], ACT.Identity, bias=b_key[:]).then_inc(keys_ready, 1)

        over_groups(act, steps)

    @block.gpsimd
    def _(pool):
        def steps(g, j):
            for u in range(GU):
                gk, uk = (g, u + 1) if u + 1 < GU else (g + 1, 0)
                jk = j if u + 1 < GU else 1 - j
                if exists(gk, NM):
                    k = GU * gk + uk
                    if uk == 0:
                        pool.wait_ge(keys_ready, gk + 1)
                    if exists(gk - 1, NM) or uk >= 2:
                        pool.wait_ge(scores_made, k - 1)
                    nc.gpsimd.tensor_tensor(key_heads[uk % 2][:],
                                            keys[jk][:, uk, :].unsqueeze(1).broadcast_to([P, HH, S]),
                                            head_mask[:].unsqueeze(2).broadcast_to([P, HH, S]),
                                            ALU.mult).then_inc(key_heads_ready, 1)

        over_groups(pool, steps)

    @block.vector
    def _(vec):
        def steps(g, j):
            nxt = exists(g + 1, NM)
            for u in range(GU):
                if exists(g, NM):
                    k = GU * g + u
                    vec.wait_ge(scores_made, k + 1)
                    nc.vector.tensor_reduce(negmax[u % 2][:], p_scores[u % 2][:], AX.X, ALU.max,
                                            negate=True).then_inc(max_ready, 1)
                    vec.wait_ge(max_ready, k + 1)
                    if exists(g - 1, NM) or u >= 2:
                        vec.wait_ge(exps_ready, k - 1)
                    nc.vector.tensor_tensor(shifted[u % 2][:], p_scores[u % 2][:],
                                            negmax[u % 2][:].unsqueeze(2).broadcast_to([P, HH, S]),
                                            ALU.add).then_inc(shifted_ready, 1)
                gv, uv = unit_before(g, u, 3)
                if exists(gv, NM):
                    k = GU * gv + uv
                    vec.wait_ge(heads_made, k + 1)
                    nc.vector.reciprocal(rsums[uv % 2][:], p_heads[:, :, VW - 2:VW]).then_inc(rsums_ready, 1)
                    vec.wait_ge(rsums_ready, k + 1)
                    if exists(gv - 1, NM) or uv >= 2:
                        vec.wait_ge(headsT_made, k - 1)
                    for half in range(2):
                        rows = slice(half * S, half * S + S)
                        w = 2 * DH1
                        nc.vector.tensor_tensor(
                            heads[uv % 2][rows, half * S:half * S + S].rearrange("p (i jj d) -> p i jj d", i=4, jj=2),
                            p_heads[rows, :, half * w:half * w + w].rearrange("p i (jj d) -> p i jj d", jj=2),
                            rsums[uv % 2][rows, :, :].unsqueeze(3).broadcast_to([S, 4, 2, DH1]),
                            ALU.mult).then_inc(heads_ready, 1)
                if u in (4, 6) and nxt:
                    n = 2 * (g + 1) + (u - 4) // 2
                    vec.wait_ge(values_made, n + 1)
                    if exists(g - 1, NM):
                        vec.wait_ge(heads_made, GU * g)
                    for jj in range(2):
                        rows = slice(jj * S, jj * S + S)
                        for half in range(2):
                            cut = slice(half * S, half * S + S)
                            src = p_values[rows, :, cut].rearrange("p b (i jj d) -> p b i jj d", i=4, jj=2)[:, :, :, jj, :]
                            bias = b_value[rows, cut].rearrange("p (i jj d) -> p i jj d", i=4, jj=2)[:, :, jj, :]
                            at = half * 2 * DH1 + jj * DH1
                            last = nc.vector.tensor_tensor(values[1 - j][rows, 2 * (u - 4):2 * (u - 4) + 4, :, at:at + DH1], src,
                                                           bias.unsqueeze(1).broadcast_to([S, 4, 4, DH1]), ALU.add)
                            if half:
                                last.then_inc(values_ready, 1)
                if u == 5 and exists(g - 1, NM):
                    vec.wait_ge(out_made, g)
                    tiles = x_sb[:, bass.ds(TT * (g - 1), TT), :]
                    nc.vector.tensor_tensor(tiles, p_turn[:].rearrange("p (t d) -> p t d", t=TT), tiles,
                                            ALU.add).then_inc(stream_ready, 1)
                if u == 3 and exists(g + 2, NM):
                    if exists(g + 1, NM):
                        vec.wait_ge(ctx_turned, g + 2)
                    for t in range(TT):
                        tile = TT * (g + 2) + t
                        nc.vector.tensor_scalar(normed[:, t, :], x_sb[:, bass.ds(tile, 1), :],
                                                mean[:, bass.ds(tile, 1)], rstd[:, bass.ds(tile, 1)],
                                                ALU.subtract, ALU.mult)
                    nc.vector.tensor_copy(ctx_rows[:], ctx_sb[:, bass.ds(TT * (g + 2), TT), :]).then_inc(normed_ready, 1)
                if u == 7 and exists(g - 1, NM):
                    vec.wait_ge(stream_ready, g)
                    for t in range(TT):
                        tile = TT * (g - 1) + t
                        last = nc.vector.bn_stats(stats[:, bass.ds(tile, 1), :], x_sb[:, bass.ds(tile, 1), :])
                    last.then_inc(stats_written, 1)

        over_groups(vec, steps)


_INS = ['x', 'ctx_1024', 'g_xattn', 'g_ffn', 'L0_xattn_ln1_g', 'L0_xattn_ln1_b', 'L0_xattn_ln2_g', 'L0_xattn_ln2_b',
        'L0_xattn_Wq', 'L0_xattn_Wkv', 'L0_xattn_Wo', 'L0_ffn_Wg', 'L0_ffn_bg', 'L0_ffn_W1', 'L0_ffn_b1', 'L0_ffn_W2',
        'L0_ffn_b2', 'L1_xattn_wq', 'L1_xattn_bq', 'L1_xattn_wk', 'L1_xattn_bk', 'L1_xattn_wv', 'L1_xattn_bv',
        'L1_xattn_wo', 'L1_xattn_bo', 'L1_ffn_wg', 'L1_ffn_w1', 'L1_ffn_w3', 'L1_ffn_w2']


def kernel(**inputs):
    import numpy as np
    import concourse.bacc as bacc
    from concourse.bass_utils import run_bass_kernel_spmd

    nc = bacc.Bacc("TRN2", target_bir_lowering=False, num_devices=1)
    arrays, args = {}, []
    for name in _INS:
        a = np.ascontiguousarray(inputs[name])
        arrays[f"in_{name}_dram"] = a
        args.append(nc.dram_tensor(f"in_{name}_dram", a.shape, mybir.dt.from_np(a.dtype), kind="ExternalInput").ap())
    args.append(nc.dram_tensor("out_0_dram", (B, S, D), F32, kind="ExternalOutput").ap())
    build(nc, *args)
    r = run_bass_kernel_spmd(nc, [arrays], core_ids=[0])
    return r.results[0]["out_0_dram"]
```

```python
from contextlib import ExitStack

import concourse.bass as bass
from concourse import mybir
from concourse.alu_op_type import AluOpType as ALU

F32 = mybir.dt.float32
F32R = mybir.dt.float32r
ACT = mybir.ActivationFunctionType
AX = mybir.AxisListType

P = 128
B, S, D = 128, 64, 128
TOK = B * S
NT = TOK // P
EPS = 1e-5
H0, DH0 = 16, 64
INNER = H0 * DH0
SCALE0 = 1.0 / 8.0
GB = 4
GT = GB * S
NG = B // GB
UN = 2 * GB
E0, F0 = 8, 512
H1, DH1 = 16, 8
E1, I1 = 8, 256
MT = 512
NM = TOK // MT


def exists(g, n):
    return (0 <= g < n) if isinstance(g, int) else True


ROOT_AT = 8
LN_STEPS = 9
AGAIN_AT = LN_STEPS + 3


def layer_norm_factors(nc, vec, stats, mean, rstd, tmp, step_done, sqrt_ready):
    m_even, v_even, m_odd, v_odd = stats[:, :, 1], stats[:, :, 2], stats[:, :, 4], stats[:, :, 5]
    arg, var, root = tmp[:, 0, :], tmp[:, 1, :], tmp[:, 2, :]
    steps = 0

    def step(instruction):
        nonlocal steps
        steps += 1
        instruction.then_inc(step_done, 1)
        vec.wait_ge(step_done, steps)

    step(nc.vector.tensor_tensor(mean, m_even, m_odd, ALU.add))
    step(nc.vector.tensor_scalar(mean, mean, 0.5, None, ALU.mult))
    step(nc.vector.tensor_tensor(arg, m_even, m_odd, ALU.subtract))
    step(nc.vector.tensor_tensor(arg, arg, arg, ALU.mult))
    step(nc.vector.tensor_tensor(var, v_even, v_odd, ALU.add))
    step(nc.vector.tensor_scalar(var, var, 1.0 / P, None, ALU.mult))
    step(nc.vector.scalar_tensor_tensor(var, arg, 0.25, var, ALU.mult, ALU.add))
    step(nc.vector.tensor_scalar(arg, var, EPS, None, ALU.add))
    vec.wait_ge(sqrt_ready, 1)
    step(nc.vector.reciprocal(rstd, root))


def factors_again(nc, vec, rstd, tmp, step_done, sqrt_ready):
    arg, var, root = tmp[:, 0, :], tmp[:, 1, :], tmp[:, 2, :]
    steps = LN_STEPS

    def step(instruction):
        nonlocal steps
        steps += 1
        instruction.then_inc(step_done, 1)
        vec.wait_ge(step_done, steps)

    step(nc.vector.tensor_tensor(arg, rstd, rstd, ALU.mult))
    step(nc.vector.tensor_tensor(arg, arg, var, ALU.mult))
    step(nc.vector.tensor_scalar(arg, arg, EPS, None, ALU.add))
    vec.wait_ge(sqrt_ready, 2)
    step(nc.vector.reciprocal(var, root))
    step(nc.vector.tensor_tensor(rstd, rstd, var, ALU.mult))


def build(nc, x, ctx_in, g_xattn, g_ffn, ln1_g, ln1_b, ln2_g, ln2_b, wq0, wkv0, wo0,
          gate0, gate0_b, w1_0, b1_0, w2_0, b2_0, wq1, bq1, wk1, bk1, wv1, bv1, wo1, bo1,
          gate1, w1_1, w3_1, w2_1, out):
    with ExitStack() as stack:
        def sem(name):
            return stack.enter_context(nc.semaphore(name))

        def sb(name, shape, dt=F32):
            return stack.enter_context(nc.sbuf_tensor(name, shape, dt))

        x_sb = sb("x_sb", [P, NT, D])
        ctx_sb = sb("ctx_sb", [P, NT, D])
        ident = sb("ident", [P, P])
        gates = sb("gates", [P, 4])
        all_stats, all_mean, all_rstd = sb("stats", [P, 2 * NT, 6]), sb("mean", [P, 2 * NT]), sb("rstd", [P, 2 * NT])
        all_tmp = sb("ln_tmp", [P, 3, 2 * NT])
        stats, mean, rstd, tmp = all_stats[:, 0:NT, :], all_mean[:, 0:NT], all_rstd[:, 0:NT], all_tmp[:, :, 0:NT]
        cols = sb("cols", [P, 4])

        with ExitStack() as inner:
            attention_0(nc, inner, sem, x, ctx_in, g_xattn, g_ffn, ln1_g, ln1_b, ln2_g, ln2_b, wq0, wkv0, wo0,
                        x_sb, ctx_sb, ident, gates, all_stats, all_mean, all_rstd, all_tmp, cols)
        with ExitStack() as inner:
            experts_0(nc, inner, sem, gate0, gate0_b, w1_0, b1_0, w2_0, b2_0,
                      x_sb, ident, gates, stats, mean, rstd, tmp)
        with ExitStack() as inner:
            attention_1(nc, inner, sem, wq1, bq1, wk1, bk1, wv1, bv1, wo1, bo1,
                        x_sb, ctx_sb, ident, gates, stats, mean, rstd, tmp)
        with ExitStack() as inner:
            experts_1(nc, inner, sem, gate1, w1_1, w3_1, w2_1,
                      x_sb, ident, gates, stats, mean, rstd, tmp, out)


def attention_0(nc, stack, new_sem, x, ctx_in, g_xattn, g_ffn, ln1_g, ln1_b, ln2_g, ln2_b, wq0, wkv0, wo0,
                x_sb, ctx_sb, ident, gates, stats, mean, rstd, tmp, cols):
    def sb(name, shape, dt=F32):
        return stack.enter_context(nc.sbuf_tensor(name, shape, dt))

    def sem(name):
        return new_sem("a0_" + name)

    score_hi = sb("score_hi", [P, H0, P], F32R)
    score_lo = sb("score_lo", [P, H0, P], F32R)
    value_hi = sb("value_hi", [P, H0, P], F32R)
    value_lo = sb("value_lo", [P, H0, P], F32R)

    with ExitStack() as setup:
        def ssb(name, shape, dt=F32):
            return setup.enter_context(nc.sbuf_tensor(name, shape, dt))

        def ssem(name):
            return new_sem("s_" + name)

        wq_sb = ssb("wq_sb", [P, INNER])
        wkv_sb = ssb("wkv_sb", [P, 2 * INNER])
        wo_sb = ssb("wo_sb", [DH0, H0, P])
        wT = [ssb(f"wT{i}", [DH0, 3, 4, P]) for i in range(2)]
        scaled = ssb("scaled", [P, 4, P])
        valued = ssb("valued", [P, 4, P])
        g_row = ssb("g_row", [P, 4])
        pT = [setup.enter_context(nc.psum_tensor(f"s_pT{i}", [DH0, 4, P], F32)) for i in range(6)]
        pA = setup.enter_context(nc.psum_tensor("s_pA", [P, 4, P], F32))
        pB = setup.enter_context(nc.psum_tensor("s_pB", [P, 4, P], F32))
        NL = 8
        LT = NT // NL
        rows_in = [ssem(f"rows_in{i}") for i in range(NL)]
        weights_in, gates_in, cols_in = ssem("weights_in"), ssem("gates_in"), ssem("cols_in")
        ident_step = ssem("ident_step")
        gates_ready = ssem("gates_ready")
        stats_done, ln_step, sqrt_ready = ssem("stats_done"), ssem("ln_step"), ssem("sqrt_ready")
        wT_filled, wT_taken = ssem("wT_filled"), ssem("wT_taken")
        ab_filled, score_hi_ready, scaled_ready, score_lo_ready = ssem("ab_filled"), ssem("score_hi_ready"), ssem("scaled_ready"), ssem("score_lo_ready")
        valued_ready, value_lo_ready = ssem("valued_ready"), ssem("value_lo_ready")
        block = setup.enter_context(nc.Block())
        xv = x.rearrange("(t two) s d -> (two s) t d", two=2)
        cv = ctx_in.rearrange("(t two) s d -> (two s) t d", two=2)

        @block.sync
        def _(sp):
            for i, v in enumerate((g_xattn, g_ffn)):
                sp.dma_start(g_row[:, 2 * i:2 * i + 2],
                             v.rearrange("(a n) -> a n", a=1).broadcast_to([P, 2])).then_inc(gates_in, 16)
            def rows(i):
                sp.dma_start(x_sb[:, i * LT:(i + 1) * LT, :], xv[:, i * LT:(i + 1) * LT, :]).then_inc(rows_in[i], 16)

            rows(0)
            rows(1)
            sp.dma_start(wq_sb[:], wq0).then_inc(weights_in, 16)
            sp.dma_start(wkv_sb[:], wkv0).then_inc(weights_in, 16)
            sp.dma_start(wo_sb[:], wo0.rearrange("(h e) f -> e h f", h=H0)).then_inc(weights_in, 16)
            for i in range(2, NL):
                rows(i)

        @block.gpsimd
        def _(pool):
            for i, v in enumerate((ln1_g, ln1_b, ln2_g, ln2_b)):
                pool.dma_start(cols[:, i:i + 1], v.rearrange("(p a) -> p a", a=1)).then_inc(cols_in, 16)
            nc.gpsimd.memset(ident[:], 0.0).then_inc(ident_step, 1)
            pool.wait_ge(ident_step, 1)
            nc.gpsimd.affine_select(out=ident[:], in_=ident[:], compare_op=ALU.not_equal, fill=1.0, base=0,
                                    pattern=[[-1, P]], channel_multiplier=1).then_inc(ident_step, 1)
            for c in range(4):
                hs = slice(4 * c, 4 * c + 4)
                pool.wait_ge(score_hi_ready, c + 1)
                nc.gpsimd.tensor_tensor(score_lo[:, hs, :], scaled[:], score_hi[:, hs, :].bitcast(F32),
                                        ALU.subtract).then_inc(score_lo_ready, 1)
                pool.wait_ge(valued_ready, 2 * c + 2)
                nc.gpsimd.tensor_tensor(value_lo[:, hs, :], valued[:], value_hi[:, hs, :].bitcast(F32),
                                        ALU.subtract).then_inc(value_lo_ready, 1)

        @block.scalar
        def _(act):
            for i in range(NL):
                act.dma_start(ctx_sb[:, i * LT:(i + 1) * LT, :], cv[:, i * LT:(i + 1) * LT, :]).then_inc(rows_in[i], 16)
            act.wait_ge(gates_in, 16 * 2)
            nc.scalar.activation(gates[:], g_row[:], ACT.Tanh).then_inc(gates_ready, 1)

            def take_turned(c):
                for i in range(3):
                    act.wait_ge(wT_filled, 3 * c + i + 1)
                    if c >= 2:
                        act.wait_ge(ab_filled, c - 1)
                    nc.scalar.copy(wT[c % 2][:, i, :, :], pT[3 * (c % 2) + i][:]).then_inc(wT_taken, 1)

            take_turned(0)
            for c in range(4):
                if c < 3:
                    take_turned(c + 1)
                act.wait_ge(ab_filled, c + 1)
                if c == 0:
                    act.wait_ge(gates_ready, 1)
                else:
                    act.wait_ge(value_lo_ready, c)
                nc.scalar.activation(value_hi[:, 4 * c:4 * c + 4, :], pB[:], ACT.Copy,
                                     scale=gates[:, 0:1]).then_inc(valued_ready, 1)
                nc.scalar.activation(valued[:], pB[:], ACT.Copy, scale=gates[:, 0:1]).then_inc(valued_ready, 1)
            for n, cut in ((ROOT_AT, 2 * NT), (AGAIN_AT, NT)):
                act.wait_ge(ln_step, n)
                nc.scalar.activation(tmp[:, 2, 0:cut], tmp[:, 0, 0:cut], ACT.Sqrt).then_inc(sqrt_ready, 1)

        @block.tensor
        def _(pe):
            pe.wait_ge(ident_step, 2)
            pe.wait_ge(weights_in, 48)

            def turn(c):
                for i in range(3):
                    if c >= 2:
                        pe.wait_ge(wT_taken, 3 * (c - 2) + i + 1)
                    for h in range(4):
                        col = (4 * c + h) * DH0
                        src = (wq_sb, wkv_sb, wkv_sb)[i][:, (0, 0, INNER)[i] + col:(0, 0, INNER)[i] + col + DH0]
                        last = nc.tensor.transpose(pT[3 * (c % 2) + i][:, h, :], src, ident[:])
                    last.then_inc(wT_filled, 1)

            turn(0)
            for c in range(4):
                if c < 3:
                    turn(c + 1)
                pe.wait_ge(wT_taken, 3 * c + 3)
                if c:
                    pe.wait_ge(scaled_ready, c)
                    pe.wait_ge(valued_ready, 2 * c)
                w = wT[c % 2]
                for h in range(4):
                    nc.tensor.matmul(pA[:, h, :], w[:, 0, h, :], w[:, 1, h, :], start=True, stop=True)
                    last = nc.tensor.matmul(pB[:, h, :], w[:, 2, h, :], wo_sb[:, 4 * c + h, :], start=True, stop=True)
                last.then_inc(ab_filled, 1)

        @block.vector
        def _(vec):
            def tile_stats(i):
                vec.wait_ge(rows_in[i], 32)
                for t in range(i * LT, (i + 1) * LT):
                    nc.vector.bn_stats(stats[:, t, :], x_sb[:, t, :])
                    last = nc.vector.bn_stats(stats[:, NT + t, :], ctx_sb[:, t, :])
                last.then_inc(stats_done, 1)

            for i in range(3):
                tile_stats(i)
            for c in range(4):
                hs = slice(4 * c, 4 * c + 4)
                vec.wait_ge(ab_filled, c + 1)
                if c:
                    vec.wait_ge(score_lo_ready, c)
                nc.vector.tensor_scalar(scaled[:], pA[:], SCALE0, None, ALU.mult).then_inc(scaled_ready, 1)
                vec.wait_ge(scaled_ready, c + 1)
                nc.vector.tensor_copy(score_hi[:, hs, :], scaled[:]).then_inc(score_hi_ready, 1)
                tile_stats(3 + c)
            for i in range(7, NL):
                tile_stats(i)
            vec.wait_ge(stats_done, NL)
            vec.wait_ge(cols_in, 16 * 4)
            layer_norm_factors(nc, vec, stats, mean[:], rstd[:], tmp, ln_step, sqrt_ready)
            factors_again(nc, vec, rstd[:, 0:NT], tmp[:, :, 0:NT], ln_step, sqrt_ready)

    normed = sb("a0_normed", [P, 4, D])
    kvT = [sb(f"a0_kvT{j}", [P, GB, 2, S]) for j in range(2)]
    latT_hi = [sb(f"a0_latT_hi{j}", [P, GB, S], F32R) for j in range(2)]
    latT_lo = [sb(f"a0_latT_lo{j}", [P, GB, S], F32R) for j in range(2)]
    rows_hi = [sb(f"a0_rows_hi{j}", [P, GB, D], F32R) for j in range(2)]
    rows_lo = [sb(f"a0_rows_lo{j}", [P, GB, D], F32R) for j in range(2)]
    queries = sb("a0_queries", [P, H0 // 2, GB, 2, S])
    attended_hi = sb("a0_attended_hi", [P, H0, GB, S], F32R)
    attended_lo = sb("a0_attended_lo", [P, H0, GB, S], F32R)
    exps = [sb(f"a0_exps{i}", [P, 4, P]) for i in range(2)]
    probs = [sb(f"a0_probs{i}", [P, 4, P]) for i in range(2)]
    probsT_hi = [sb(f"a0_probsT_hi{i}", [P, 4 * P], F32R) for i in range(2)]
    probsT_lo = [sb(f"a0_probsT_lo{i}", [P, 4 * P], F32R) for i in range(2)]
    negmax = [sb(f"a0_negmax{i}", [P, 4]) for i in range(2)]
    sums = [sb(f"a0_sums{i}", [P, 4]) for i in range(2)]
    rsums = [sb(f"a0_rsums{i}", [P, 4]) for i in range(2)]
    projT = sb("a0_projT", [P, GT])

    def ps(name, shape):
        return stack.enter_context(nc.psum_tensor("a0_" + name, shape, F32))

    p_scores = [ps(f"p_scores{i}", [P, 4, P]) for i in range(2)]
    p_probsT = [ps(f"p_probsT{i}", [P, 4 * P]) for i in range(2)]
    p_attended = ps("p_attended", [P, UN, S])
    p_queries = ps("p_queries", [P, 2, GB, S])
    p_turn = ps("p_turn", [P, 4, P])
    p_proj = ps("p_proj", [P, GT])

    normed_ready = sem("normed_ready")
    rows_turned = sem("rows_turned")
    kvT_ready = sem("kvT_ready")
    lat_hi_ready, lat_lo_ready = sem("lat_hi_ready"), sem("lat_lo_ready")
    keys_turned = sem("keys_turned")
    rows_hi_ready, rows_lo_ready = sem("rows_hi_ready"), sem("rows_lo_ready")
    queries_made, queries_ready = sem("queries_made"), sem("queries_ready")
    scores_made = sem("scores_made")
    max_ready, exps_ready = sem("max_ready"), sem("exps_ready")
    rsums_ready, probs_ready = sem("rsums_ready"), sem("probs_ready")
    probs_turned, probsT_hi_ready, probsT_lo_ready = sem("probs_turned"), sem("probsT_hi_ready"), sem("probsT_lo_ready")
    attended_made, attended_hi_ready, attended_lo_ready = sem("attended_made"), sem("attended_hi_ready"), sem("attended_lo_ready")
    half_projected = sem("half_projected")
    proj_ready = sem("proj_ready")
    proj_turned, stream_ready = sem("proj_turned"), sem("stream_ready")
    stats_written = sem("stats_written")
    block = stack.enter_context(nc.Block())


    def query_chunk_of(g, j, u):
        return (g + 1, 1 - j, u - 4) if u >= 4 else (g, j, u + 4)

    def projected_by(g, u):
        return (g, 0) if u == 7 else (g - 1, u + 1)

    def unit_before(g, u, lag):
        return (g, u - lag) if u >= lag else (g - 1, u - lag + UN)

    def over_groups(engine, steps):
        for g in range(-2, 2):
            steps(g, g % 2)
        with engine.Fori(1, NG // 2 - 1) as it:
            for j in range(2):
                steps(2 * it + j, j)
        for g in range(NG - 2, NG + 2):
            steps(g, g % 2)

    @block.tensor
    def _(pe):
        def split_product(o, w_hi, w_lo, m_hi, m_lo, start=True, stop=True):
            nc.tensor.matmul(o, w_hi, m_hi, start=start, stop=False)
            nc.tensor.matmul(o, w_hi, m_lo, start=False, stop=False)
            return nc.tensor.matmul(o, w_lo, m_hi, start=False, stop=stop)

        def query_chunk(g, j, c):
            if c == 0:
                pe.wait_ge(lat_hi_ready, g + 1)
                pe.wait_ge(lat_lo_ready, g + 1)
            if exists(g - 1, NG) or c:
                pe.wait_ge(queries_ready, 8 * g + c)
            for h in range(2):
                last = split_product(p_queries[:, h, :, :], score_hi[:, 2 * c + h, :], score_lo[:, 2 * c + h, :],
                                     latT_hi[j][:], latT_lo[j][:])
            last.then_inc(queries_made, 1)

        def project(g, r):
            if r % 4 == 0:
                pe.wait_ge(attended_lo_ready, UN * g + r + 4)
            if r == 0 and exists(g - 1, NG):
                pe.wait_ge(proj_ready, g)
            for h in (2 * r, 2 * r + 1):
                last = split_product(p_proj[:], value_hi[:, h, :], value_lo[:, h, :], attended_hi[:, h, :, :],
                                     attended_lo[:, h, :, :], start=h == 0, stop=h == H0 - 1)
            if r % 4 == 3:
                last.then_inc(half_projected, 1)

        def steps(g, j):
            for u in range(UN):
                gq, jq, c = query_chunk_of(g, j, u)
                if exists(gq, NG):
                    query_chunk(gq, jq, c)
                if exists(g, NG):
                    half, b = divmod(u, GB)
                    if b == 0:
                        pe.wait_ge(queries_ready, 8 * g + 4 * half + 4)
                    if exists(g - 1, NG) or u >= 2:
                        pe.wait_ge(exps_ready, UN * g + u - 1)
                    for i in range(4):
                        last = nc.tensor.matmul(p_scores[u % 2][:, i, :], queries[:, 4 * half + i, b, :, :],
                                                kvT[j][:, b, :, :], start=True, stop=True)
                    last.then_inc(scores_made, 1)
                gt, ut = unit_before(g, u, 2)
                if exists(gt, NG):
                    pe.wait_ge(probs_ready, UN * gt + ut + 1)
                    if exists(gt - 1, NG) or ut >= 2:
                        pe.wait_ge(probsT_lo_ready, UN * gt + ut - 1)
                    for i in range(4):
                        last = nc.tensor.transpose(p_probsT[u % 2][:, i * P:(i + 1) * P], probs[u % 2][:, i, :], ident[:])
                    last.then_inc(probs_turned, 1)
                ga, ua = unit_before(g, u, 3)
                ja = j if u >= 3 else 1 - j
                if exists(ga, NG):
                    pe.wait_ge(probsT_lo_ready, UN * ga + ua + 1)
                    if ua == 0:
                        pe.wait_ge(rows_lo_ready, ga + 1)
                    if exists(ga - 1, NG) or ua >= 1:
                        pe.wait_ge(attended_lo_ready, UN * ga + ua)
                    split_product(p_attended[:], rows_hi[ja][:, ua % GB, :], rows_lo[ja][:, ua % GB, :],
                                  probsT_hi[ua % 2][:], probsT_lo[ua % 2][:]).then_inc(attended_made, 1)
                if u == 0 and exists(g + 1, NG):
                    pe.wait_ge(normed_ready, g + 2)
                    if exists(g - 3, NG):
                        pe.wait_ge(stream_ready, g - 2)
                    for i in range(4):
                        last = nc.tensor.transpose(p_turn[:, i, :], normed[:, i, :], ident[:])
                    last.then_inc(rows_turned, 1)
                if u == 2 and exists(g + 1, NG):
                    pe.wait_ge(kvT_ready, 2 * (g + 2))
                    for b in range(GB):
                        last = nc.tensor.transpose(p_turn[:, b, :], kvT[1 - j][:, b, :, :], ident[:])
                    last.then_inc(keys_turned, 1)
                if u == 5 and exists(g - 2, NG):
                    if exists(g + 1, NG):
                        pe.wait_ge(rows_lo_ready, g + 2)
                    elif exists(g - 3, NG):
                        pe.wait_ge(stream_ready, g - 2)
                    pe.wait_ge(proj_ready, g - 1)
                    for t in range(2):
                        last = nc.tensor.transpose(p_turn[:, t, :], projT[:, t * P:(t + 1) * P], ident[:])
                    last.then_inc(proj_turned, 1)
                gp, r = projected_by(g, u)
                if exists(gp, NG):
                    project(gp, r)

        over_groups(pe, steps)

    @block.scalar
    def _(act):
        def take_projection(g):
            act.wait_ge(half_projected, 2 * (g + 1))
            if exists(g - 1, NG):
                act.wait_ge(proj_turned, g)
            nc.scalar.copy(projT[:], p_proj[:]).then_inc(proj_ready, 1)

        def take_queries(g, c):
            act.wait_ge(queries_made, 8 * g + c + 1)
            if c % 4 == 0 and exists(g - 1, NG):
                act.wait_ge(scores_made, UN * (g - 1) + c + 4)
            nc.scalar.copy(queries[:, c, :, :, :].rearrange("p b h s -> p h b s"),
                           p_queries[:]).then_inc(queries_ready, 1)

        def steps(g, j):
            for u in range(UN):
                if u == 7 and exists(g - 1, NG):
                    take_projection(g - 1)
                gq, jq, c = query_chunk_of(g, j, u)
                if exists(gq, NG):
                    take_queries(gq, c)
                gt, ut = unit_before(g, u, 2)
                if exists(gt, NG):
                    act.wait_ge(probs_turned, UN * gt + ut + 1)
                    if exists(gt - 1, NG) or ut >= 2:
                        act.wait_ge(attended_made, UN * gt + ut - 1)
                    nc.scalar.copy(probsT_hi[u % 2][:], p_probsT[u % 2][:]).then_inc(probsT_hi_ready, 1)
                ga, ua = unit_before(g, u, 3)
                if exists(ga, NG):
                    act.wait_ge(attended_made, UN * ga + ua + 1)
                    half, b = divmod(ua, GB)
                    if b == 0 and exists(ga - 1, NG):
                        act.wait_ge(half_projected, 2 * ga - 1 + half)
                    nc.scalar.copy(attended_hi[:, UN * half:UN * half + UN, b, :],
                                   p_attended[:]).then_inc(attended_hi_ready, 1)
                if exists(g, NG):
                    act.wait_ge(max_ready, UN * g + u + 1)
                    if exists(g - 1, NG) or u >= 2:
                        act.wait_ge(probs_ready, UN * g + u - 1)
                    for i in range(4):
                        last = nc.scalar.activation(exps[u % 2][:, i, :], p_scores[u % 2][:, i, :], ACT.Exp,
                                                    bias=negmax[u % 2][:, i:i + 1], accum_out=sums[u % 2][:, i:i + 1])
                    last.then_inc(exps_ready, 1)
                if u == 2 and exists(g + 1, NG):
                    act.wait_ge(keys_turned, g + 2)
                    if exists(g - 1, NG):
                        act.wait_ge(attended_made, UN * g)
                    nc.scalar.copy(rows_hi[1 - j][:], p_turn[:]).then_inc(rows_hi_ready, 1)

        over_groups(act, steps)

    @block.vector
    def _(vec):
        def steps(g, j):
            for u in range(UN):
                gs, us = unit_before(g, u, 1)
                if exists(gs, NG):
                    k = UN * gs + us
                    vec.wait_ge(exps_ready, k + 1)
                    if exists(gs - 1, NG) or us >= 2:
                        vec.wait_ge(probs_ready, k - 1)
                    nc.vector.reciprocal(rsums[us % 2][:], sums[us % 2][:]).then_inc(rsums_ready, 1)
                if exists(g, NG):
                    vec.wait_ge(scores_made, UN * g + u + 1)
                    nc.vector.tensor_reduce(negmax[u % 2][:], p_scores[u % 2][:], AX.X, ALU.max,
                                            negate=True).then_inc(max_ready, 1)
                gt, ut = unit_before(g, u, 2)
                if exists(gt, NG):
                    vec.wait_ge(probsT_hi_ready, UN * gt + ut + 1)
                    nc.vector.tensor_tensor(probsT_lo[u % 2][:], p_probsT[u % 2][:], probsT_hi[u % 2][:].bitcast(F32),
                                            ALU.subtract).then_inc(probsT_lo_ready, 1)
                ga, ua = unit_before(g, u, 3)
                if exists(ga, NG):
                    vec.wait_ge(attended_hi_ready, UN * ga + ua + 1)
                    half, b = divmod(ua, GB)
                    own = slice(UN * half, UN * half + UN)
                    nc.vector.tensor_tensor(attended_lo[:, own, b, :], p_attended[:], attended_hi[:, own, b, :].bitcast(F32),
                                            ALU.subtract).then_inc(attended_lo_ready, 1)
                if u == 1 and exists(g + 1, NG):
                    vec.wait_ge(rows_turned, g + 2)
                    if exists(g - 1, NG):
                        vec.wait_ge(scores_made, UN * g)
                        vec.wait_ge(lat_lo_ready, g)
                    for kind in range(2):
                        src = p_turn[:, 2 * kind:2 * kind + 2, :].rearrange("p t (two s) -> p (t two) s", two=2)
                        nc.vector.tensor_scalar(kvT[1 - j][:, :, kind, :], src, cols[:, 2 * kind:2 * kind + 1],
                                                cols[:, 2 * kind + 1:2 * kind + 2], ALU.mult, ALU.add).then_inc(kvT_ready, 1)
                    vec.wait_ge(kvT_ready, 2 * (g + 2))
                    if exists(g - 1, NG):
                        vec.wait_ge(queries_made, 8 * g)
                    nc.vector.tensor_copy(latT_hi[1 - j][:], kvT[1 - j][:, :, 1, :]).then_inc(lat_hi_ready, 1)
                if u == 3 and exists(g + 1, NG):
                    vec.wait_ge(rows_hi_ready, g + 2)
                    nc.vector.tensor_tensor(rows_lo[1 - j][:], p_turn[:], rows_hi[1 - j][:].bitcast(F32),
                                            ALU.subtract).then_inc(rows_lo_ready, 1)
                if u == 6 and exists(g - 2, NG):
                    vec.wait_ge(proj_turned, g - 1)
                    tiles = x_sb[:, bass.ds(2 * (g - 2), 2), :]
                    nc.vector.tensor_tensor(tiles, p_turn[:, 0:2, :], tiles, ALU.add).then_inc(stream_ready, 1)
                if u == 4 and exists(g + 2, NG):
                    if exists(g + 1, NG):
                        vec.wait_ge(rows_turned, g + 2)
                    for kind, (rows, behind) in enumerate(((ctx_sb, NT), (x_sb, 0))):
                        for t in range(2):
                            tile = 2 * (g + 2) + t
                            factor = bass.ds(tile + behind, 1)
                            last = nc.vector.tensor_scalar(normed[:, 2 * kind + t, :], rows[:, bass.ds(tile, 1), :],
                                                           mean[:, factor], rstd[:, factor],
                                                           ALU.subtract, ALU.mult)
                    last.then_inc(normed_ready, 1)
                if u == 7 and exists(g - 2, NG):
                    vec.wait_ge(stream_ready, g - 1)
                    for t in range(2):
                        tile = 2 * (g - 2) + t
                        last = nc.vector.bn_stats(stats[:, bass.ds(tile, 1), :], x_sb[:, bass.ds(tile, 1), :])
                    last.then_inc(stats_written, 1)

        over_groups(vec, steps)
        vec.wait_ge(stats_written, NG)

    @block.gpsimd
    def _(pool):
        def steps(g, j):
            for u in range(UN):
                gs, us = unit_before(g, u, 1)
                if exists(gs, NG):
                    k = UN * gs + us
                    pool.wait_ge(rsums_ready, k + 1)
                    if exists(gs - 1, NG) or us >= 2:
                        pool.wait_ge(probs_turned, k - 1)
                    nc.gpsimd.tensor_tensor(probs[us % 2][:], exps[us % 2][:],
                                            rsums[us % 2][:].unsqueeze(2).broadcast_to([P, 4, P]),
                                            ALU.mult).then_inc(probs_ready, 1)
                if u == 1 and exists(g + 1, NG):
                    pool.wait_ge(lat_hi_ready, g + 2)
                    nc.gpsimd.tensor_tensor(latT_lo[1 - j][:], kvT[1 - j][:, :, 1, :], latT_hi[1 - j][:].bitcast(F32),
                                            ALU.subtract).then_inc(lat_lo_ready, 1)

        over_groups(pool, steps)

def new_factors(nc, new_sem, tag, stats, mean, rstd, tmp):
    step_done = new_sem(tag + "_ln_step")
    sqrt_ready = new_sem(tag + "_sqrt_ready")

    def on_vector(vec):
        layer_norm_factors(nc, vec, stats, mean, rstd, tmp, step_done, sqrt_ready)

    def on_scalar(act):
        act.wait_ge(step_done, ROOT_AT)
        nc.scalar.activation(tmp[:, 2, :], tmp[:, 0, :], ACT.Sqrt).then_inc(sqrt_ready, 1)

    return on_vector, on_scalar


def expert_weights_0(nc, stack, new_sem, gate0, gate0_b, w1_0, b1_0, w2_0, b2_0, stats, mean, rstd, tmp):
    def sb(name, shape, dt=F32):
        return stack.enter_context(nc.sbuf_tensor("m0_" + name, shape, dt))

    n_chunks = F0 // P
    up = [(sb("up_hi", [P, E0 * n_chunks, P], F32R), sb("up_lo", [P, E0 * n_chunks, P], F32R))]
    down = (sb("down_hi", [P, E0 * n_chunks, P], F32R), sb("down_lo", [P, E0 * n_chunks, P], F32R))
    router, router_b = sb("router", [P, E0]), sb("router_b", [P, E0])
    up_b, down_b = sb("up_b", [P, E0, n_chunks]), sb("down_b", [P, E0])
    with ExitStack() as setup:
        raw = [setup.enter_context(nc.sbuf_tensor(f"m0_raw{i}", [P, E0 * n_chunks, P], F32)) for i in range(2)]
        weights_in = [new_sem(f"m0_in{i}") for i in range(4)]
        small_in = new_sem("m0_small_in")
        hi_ready = new_sem("m0_weights_hi")
        factors_vector, factors_scalar = new_factors(nc, new_sem, "m0", stats, mean, rstd, tmp)
        block = setup.enter_context(nc.Block())
        half = E0 // 2
        views = [(raw[0], w1_0.rearrange("e d (c m) -> d e c m", m=P)), (raw[1], w2_0.rearrange("e (c p) f -> p e c f", p=P))]
        parts = [(i, s) for s in range(2) for i in range(2)]

        @block.sync
        def _(sp):
            for n, (i, s) in enumerate(parts):
                dst = views[i][0][:].rearrange("p (e c) m -> p e c m", e=E0)
                for e in range(s * half, (s + 1) * half):
                    sp.dma_start(dst[:, e, :, :], views[i][1][:, e, :, :]).then_inc(weights_in[n], 16)

        @block.gpsimd
        def _(pool):
            pool.dma_start(router[:], gate0).then_inc(small_in, 16)
            pool.dma_start(router_b[:], gate0_b.rearrange("(a n) -> a n", a=1).broadcast_to([P, E0])).then_inc(small_in, 16)
            for e in range(E0):
                pool.dma_start(up_b[:, e, :], b1_0[e, :].rearrange("(c p) -> p c", p=P),
                               allow_slow_non_contiguous=True).then_inc(small_in, 16)
            pool.dma_start(down_b[:], b2_0.rearrange("e f -> f e"), allow_slow_non_contiguous=True).then_inc(small_in, 16)
            pool.wait_ge(small_in, 16 * (E0 + 3))

        @block.scalar
        def _(act):
            factors_scalar(act)
            for n, (i, s) in enumerate(parts):
                rows = slice(s * half * n_chunks, (s + 1) * half * n_chunks)
                act.wait_ge(weights_in[n], 16 * half)
                nc.scalar.copy((up[0], down)[i][0][:, rows, :], raw[i][:, rows, :]).then_inc(hi_ready, 1)

        @block.vector
        def _(vec):
            factors_vector(vec)
            for n, (i, s) in enumerate(parts):
                rows = slice(s * half * n_chunks, (s + 1) * half * n_chunks)
                hi, lo = (up[0], down)[i]
                vec.wait_ge(hi_ready, n + 1)
                nc.vector.tensor_tensor(lo[:, rows, :], raw[i][:, rows, :], hi[:, rows, :].bitcast(F32), ALU.subtract)

    return up, down, router, router_b, up_b, down_b


def expert_weights_1(nc, stack, new_sem, gate1, w1_1, w3_1, w2_1, ident, stats, mean, rstd, tmp):
    def sb(name, shape, dt=F32):
        return stack.enter_context(nc.sbuf_tensor("m1_" + name, shape, dt))

    n_chunks = I1 // P
    up = [(sb(f"up_hi{i}", [P, E1 * n_chunks, P], F32R), sb(f"up_lo{i}", [P, E1 * n_chunks, P], F32R)) for i in range(2)]
    down = (sb("down_hi", [P, E1 * n_chunks, P], F32R), sb("down_lo", [P, E1 * n_chunks, P], F32R))
    router = sb("router", [P, E1])
    with ExitStack() as setup:
        raw = [setup.enter_context(nc.sbuf_tensor(f"m1_raw{i}", [P, E1 * n_chunks, P], F32)) for i in range(3)]
        raw_router = setup.enter_context(nc.sbuf_tensor("m1_raw_router", [E1, P], F32))
        banks = [setup.enter_context(nc.psum_tensor(f"m1_bank{i}", [P, 4, P], F32)) for i in range(4)]
        weights_in = [new_sem(f"m1_in{i}") for i in range(3)]
        turned = new_sem("m1_turned")
        hi_ready = new_sem("m1_weights_hi")
        lo_ready = new_sem("m1_weights_lo")
        router_turned = new_sem("m1_router_turned")
        factors_vector, factors_scalar = new_factors(nc, new_sem, "m1", stats, mean, rstd, tmp)
        block = setup.enter_context(nc.Block())
        quads = E1 * n_chunks // 4
        hi_lo = [up[0], up[1], down]

        @block.sync
        def _(sp):
            for i, w in enumerate((w1_1, w3_1)):
                sp.dma_start(raw[i][:].rearrange("p (e c) h -> p e c h", e=E1),
                             w.rearrange("e (c p) h -> p e c h", p=P)).then_inc(weights_in[i], 16)
            sp.dma_start(raw[2][:].rearrange("p (e c) i -> p e (c i)", e=E1),
                         w2_1.rearrange("e h i -> h e i")).then_inc(weights_in[2], 16)
            sp.dma_start(raw_router[:], gate1).then_inc(weights_in[2], 16)

        @block.tensor
        def _(pe):
            for i in range(3):
                pe.wait_ge(weights_in[i], 32 if i == 2 else 16)
                for q in range(quads):
                    n = quads * i + q
                    if n >= 4:
                        pe.wait_ge(lo_ready, n - 3)
                    for b in range(4):
                        last = nc.tensor.transpose(banks[n % 4][:, b, :], raw[i][:, 4 * q + b, :], ident[:])
                    last.then_inc(turned, 1)
            pe.wait_ge(lo_ready, 3 * quads - 3)
            nc.tensor.transpose(banks[0][:, 0, 0:E1], raw_router[:], ident[0:E1, 0:E1]).then_inc(router_turned, 1)

        @block.scalar
        def _(act):
            factors_scalar(act)
            for n in range(3 * quads):
                i, q = divmod(n, quads)
                act.wait_ge(turned, n + 1)
                nc.scalar.copy(hi_lo[i][0][:, 4 * q:4 * q + 4, :], banks[n % 4][:]).then_inc(hi_ready, 1)

        @block.vector
        def _(vec):
            factors_vector(vec)
            for n in range(3 * quads):
                i, q = divmod(n, quads)
                hi, lo = hi_lo[i]
                vec.wait_ge(hi_ready, n + 1)
                nc.vector.tensor_tensor(lo[:, 4 * q:4 * q + 4, :], banks[n % 4][:], hi[:, 4 * q:4 * q + 4, :].bitcast(F32),
                                        ALU.subtract).then_inc(lo_ready, 1)
            vec.wait_ge(router_turned, 1)
            nc.vector.tensor_copy(router[:], banks[0][:, 0, 0:E1])

    return up, down, router


def experts(nc, stack, new_sem, tag, up, down, router, router_b, up_b, down_b, sum_eps, gate_col,
            x_sb, ident, gates, stats, mean, rstd, out):
    n_exp = 8
    n_chunks = down[0].shape[1] // n_exp
    gated = up_b is None
    N = n_exp * n_chunks
    LAG = 4 if gated else 5
    ROWS_TURN, LOGITS, SPLIT = (1, 3, 5) if gated else (2, 5, 6)
    GATE_A, GATE_B, GATE_C = (4, 6, 8) if gated else (7, 10, 13)
    GATES_TURN, OUT_TURN, NORM = (11, 14, 15) if gated else (18, 23, 28)
    TT = MT // P

    def sb(name, shape, dt=F32):
        return stack.enter_context(nc.sbuf_tensor(f"{tag}_{name}", shape, dt))

    def sem(name):
        return new_sem(f"{tag}_{name}")

    def ps(name, shape):
        return stack.enter_context(nc.psum_tensor(f"{tag}_{name}", shape, F32))

    normed = sb("normed", [P, TT, D])
    xT = sb("xT", [P, MT])
    xT_hi = [sb(f"xT_hi{j}", [P, MT], F32R) for j in range(2)]
    xT_lo = [sb(f"xT_lo{j}", [P, MT], F32R) for j in range(2)]
    silu = [sb(f"silu{i}", [P, MT]) for i in range(4)] if gated else None
    linear = [sb(f"linear{i}", [P, MT]) for i in range(4)] if gated else None
    hidden = [sb(f"hidden{i}", [P, MT]) for i in range(4)]
    RING = 8
    hidden_hi = [sb(f"hidden_hi{i}", [P, MT], F32R) for i in range(RING)]
    hidden_lo = [sb(f"hidden_lo{i}", [P, MT], F32R) for i in range(RING)]
    GATE_RING = 4
    gate_rows = [sb(f"gate_rows{i}", [P, MT]) for i in range(GATE_RING)]
    terms = [sb(f"terms{i}", [P, MT]) for i in range(2)]
    acc = [sb(f"acc{j}", [P, MT]) for j in range(2)]
    small = {name: sb(name, [P, TT, n_exp]) for name in ("logits", "shifted", "exps", "soft", "rank", "mask", "weights")}
    per_row = {name: sb(name, [P, TT]) for name in ("negmax", "sums", "rsums", "chosen", "rchosen")}
    above, equal = sb("above", [P, TT, n_exp, n_exp]), sb("equal", [P, TT, n_exp, n_exp])
    earlier = sb("earlier", [P, n_exp, n_exp])
    ones = sb("ones", [P, 1])
    gatesT = sb("gatesT", [n_exp, MT])
    gates_dram = [nc.dram_tensor(f"{tag}_gates_dram{j}", (n_exp, MT), F32, kind="Internal").ap() for j in range(2)]

    p_hidden = [ps(f"p_hidden{i}", [P, MT]) for i in range(4)]
    p_out = [ps(f"p_out{i}", [P, MT]) for i in range(2)]
    p_turn = ps("p_turn", [P, MT])

    const_step = sem("const_step")
    normed_ready, rows_turned, xT_ready = sem("normed_ready"), sem("rows_turned"), sem("xT_ready")
    xT_hi_ready, split_ready = sem("xT_hi_ready"), sem("split_ready")
    logits_made, gate_step, exps_ready = sem("logits_made"), sem("gate_step"), sem("exps_ready")
    weights_turned, gatesT_ready = sem("weights_turned"), sem("gatesT_ready")
    gates_stored = sem("gates_stored")
    gate_rows_in = [sem(f"gate_rows_in{i}") for i in range(GATE_RING)]
    up_made, linear_ready, hidden_ready = sem("up_made"), sem("linear_ready") if gated else None, sem("hidden_ready")
    own_hi_ready = sem("own_hi_ready") if not gated else None
    act_hi_ready = sem("act_hi_ready") if not gated else None
    hi_ready, lo_ready, down_made = sem("hi_ready"), sem("lo_ready"), sem("down_made")
    term_ready, added = sem("term_ready"), sem("added")
    acc_turned, stream_ready = sem("acc_turned"), sem("stream_ready")
    stored = sem("stored") if out is not None else None
    stats_written = sem("stats_written") if out is None else None
    block = stack.enter_context(nc.Block())
    STEPS_A, STEPS_B, STEPS_C = 3, 5, 8
    STEPS = STEPS_A + STEPS_B + STEPS_C

    def on_pool(n):
        return gated or n % 2 == 0

    def on_scalar(n):
        return not gated and n % 4 == 1

    def chunk_before(g, n, lag):
        return (g, n - lag) if n >= lag else (g - 1, n - lag + N)

    def over_groups(engine, steps):
        for g in (-2, -1, 0, 1):
            steps(g, g % 2)
        with engine.Fori(1, NM // 2 - 1) as it:
            for j in range(2):
                steps(2 * it + j, j)
        for g in (NM - 2, NM - 1, NM):
            steps(g, g % 2)

    def gates_wanted(g, e):
        return 16 * (n_exp // GATE_RING * g + e // GATE_RING + 1)

    @block.sync
    def _(sp):
        def steps(g, j):
            if exists(g, NM):
                sp.wait_ge(gatesT_ready, g + 1)
                if exists(g - 2, NM):
                    for i in range(GATE_RING):
                        sp.wait_ge(gate_rows_in[i], gates_wanted(g - 2, n_exp - GATE_RING + i))
                sp.dma_start(gates_dram[j], gatesT[:]).then_inc(gates_stored, 16)
                sp.wait_ge(gates_stored, 16 * (g + 1))
                for e in range(n_exp):
                    if exists(g - 1, NM) or e >= GATE_RING:
                        sp.wait_ge(term_ready, n_exp * g + e + 1 - GATE_RING)
                    sp.dma_start(gate_rows[e % GATE_RING][:],
                                 gates_dram[j][e:e + 1, :].broadcast_to([P, MT])).then_inc(gate_rows_in[e % GATE_RING], 16)
            if exists(g - 1, NM) and out is not None:
                sp.wait_ge(stream_ready, g)
                sp.dma_start(view[:, bass.ds(TT * (g - 1), TT), :], x_sb[:, bass.ds(TT * (g - 1), TT), :]).then_inc(stored, 16)

        if out is not None:
            view = out.rearrange("(t two) s d -> (two s) t d", two=2)
        over_groups(sp, steps)
        if out is not None:
            sp.wait_ge(stored, 16 * NM)

    @block.tensor
    def _(pe):
        def split_product(o, w, row, hi, lo, first, last_one):
            nc.tensor.matmul(o, w[0][:, row, :], hi, start=first, stop=False)
            nc.tensor.matmul(o, w[0][:, row, :], lo, start=False, stop=False)
            return nc.tensor.matmul(o, w[1][:, row, :], hi, start=False, stop=last_one)

        def turn_gates(g):
            pe.wait_ge(gate_step, STEPS * (g + 1))
            for t in range(TT):
                last = nc.tensor.transpose(p_turn[0:n_exp, t * P:(t + 1) * P], small["weights"][:, t, :], ident[:])
            last.then_inc(weights_turned, 1)

        def steps(g, j):
            first = not exists(g - 1, NM) and exists(g, NM)
            for n in range(N):
                e, c = divmod(n, n_chunks)
                if exists(g, NM):
                    if n == 0:
                        pe.wait_ge(split_ready, g + 1)
                    if gated:
                        if exists(g - 1, NM) or n >= 2:
                            pe.wait_ge(linear_ready, N * g + n - 1)
                        split_product(p_hidden[n % 2][:], up[0], n, xT_hi[j][:], xT_lo[j][:], True, True)
                        split_product(p_hidden[2 + n % 2][:], up[1], n, xT_hi[j][:], xT_lo[j][:], True, True).then_inc(up_made, 1)
                    else:
                        if exists(g - 1, NM) or n >= 4:
                            pe.wait_ge(hidden_ready, N * g + n - 3)
                        split_product(p_hidden[n % 4][:], up[0], n, xT_hi[j][:], xT_lo[j][:], True, True).then_inc(up_made, 1)
                gd, nd = chunk_before(g, n, LAG)
                if exists(gd, NM):
                    ed, cd = divmod(nd, n_chunks)
                    pe.wait_ge(lo_ready, N * gd + nd + 1)
                    if cd == 0 and (exists(gd - 1, NM) or ed >= 2):
                        pe.wait_ge(term_ready, n_exp * gd + ed - 1)
                    split_product(p_out[ed % 2][:], down, nd, hidden_hi[nd % RING][:], hidden_lo[nd % RING][:],
                                  cd == 0, cd == n_chunks - 1).then_inc(down_made, 1)
                if n == 1 and first:
                    turn_gates(g)
                if n == ROWS_TURN and exists(g + 1, NM):
                    pe.wait_ge(normed_ready, g + 2)
                    if exists(g - 2, NM):
                        pe.wait_ge(stream_ready, g - 1)
                    elif exists(g, NM):
                        pe.wait_ge(gatesT_ready, g + 1)
                    for t in range(TT):
                        last = nc.tensor.transpose(p_turn[:, t * P:(t + 1) * P], normed[:, t, :], ident[:])
                    last.then_inc(rows_turned, 1)
                if n == LOGITS and exists(g + 1, NM):
                    pe.wait_ge(xT_ready, g + 2)
                    for t in range(TT):
                        last = nc.tensor.matmul(p_turn[:, t * n_exp:(t + 1) * n_exp], xT[:, t * P:(t + 1) * P], router[:],
                                                start=True, stop=True)
                    last.then_inc(logits_made, 1)
                if n == GATES_TURN and exists(g + 1, NM) and exists(g, NM):
                    turn_gates(g + 1)
                if n == OUT_TURN and exists(g - 1, NM):
                    pe.wait_ge(added, (n_exp - 1) * g)
                    if exists(g + 1, NM):
                        pe.wait_ge(gatesT_ready, g + 2)
                    else:
                        pe.wait_ge(stream_ready, g - 1)
                    for t in range(TT):
                        last = nc.tensor.transpose(p_turn[:, t * P:(t + 1) * P], acc[1 - j][:, t * P:(t + 1) * P], ident[:])
                    last.then_inc(acc_turned, 1)

        over_groups(pe, steps)

    @block.scalar
    def _(act):
        def steps(g, j):
            for n in range(N):
                e, c = divmod(n, n_chunks)
                if exists(g, NM):
                    act.wait_ge(up_made, N * g + n + 1)
                    if gated:
                        if exists(g - 1, NM) or n >= 4:
                            act.wait_ge(hidden_ready, N * g + n - 3)
                        nc.scalar.activation(silu[n % 4][:], p_hidden[n % 2][:], ACT.Silu)
                        nc.scalar.copy(linear[n % 4][:], p_hidden[2 + n % 2][:]).then_inc(linear_ready, 1)
                    else:
                        if exists(g - 1, NM) or n >= 4:
                            act.wait_ge(lo_ready, N * g + n - 3)
                        nc.scalar.activation(hidden[n % 4][:], p_hidden[n % 4][:], ACT.Gelu_apprx_tanh,
                                             bias=up_b[:, e, c:c + 1]).then_inc(hidden_ready, 1)
                gs, ns = chunk_before(g, n, 1)
                if exists(gs, NM) and on_scalar(ns):
                    act.wait_ge(hidden_ready, N * gs + ns + 1)
                    if exists(gs - 1, NM) or ns >= RING:
                        act.wait_ge(down_made, N * gs + ns + 1 - RING)
                    nc.scalar.copy(hidden_hi[ns % RING][:], hidden[ns % 4][:]).then_inc(act_hi_ready, 1)
                if n == ROWS_TURN + 1 and exists(g + 1, NM):
                    act.wait_ge(rows_turned, g + 2)
                    if exists(g, NM):
                        act.wait_ge(split_ready, g + 1)
                        act.wait_ge(logits_made, g + 1)
                    nc.scalar.copy(xT[:], p_turn[:]).then_inc(xT_ready, 1)
                if n == GATE_A + 1 and exists(g + 1, NM):
                    act.wait_ge(gate_step, STEPS * (g + 1) + STEPS_A)
                    nc.scalar.activation(small["exps"][:], small["shifted"][:], ACT.Exp).then_inc(exps_ready, 1)

        over_groups(act, steps)

    @block.gpsimd
    def _(pool):
        nc.gpsimd.memset(ones[:], 1.0).then_inc(const_step, 1)
        nc.gpsimd.memset(earlier[:], 1.0).then_inc(const_step, 1)
        pool.wait_ge(const_step, 2)
        nc.gpsimd.affine_select(out=earlier[:], in_=earlier[:], compare_op=ALU.is_gt, fill=0.0, base=0,
                                pattern=[[1, n_exp], [-1, n_exp]], channel_multiplier=0).then_inc(const_step, 1)

        def steps(g, j):
            for n in range(N):
                if exists(g, NM) and on_pool(n):
                    k = N * g + n
                    pool.wait_ge(hidden_ready, k + 1)
                    if exists(g - 1, NM) or n >= RING:
                        pool.wait_ge(down_made, k + 1 - RING)
                    nc.gpsimd.tensor_tensor(hidden_hi[n % RING][:], hidden[n % 4][:], ones[:].broadcast_to([P, MT]),
                                            ALU.mult).then_inc(hi_ready, 1)
                gd, nd = chunk_before(g, n, LAG + 1)
                jd = j if n > LAG else 1 - j
                ed, cd = divmod(nd, n_chunks)
                if exists(gd, NM) and cd == n_chunks - 1 and ed:
                    pool.wait_ge(term_ready, n_exp * gd + ed + 1)
                    if ed > 1:
                        pool.wait_ge(added, (n_exp - 1) * gd + ed - 1)
                    nc.gpsimd.tensor_tensor(acc[jd][:], acc[jd][:], terms[ed % 2][:], ALU.add).then_inc(added, 1)

        over_groups(pool, steps)

    @block.vector
    def _(vec):
        def split_rows(g, j):
            vec.wait_ge(xT_ready, g + 1)
            if exists(g - 2, NM):
                vec.wait_ge(up_made, N * (g - 1))
            nc.vector.tensor_copy(xT_hi[j][:], xT[:]).then_inc(xT_hi_ready, 1)
            vec.wait_ge(xT_hi_ready, g + 1)
            nc.vector.tensor_tensor(xT_lo[j][:], xT[:], xT_hi[j][:].bitcast(F32), ALU.subtract).then_inc(split_ready, 1)

        def gate_steps(g, part):
            done = (0, STEPS_A, STEPS_A + STEPS_B)[part]

            def step(instruction):
                nonlocal done
                done += 1
                instruction.then_inc(gate_step, 1)
                vec.wait_ge(gate_step, STEPS * g + done)

            def spread(rows):
                return rows[:].unsqueeze(2).broadcast_to([P, TT, n_exp])

            lg = small["logits"][:]
            if part == 0:
                vec.wait_ge(logits_made, g + 1)
                src = p_turn[:, 0:TT * n_exp].rearrange("p (t e) -> p t e", t=TT)
                if router_b is not None:
                    step(nc.vector.tensor_tensor(lg, src, router_b[:].unsqueeze(1).broadcast_to([P, TT, n_exp]), ALU.add))
                else:
                    step(nc.vector.tensor_copy(lg, src))
                step(nc.vector.tensor_reduce(per_row["negmax"][:], lg, AX.X, ALU.max, negate=True))
                step(nc.vector.tensor_tensor(small["shifted"][:], lg, spread(per_row["negmax"]), ALU.add))
            if part == 1:
                of_j = lg.unsqueeze(2).broadcast_to([P, TT, n_exp, n_exp])
                of_i = lg.unsqueeze(3).broadcast_to([P, TT, n_exp, n_exp])
                step(nc.vector.tensor_tensor(above[:], of_j, of_i, ALU.is_gt))
                step(nc.vector.tensor_tensor(equal[:], of_j, of_i, ALU.is_equal))
                step(nc.vector.tensor_tensor(equal[:], equal[:],
                                             earlier[:].unsqueeze(1).broadcast_to([P, TT, n_exp, n_exp]), ALU.mult))
                step(nc.vector.tensor_tensor(above[:], above[:], equal[:], ALU.add))
                step(nc.vector.tensor_reduce(small["rank"][:], above[:], AX.X, ALU.add))
            if part == 2:
                vec.wait_ge(exps_ready, g + 1)
                step(nc.vector.tensor_reduce(per_row["sums"][:], small["exps"][:], AX.X, ALU.add))
                step(nc.vector.reciprocal(per_row["rsums"][:], per_row["sums"][:]))
                step(nc.vector.tensor_tensor(small["soft"][:], small["exps"][:], spread(per_row["rsums"]), ALU.mult))
                step(nc.vector.scalar_tensor_tensor(small["mask"][:], small["rank"][:], 1.5, small["soft"][:],
                                                    ALU.is_lt, ALU.mult))
                step(nc.vector.tensor_reduce(per_row["chosen"][:], small["mask"][:], AX.X, ALU.add))
                step(nc.vector.tensor_scalar(per_row["chosen"][:], per_row["chosen"][:], sum_eps, None, ALU.add))
                step(nc.vector.reciprocal(per_row["rchosen"][:], per_row["chosen"][:]))
                if exists(g - 1, NM):
                    vec.wait_ge(weights_turned, g)
                step(nc.vector.scalar_tensor_tensor(small["weights"][:], small["mask"][:], gates[:, gate_col:gate_col + 1],
                                                    spread(per_row["rchosen"]), ALU.mult, ALU.mult))

        def steps(g, j):
            for n in range(N):
                gh, nh = chunk_before(g, n, 1)
                if gated and exists(gh, NM):
                    k = N * gh + nh
                    vec.wait_ge(linear_ready, k + 1)
                    if exists(gh - 1, NM) or nh >= 4:
                        vec.wait_ge(lo_ready, k - 3)
                    nc.vector.tensor_tensor(hidden[nh % 4][:], silu[nh % 4][:], linear[nh % 4][:],
                                            ALU.mult).then_inc(hidden_ready, 1)
                gl, nl = chunk_before(g, n, 2)
                if exists(gl, NM):
                    if gated:
                        vec.wait_ge(hi_ready, N * gl + nl + 1)
                    elif on_pool(nl):
                        vec.wait_ge(hi_ready, N // 2 * gl + nl // 2 + 1)
                    elif on_scalar(nl):
                        vec.wait_ge(act_hi_ready, N // 4 * gl + nl // 4 + 1)
                    else:
                        vec.wait_ge(hidden_ready, N * gl + nl + 1)
                        if exists(gl - 1, NM) or nl >= RING:
                            vec.wait_ge(down_made, N * gl + nl + 1 - RING)
                        nc.vector.tensor_copy(hidden_hi[nl % RING][:], hidden[nl % 4][:]).then_inc(own_hi_ready, 1)
                        vec.wait_ge(own_hi_ready, N // 4 * gl + nl // 4 + 1)
                    nc.vector.tensor_tensor(hidden_lo[nl % RING][:], hidden[nl % 4][:], hidden_hi[nl % RING][:].bitcast(F32),
                                            ALU.subtract).then_inc(lo_ready, 1)
                gd, nd = chunk_before(g, n, LAG + 1)
                jd = j if n > LAG else 1 - j
                ed, cd = divmod(nd, n_chunks)
                if exists(gd, NM) and cd == n_chunks - 1:
                    vec.wait_ge(down_made, N * gd + nd + 1)
                    vec.wait_ge(gate_rows_in[ed % GATE_RING], gates_wanted(gd, ed))
                    if ed == 0:
                        to = acc[jd]
                        if exists(gd - 2, NM):
                            vec.wait_ge(acc_turned, gd - 1)
                    else:
                        to = terms[ed % 2]
                        if ed >= 3:
                            vec.wait_ge(added, (n_exp - 1) * gd + ed - 2)
                        elif exists(gd - 1, NM):
                            vec.wait_ge(added, (n_exp - 1) * gd)
                    bias = down_b[:, ed:ed + 1] if down_b is not None else 0.0
                    nc.vector.scalar_tensor_tensor(to[:], p_out[ed % 2][:], bias, gate_rows[ed % GATE_RING][:],
                                                   ALU.add, ALU.mult).then_inc(term_ready, 1)
                if n == NORM and exists(g + 2, NM):
                    if exists(g + 1, NM):
                        vec.wait_ge(rows_turned, g + 2)
                    for t in range(TT):
                        tile = TT * (g + 2) + t
                        last = nc.vector.tensor_scalar(normed[:, t, :], x_sb[:, bass.ds(tile, 1), :],
                                                       mean[:, bass.ds(tile, 1)], rstd[:, bass.ds(tile, 1)],
                                                       ALU.subtract, ALU.mult)
                    last.then_inc(normed_ready, 1)
                if n == OUT_TURN + 1 and exists(g - 1, NM):
                    vec.wait_ge(acc_turned, g)
                    tiles = x_sb[:, bass.ds(TT * (g - 1), TT), :]
                    nc.vector.tensor_tensor(tiles, p_turn[:].rearrange("p (t d) -> p t d", t=TT), tiles,
                                            ALU.add).then_inc(stream_ready, 1)
                if n == OUT_TURN + 3 and exists(g - 1, NM) and out is None:
                    vec.wait_ge(stream_ready, g)
                    for t in range(TT):
                        tile = TT * (g - 1) + t
                        last = nc.vector.bn_stats(stats[:, bass.ds(tile, 1), :], x_sb[:, bass.ds(tile, 1), :])
                    last.then_inc(stats_written, 1)
                if n == SPLIT and exists(g + 1, NM):
                    split_rows(g + 1, 1 - j)
                if n == GATE_A and exists(g + 1, NM):
                    gate_steps(g + 1, 0)
                if n == GATE_B and exists(g + 1, NM):
                    if not exists(g, NM):
                        vec.wait_ge(const_step, 3)
                    gate_steps(g + 1, 1)
                if n == GATE_C and exists(g + 1, NM):
                    gate_steps(g + 1, 2)
                if n == GATES_TURN + 1 and exists(g + 1, NM):
                    vec.wait_ge(weights_turned, g + 2)
                    if exists(g, NM):
                        vec.wait_ge(gates_stored, 16 * (g + 1))
                    nc.vector.tensor_copy(gatesT[:], p_turn[0:n_exp, :]).then_inc(gatesT_ready, 1)

        over_groups(vec, steps)


def experts_0(nc, stack, new_sem, gate0, gate0_b, w1_0, b1_0, w2_0, b2_0, x_sb, ident, gates, stats, mean, rstd, tmp):
    up, down, router, router_b, up_b, down_b = expert_weights_0(
        nc, stack, new_sem, gate0, gate0_b, w1_0, b1_0, w2_0, b2_0, stats, mean, rstd, tmp)
    experts(nc, stack, new_sem, "m0", up, down, router, router_b, up_b, down_b, 1e-8, 2, x_sb, ident, gates, stats, mean, rstd, None)


def experts_1(nc, stack, new_sem, gate1, w1_1, w3_1, w2_1, x_sb, ident, gates, stats, mean, rstd, tmp, out):
    up, down, router = expert_weights_1(nc, stack, new_sem, gate1, w1_1, w3_1, w2_1, ident, stats, mean, rstd, tmp)
    experts(nc, stack, new_sem, "m1", up, down, router, None, None, None, 0.0, 3, x_sb, ident, gates, stats, mean, rstd, out)


def attention_1(nc, stack, new_sem, wq1, bq1, wk1, bk1, wv1, bv1, wo1, bo1, x_sb, ctx_sb, ident, gates, stats, mean, rstd, tmp):
    GU = MT // S
    TT = MT // P
    HH = H1 // 2
    VW = 2 * 2 * DH1 + 2

    def sb(name, shape, dt=F32):
        return stack.enter_context(nc.sbuf_tensor("a1_" + name, shape, dt))

    def sem(name):
        return new_sem("a1_" + name)

    def ps(name, shape):
        return stack.enter_context(nc.psum_tensor("a1_" + name, shape, F32))

    w_query, w_key, w_value, w_out = sb("w_query", [P, P]), sb("w_key", [P, P]), sb("w_value", [P, P]), sb("w_out", [P, P])
    b_query, b_key, b_value = sb("b_query", [P, 1]), sb("b_key", [P, 1]), sb("b_value", [P, P])
    b_out = sb("b_out", [P, P])
    fold = sb("fold", [P, S])
    head_mask = sb("head_mask", [P, HH])
    normed, ctx_rows = sb("normed", [P, TT, D]), sb("ctx_rows", [P, TT, D])
    xT, ctxT = sb("xT", [P, MT]), sb("ctxT", [P, GU, 2, S])
    queries = sb("queries", [P, MT])
    queries_hi = [sb(f"queries_hi{j}", [P, GU, 2, S], F32R) for j in range(2)]
    queries_lo = [sb(f"queries_lo{j}", [P, GU, 2, S], F32R) for j in range(2)]
    keys = sb("keys", [P, MT])
    keys_hi = [sb(f"keys_hi{j}", [P, GU, S], F32R) for j in range(2)]
    keys_lo = [sb(f"keys_lo{j}", [P, GU, S]) for j in range(2)]
    values = [sb(f"values{j}", [P, GU, 4, VW]) for j in range(2)]
    key_heads_hi = [sb(f"key_heads_hi{i}", [P, HH, S], F32R) for i in range(2)]
    key_heads_lo = [sb(f"key_heads_lo{i}", [P, HH, S], F32R) for i in range(2)]
    negmax = [sb(f"negmax{i}", [P, HH]) for i in range(2)]
    shifted = [sb(f"shifted{i}", [P, HH, S]) for i in range(2)]
    exps = [sb(f"exps{i}", [P, 4, P]) for i in range(4)]
    expsT = [sb(f"expsT{i}", [P, 4, P]) for i in range(2)]
    rsums = [sb(f"rsums{i}", [P, 4, 2]) for i in range(2)]
    heads = [sb(f"heads{i}", [P, P]) for i in range(2)]
    headsT = sb("headsT", [P, MT])

    p_scores = [ps(f"p_scores{i}", [P, HH, S]) for i in range(2)]
    p_expsT = [ps(f"p_expsT{i}", [P, 4, P]) for i in range(2)]
    p_heads = ps("p_heads", [P, 4, VW])
    p_headsT = ps("p_headsT", [P, MT])
    p_turn = ps("p_turn", [P, MT])
    p_values = ps("p_values", [P, 4, 4 * 4 * DH1])

    with ExitStack() as setup:
        weights_in = new_sem("a1_weights_in")
        cleared = new_sem("a1_cleared")
        step_ready = new_sem("a1_setup_step")
        factors_vector, factors_scalar = new_factors(nc, new_sem, "a1", stats, mean, rstd, tmp)
        block = setup.enter_context(nc.Block())
        loads = [(w_query, wq1), (w_key, wk1), (w_value, wv1), (w_out, wo1),
                 (b_query, bq1.rearrange("(p a) -> p a", a=1)), (b_key, bk1.rearrange("(p a) -> p a", a=1)),
                 (b_value, bv1.rearrange("(a n) -> a n", a=1).broadcast_to([P, P])), (b_out, bo1.rearrange("(a n) -> a n", a=1).broadcast_to([P, P]))]

        @block.sync
        def _(sp):
            for dst, src in loads:
                sp.dma_start(dst[:], src).then_inc(weights_in, 16)

        @block.gpsimd
        def _(pool):
            for j in range(2):
                nc.gpsimd.memset(queries_hi[j][:].bitcast(F32), 0.0)
                nc.gpsimd.memset(queries_lo[j][:].bitcast(F32), 0.0)
                nc.gpsimd.memset(heads[j][:], 0.0)
                nc.gpsimd.memset(values[j][:], 0.0).then_inc(cleared, 1)
            pool.wait_ge(cleared, 2)
            for j in range(2):
                for jj in range(2):
                    nc.gpsimd.memset(values[j][S * jj:S * jj + S, :, :, VW - 2 + jj], 1.0)

        @block.scalar
        def _(act):
            factors_scalar(act)

        @block.vector
        def _(vec):
            factors_vector(vec)
            nc.vector.tensor_tensor(fold[:], ident[:, 0:S], ident[:, S:P], ALU.add).then_inc(step_ready, 1)
            vec.wait_ge(step_ready, 1)
            nc.vector.tensor_reduce(head_mask[:], fold[:].rearrange("p (j d) -> p j d", d=DH1), AX.X, ALU.add)
            vec.wait_ge(weights_in, 16 * len(loads))
            nc.vector.tensor_scalar(w_out[:], w_out[:], gates[:, 1:2], None, ALU.mult)
            nc.vector.tensor_scalar(b_out[:], b_out[:], gates[:, 1:2], None, ALU.mult)

    normed_ready, rows_turned, xT_ready = sem("normed_ready"), sem("rows_turned"), sem("xT_ready")
    ctx_turned, ctxT_ready = sem("ctx_turned"), sem("ctxT_ready")
    queries_made, queries_hi_ready, queries_lo_ready = sem("queries_made"), sem("queries_hi_ready"), sem("queries_lo_ready")
    keys_made, keys_hi_ready, keys_lo_ready = sem("keys_made"), sem("keys_hi_ready"), sem("keys_lo_ready")
    values_made, values_ready = sem("values_made"), sem("values_ready")
    key_heads_ready, scores_made, max_ready = sem("key_heads_ready"), sem("scores_made"), sem("max_ready")
    shifted_ready, exps_ready, exps_turned, expsT_ready = sem("shifted_ready"), sem("exps_ready"), sem("exps_turned"), sem("expsT_ready")
    heads_made, rsums_ready, heads_ready, headsT_made = sem("heads_made"), sem("rsums_ready"), sem("heads_ready"), sem("headsT_made")
    bias_added = sem("bias_added")
    headsT_ready, out_made, stream_ready, stats_written = sem("headsT_ready"), sem("out_made"), sem("stream_ready"), sem("stats_written")
    block = stack.enter_context(nc.Block())

    def unit_before(g, u, lag):
        return (g, u - lag) if u >= lag else (g - 1, u - lag + GU)

    def over_groups(engine, steps):
        for g in range(-2, 2):
            steps(g, g % 2)
        with engine.Fori(1, NM // 2 - 1) as it:
            for j in range(2):
                steps(2 * it + j, j)
        for g in range(NM - 2, NM + 1):
            steps(g, g % 2)

    @block.tensor
    def _(pe):
        def steps(g, j):
            nxt = exists(g + 1, NM)
            for u in range(GU):
                if exists(g, NM):
                    k = GU * g + u
                    pe.wait_ge(key_heads_ready, 2 * (k + 1))
                    if u == 0:
                        pe.wait_ge(queries_lo_ready, 2 * (g + 1))
                    if exists(g - 1, NM) or u >= 2:
                        pe.wait_ge(shifted_ready, k - 1)
                    o, q_hi, k_hi = p_scores[u % 2][:], queries_hi[j][:, u, :, :], key_heads_hi[u % 2][:]
                    nc.tensor.matmul(o, q_hi, k_hi, start=True, stop=False)
                    nc.tensor.matmul(o, q_hi, key_heads_lo[u % 2][:], start=False, stop=False)
                    nc.tensor.matmul(o, queries_lo[j][:, u, :, :], k_hi, start=False, stop=True).then_inc(scores_made, 1)
                gt, ut = unit_before(g, u, 2)
                if exists(gt, NM):
                    k = GU * gt + ut
                    pe.wait_ge(exps_ready, k + 1)
                    if exists(gt - 1, NM) or ut >= 2:
                        pe.wait_ge(expsT_ready, k - 1)
                    for i in range(4):
                        last = nc.tensor.transpose(p_expsT[ut % 2][:, i, :], exps[ut % 4][:, i, :], ident[:])
                    last.then_inc(exps_turned, 1)
                gv, uv = unit_before(g, u, 3)
                jv = j if u >= 3 else 1 - j
                if exists(gv, NM):
                    k = GU * gv + uv
                    pe.wait_ge(expsT_ready, k + 1)
                    if uv % 4 == 0:
                        pe.wait_ge(values_ready, 4 * gv + uv // 2 + 2)
                    if exists(gv - 1, NM) or uv >= 1:
                        pe.wait_ge(heads_ready, 2 * k)
                    for i in range(4):
                        last = nc.tensor.matmul(p_heads[:, i, :], expsT[uv % 2][:, i, :], values[jv][:, uv, i, :],
                                                start=True, stop=True)
                    last.then_inc(heads_made, 1)
                if u == 0 and nxt:
                    pe.wait_ge(normed_ready, g + 2)
                    if exists(g - 2, NM):
                        pe.wait_ge(stream_ready, g - 1)
                    for t in range(TT):
                        last = nc.tensor.transpose(p_turn[:, t * P:(t + 1) * P], normed[:, t, :], ident[:])
                    last.then_inc(rows_turned, 1)
                if u == 1 and nxt:
                    pe.wait_ge(xT_ready, g + 2)
                    for t in range(TT):
                        last = nc.tensor.transpose(p_turn[:, t * P:(t + 1) * P], ctx_rows[:, t, :], ident[:])
                    last.then_inc(ctx_turned, 1)
                if u == 2 and nxt:
                    pe.wait_ge(ctxT_ready, g + 2)
                    nc.tensor.matmul(p_turn[:], w_query[:], xT[:], start=True, stop=True).then_inc(queries_made, 1)
                if u == 3 and nxt:
                    pe.wait_ge(queries_hi_ready, 3 * (g + 2))
                    nc.tensor.matmul(p_turn[:], w_key[:], ctxT[:, :, 0, :], start=True, stop=True).then_inc(keys_made, 1)
                if u in (4, 6) and nxt:
                    if u == 6 or exists(g, NM):
                        pe.wait_ge(values_ready, 4 * (g + 1) + u - 4)
                    for b in range(4):
                        last = nc.tensor.matmul(p_values[:, b, :], ctxT[:, 2 * (u - 4) + b, :, :], w_value[:],
                                                start=True, stop=True)
                    last.then_inc(values_made, 1)
                if u == 5 and exists(g - 1, NM):
                    pe.wait_ge(headsT_ready, g)
                    if nxt:
                        pe.wait_ge(keys_hi_ready, 2 * (g + 2))
                    elif exists(g - 2, NM):
                        pe.wait_ge(stream_ready, g - 1)
                    for t in range(TT):
                        last = nc.tensor.matmul(p_turn[:, t * P:(t + 1) * P], headsT[:, t * P:(t + 1) * P], w_out[:],
                                                start=True, stop=True)
                    last.then_inc(out_made, 1)
                gc, uc = unit_before(g, u, 4)
                if exists(gc, NM):
                    pe.wait_ge(heads_ready, 2 * (GU * gc + uc + 1))
                    if uc == 0 and exists(gc - 1, NM):
                        pe.wait_ge(headsT_ready, gc)
                    nc.tensor.matmul(p_headsT[:, S * uc:S * uc + S], heads[uc % 2][:], fold[:],
                                     start=True, stop=True).then_inc(headsT_made, 1)

        over_groups(pe, steps)

    @block.scalar
    def _(act):
        def steps(g, j):
            nxt = exists(g + 1, NM)
            for u in range(GU):
                if u == 4 and exists(g - 1, NM):
                    act.wait_ge(headsT_made, GU * g)
                    if exists(g - 2, NM):
                        act.wait_ge(out_made, g - 1)
                    nc.scalar.copy(headsT[:], p_headsT[:]).then_inc(headsT_ready, 1)
                gt, ut = unit_before(g, u, 2)
                if exists(gt, NM):
                    k = GU * gt + ut
                    act.wait_ge(exps_turned, k + 1)
                    if exists(gt - 1, NM) or ut >= 2:
                        act.wait_ge(heads_made, k - 1)
                    nc.scalar.copy(expsT[ut % 2][:], p_expsT[ut % 2][:]).then_inc(expsT_ready, 1)
                if exists(g, NM):
                    k = GU * g + u
                    act.wait_ge(shifted_ready, k + 1)
                    if exists(g - 1, NM) or u >= 4:
                        act.wait_ge(exps_turned, k - 3)
                    nc.scalar.activation(exps[u % 4][:], shifted[u % 2][:], ACT.Exp).then_inc(exps_ready, 1)
                if u == 0 and nxt:
                    act.wait_ge(rows_turned, g + 2)
                    if exists(g, NM):
                        act.wait_ge(queries_made, g + 1)
                    nc.scalar.copy(xT[:], p_turn[:]).then_inc(xT_ready, 1)
                if u == 1 and nxt:
                    act.wait_ge(ctx_turned, g + 2)
                    if exists(g, NM):
                        act.wait_ge(values_made, 2 * (g + 1))
                    nc.scalar.copy(ctxT[:], p_turn[:].rearrange("p (b s) -> p b s", s=S).unsqueeze(2)
                                   .broadcast_to([P, GU, 2, S])).then_inc(ctxT_ready, 1)
                if u == 2 and nxt:
                    act.wait_ge(queries_made, g + 2)
                    if exists(g - 1, NM):
                        act.wait_ge(scores_made, GU * g)
                    if exists(g, NM):
                        act.wait_ge(queries_lo_ready, 2 * (g + 1))
                    nc.scalar.activation(queries[:], p_turn[:], ACT.Identity, bias=b_query[:]).then_inc(queries_hi_ready, 1)
                    for half in range(2):
                        rows = slice(half * S, half * S + S)
                        nc.scalar.activation(queries_hi[1 - j][rows, :, half, :], p_turn[rows, :], ACT.Identity,
                                             bias=b_query[rows, :]).then_inc(queries_hi_ready, 1)
                if u == 3 and nxt:
                    act.wait_ge(keys_made, g + 2)
                    if exists(g - 1, NM):
                        act.wait_ge(key_heads_ready, 2 * GU * g)
                    if exists(g, NM):
                        act.wait_ge(keys_lo_ready, g + 1)
                    nc.scalar.activation(keys[:], p_turn[:], ACT.Identity, bias=b_key[:]).then_inc(keys_hi_ready, 1)
                    nc.scalar.activation(keys_hi[1 - j][:], p_turn[:], ACT.Identity, bias=b_key[:]).then_inc(keys_hi_ready, 1)

        over_groups(act, steps)

    @block.gpsimd
    def _(pool):
        def steps(g, j):
            for u in range(GU):
                if u == 5 and exists(g, NM):
                    pool.wait_ge(normed_ready, g + 1)
                    tiles = x_sb[:, bass.ds(TT * g, TT), :]
                    nc.gpsimd.tensor_tensor(tiles, tiles, b_out[:].unsqueeze(1).broadcast_to([P, TT, D]),
                                            ALU.add).then_inc(bias_added, 1)
                gk, uk = (g, u + 1) if u + 1 < GU else (g + 1, 0)
                jk = j if u + 1 < GU else 1 - j
                if exists(gk, NM):
                    k = GU * gk + uk
                    if uk == 0:
                        pool.wait_ge(keys_lo_ready, gk + 1)
                    if exists(gk - 1, NM) or uk >= 2:
                        pool.wait_ge(scores_made, k - 1)
                    for heads_of, part in ((key_heads_hi[uk % 2], keys_hi[jk][:, uk, :].bitcast(F32)),
                                           (key_heads_lo[uk % 2], keys_lo[jk][:, uk, :])):
                        nc.gpsimd.tensor_tensor(heads_of[:], part.unsqueeze(1).broadcast_to([P, HH, S]),
                                                head_mask[:].unsqueeze(2).broadcast_to([P, HH, S]),
                                                ALU.mult).then_inc(key_heads_ready, 1)

        over_groups(pool, steps)

    @block.vector
    def _(vec):
        def steps(g, j):
            nxt = exists(g + 1, NM)
            for u in range(GU):
                if exists(g, NM):
                    k = GU * g + u
                    vec.wait_ge(scores_made, k + 1)
                    nc.vector.tensor_reduce(negmax[u % 2][:], p_scores[u % 2][:], AX.X, ALU.max,
                                            negate=True).then_inc(max_ready, 1)
                    vec.wait_ge(max_ready, k + 1)
                    if exists(g - 1, NM) or u >= 2:
                        vec.wait_ge(exps_ready, k - 1)
                    nc.vector.tensor_tensor(shifted[u % 2][:], p_scores[u % 2][:],
                                            negmax[u % 2][:].unsqueeze(2).broadcast_to([P, HH, S]),
                                            ALU.add).then_inc(shifted_ready, 1)
                gv, uv = unit_before(g, u, 3)
                if exists(gv, NM):
                    k = GU * gv + uv
                    vec.wait_ge(heads_made, k + 1)
                    nc.vector.reciprocal(rsums[uv % 2][:], p_heads[:, :, VW - 2:VW]).then_inc(rsums_ready, 1)
                    vec.wait_ge(rsums_ready, k + 1)
                    if exists(gv - 1, NM) or uv >= 2:
                        vec.wait_ge(headsT_made, k - 1)
                    for half in range(2):
                        rows = slice(half * S, half * S + S)
                        w = 2 * DH1
                        nc.vector.tensor_tensor(
                            heads[uv % 2][rows, half * S:half * S + S].rearrange("p (i jj d) -> p i jj d", i=4, jj=2),
                            p_heads[rows, :, half * w:half * w + w].rearrange("p i (jj d) -> p i jj d", jj=2),
                            rsums[uv % 2][rows, :, :].unsqueeze(3).broadcast_to([S, 4, 2, DH1]),
                            ALU.mult).then_inc(heads_ready, 1)
                if u == 3 and nxt:
                    vec.wait_ge(queries_hi_ready, 3 * (g + 2))
                    if exists(g - 1, NM):
                        vec.wait_ge(scores_made, GU * g)
                    for half in range(2):
                        rows = slice(half * S, half * S + S)
                        nc.vector.tensor_tensor(queries_lo[1 - j][rows, :, half, :],
                                                queries[rows, :].rearrange("p (b s) -> p b s", s=S),
                                                queries_hi[1 - j][rows, :, half, :].bitcast(F32),
                                                ALU.subtract).then_inc(queries_lo_ready, 1)
                if u == 4 and nxt:
                    vec.wait_ge(keys_hi_ready, 2 * (g + 2))
                    if exists(g - 1, NM):
                        vec.wait_ge(key_heads_ready, 2 * GU * g)
                    nc.vector.tensor_tensor(keys_lo[1 - j][:], keys[:].rearrange("p (b s) -> p b s", s=S),
                                            keys_hi[1 - j][:].bitcast(F32), ALU.subtract).then_inc(keys_lo_ready, 1)
                if u in (4, 6) and nxt:
                    n = 2 * (g + 1) + (u - 4) // 2
                    vec.wait_ge(values_made, n + 1)
                    if exists(g - 1, NM):
                        vec.wait_ge(heads_made, GU * g)
                    for jj in range(2):
                        rows = slice(jj * S, jj * S + S)
                        for half in range(2):
                            cut = slice(half * S, half * S + S)
                            src = p_values[rows, :, cut].rearrange("p b (i jj d) -> p b i jj d", i=4, jj=2)[:, :, :, jj, :]
                            bias = b_value[rows, cut].rearrange("p (i jj d) -> p i jj d", i=4, jj=2)[:, :, jj, :]
                            at = half * 2 * DH1 + jj * DH1
                            last = nc.vector.tensor_tensor(values[1 - j][rows, 2 * (u - 4):2 * (u - 4) + 4, :, at:at + DH1], src,
                                                           bias.unsqueeze(1).broadcast_to([S, 4, 4, DH1]), ALU.add)
                            if half:
                                last.then_inc(values_ready, 1)
                if u == 5 and exists(g - 1, NM):
                    vec.wait_ge(out_made, g)
                    vec.wait_ge(bias_added, g)
                    tiles = x_sb[:, bass.ds(TT * (g - 1), TT), :]
                    nc.vector.tensor_tensor(tiles, p_turn[:].rearrange("p (t d) -> p t d", t=TT), tiles,
                                            ALU.add).then_inc(stream_ready, 1)
                if u == 3 and exists(g + 2, NM):
                    if exists(g + 1, NM):
                        vec.wait_ge(ctx_turned, g + 2)
                    for t in range(TT):
                        tile = TT * (g + 2) + t
                        nc.vector.tensor_scalar(normed[:, t, :], x_sb[:, bass.ds(tile, 1), :],
                                                mean[:, bass.ds(tile, 1)], rstd[:, bass.ds(tile, 1)],
                                                ALU.subtract, ALU.mult)
                    nc.vector.tensor_copy(ctx_rows[:], ctx_sb[:, bass.ds(TT * (g + 2), TT), :]).then_inc(normed_ready, 1)
                if u == 7 and exists(g - 1, NM):
                    vec.wait_ge(stream_ready, g)
                    for t in range(TT):
                        tile = TT * (g - 1) + t
                        last = nc.vector.bn_stats(stats[:, bass.ds(tile, 1), :], x_sb[:, bass.ds(tile, 1), :])
                    last.then_inc(stats_written, 1)

        over_groups(vec, steps)


_INS = ['x', 'ctx_1024', 'g_xattn', 'g_ffn', 'L0_xattn_ln1_g', 'L0_xattn_ln1_b', 'L0_xattn_ln2_g', 'L0_xattn_ln2_b',
        'L0_xattn_Wq', 'L0_xattn_Wkv', 'L0_xattn_Wo', 'L0_ffn_Wg', 'L0_ffn_bg', 'L0_ffn_W1', 'L0_ffn_b1', 'L0_ffn_W2',
        'L0_ffn_b2', 'L1_xattn_wq', 'L1_xattn_bq', 'L1_xattn_wk', 'L1_xattn_bk', 'L1_xattn_wv', 'L1_xattn_bv',
        'L1_xattn_wo', 'L1_xattn_bo', 'L1_ffn_wg', 'L1_ffn_w1', 'L1_ffn_w3', 'L1_ffn_w2']


def kernel(**inputs):
    import numpy as np
    import concourse.bacc as bacc
    from concourse.bass_utils import run_bass_kernel_spmd

    nc = bacc.Bacc("TRN2", target_bir_lowering=False, num_devices=1)
    arrays, args = {}, []
    for name in _INS:
        a = np.ascontiguousarray(inputs[name])
        arrays[f"in_{name}_dram"] = a
        args.append(nc.dram_tensor(f"in_{name}_dram", a.shape, mybir.dt.from_np(a.dtype), kind="ExternalInput").ap())
    args.append(nc.dram_tensor("out_0_dram", (B, S, D), F32, kind="ExternalOutput").ap())
    build(nc, *args)
    r = run_bass_kernel_spmd(nc, [arrays], core_ids=[0])
    return r.results[0]["out_0_dram"]
```
